# Optimizing a Trainium2 kernel written in Bass

```python
import numpy as np
import jax
import jax.numpy as jnp

def _softmax(x, axis=-1):
    return jax.nn.softmax(x, axis=axis)

def _gelu(x):
    return jax.nn.gelu(x, approximate=True)

def _silu(x):
    return jax.nn.silu(x)

def _sigmoid(x):
    return jax.nn.sigmoid(x)

def _layernorm(x, axis=-1, eps=1e-05):
    m = jnp.mean(x, axis=axis, keepdims=True)
    v = jnp.var(x, axis=axis, keepdims=True)
    return (x - m) / jnp.sqrt(v + eps)

def _scatter_add(tgt, idx, src, axis=0):
    return tgt.at[idx].add(src)

def _segment_sum(src, seg, n):
    return jax.ops.segment_sum(src, seg, n)
kernel_name = 'mk_recurrent_d2_jaxref_r8_0df8f3'

def setup_inputs(seed: int=0):
    np.random.seed(seed)
    _w = jnp.asarray

    def _L0_attn_setup():
        import jax, jax.numpy as jnp
        import numpy as np
        B, S, D = (4, 256, 128)

        def givens_rotate(r, x):
            g = r.reshape(-1, 2)
            g = g / jnp.linalg.norm(g, axis=-1, keepdims=True)
            xp = x.reshape(x.shape[:-1] + (x.shape[-1] // 2, 2))
            c, s = (g[:, 0], g[:, 1])
            y0 = c * xp[..., 0] - s * xp[..., 1]
            y1 = c * xp[..., 1] + s * xp[..., 0]
            return jnp.stack([y0, y1], axis=-1).reshape(x.shape)
        key = jax.random.key(seed)
        k1, k2 = jax.random.split(key, 2)
        Q = jax.random.normal(k1, (B, S, D), dtype=jnp.float32)
        rot_w = jax.random.uniform(k2, (3, D), dtype=jnp.float32, minval=-1.0, maxval=1.0)
        scale = jnp.array([np.sqrt(D)], dtype=jnp.float32)
        bias = jnp.zeros((), dtype=jnp.float32)
        return {'Q': Q, 'rot_w': rot_w, 'scale': scale, 'bias': bias}
    _L0_attn_in = _L0_attn_setup()

    def _L0_ffn_setup():
        import jax, jax.numpy as jnp
        import numpy as np
        DMODEL = 128
        N_EXPERTS = 16
        EXPERT_SIZE = 32
        K = 4
        key = jax.random.key(seed)
        k1, k2, k3, k4 = jax.random.split(key, 4)
        std_sel = 1.0 / np.sqrt(DMODEL)
        std_val = 1.0 / np.sqrt(N_EXPERTS * EXPERT_SIZE)
        return {'x': jax.random.normal(k1, (4, 256, DMODEL), dtype=jnp.float32), 'expert_sel': jax.random.normal(k2, (N_EXPERTS, DMODEL), dtype=jnp.float32) * std_sel, 'keys': jax.random.normal(k3, (N_EXPERTS, DMODEL, EXPERT_SIZE), dtype=jnp.float32) * std_sel, 'values': jax.random.normal(k4, (N_EXPERTS, EXPERT_SIZE, DMODEL), dtype=jnp.float32) * std_val, 'route_scale': jnp.ones((1,), dtype=jnp.float32)}
    _L0_ffn_in = _L0_ffn_setup()

    def _L1_attn_setup():
        import jax, jax.numpy as jnp
        import numpy as np
        E = 128
        NH = 4
        DH = E // NH
        GATE_SOFT_CAP = 15.0
        NORM_EPS = 1e-06
        BACKEND_EPS = 1e-06

        def soft_cap(x, cap):
            return cap * jnp.tanh(x / cap)

        def mlstm_parallel(q, k, v, ig, fg):
            q = q.transpose(0, 2, 1, 3)
            k = k.transpose(0, 2, 1, 3)
            v = v.transpose(0, 2, 1, 3)
            ig = ig.squeeze(-1).transpose(0, 2, 1)
            fg = fg.squeeze(-1).transpose(0, 2, 1)
            S = q.shape[2]
            log_fg = jax.nn.log_sigmoid(fg)
            lf_cum = jnp.cumsum(log_fg, axis=-1)
            fg_mat = lf_cum[..., :, None] - lf_cum[..., None, :]
            causal = jnp.tril(jnp.ones((S, S), dtype=bool))
            neg_inf = jnp.finfo(q.dtype).min
            log_D = jnp.where(causal, fg_mat + ig[..., None, :], neg_inf)
            m = jnp.max(log_D, axis=-1, keepdims=True)
            D = jnp.exp(log_D - m)
            scores = jnp.einsum('bhid,bhjd->bhij', q, k) / jnp.sqrt(jnp.float32(DH))
            C = scores * D
            n = jnp.maximum(jnp.abs(C.sum(axis=-1, keepdims=True)), jnp.exp(-m))
            h = jnp.einsum('bhij,bhjd->bhid', C, v) / (n + BACKEND_EPS)
            return h.transpose(0, 2, 1, 3)

        def multi_head_norm(h, w, eps):
            mu = h.mean(axis=-1, keepdims=True)
            var = ((h - mu) ** 2).mean(axis=-1, keepdims=True)
            return (h - mu) * jax.lax.rsqrt(var + eps) * w
        key = jax.random.key(seed)
        ks = jax.random.split(key, 12)
        B, S = (2, 256)
        sd = 1.0 / np.sqrt(E)
        x = jax.random.normal(ks[0], (B, S, E), jnp.float32)
        Wq = jax.random.normal(ks[1], (E, E), jnp.float32) * sd
        Wk = jax.random.normal(ks[2], (E, E), jnp.float32) * sd
        Wv = jax.random.normal(ks[3], (E, E), jnp.float32) * sd
        Wo = jax.random.normal(ks[4], (E, E), jnp.float32) * sd
        Wig = jax.random.normal(ks[5], (E, NH), jnp.float32) * 0.01
        big = jax.random.normal(ks[6], (NH,), jnp.float32) * 0.1 - 10.0
        Wfg = jax.random.normal(ks[7], (E, NH), jnp.float32) * 0.01
        bfg = jnp.linspace(3.0, 6.0, NH, dtype=jnp.float32)
        norm_w = jnp.ones((NH, DH), jnp.float32)
        Wdown = jax.random.normal(ks[8], (E, E), jnp.float32) * sd
        return {'x': x, 'Wq': Wq, 'Wk': Wk, 'Wv': Wv, 'Wo': Wo, 'Wig': Wig, 'big': big, 'Wfg': Wfg, 'bfg': bfg, 'norm_w': norm_w, 'Wdown': Wdown}
    _L1_attn_in = _L1_attn_setup()

    def _L1_ffn_setup():
        import jax, jax.numpy as jnp
        import numpy as np
        NUM_EXPERTS = 160
        TOP_K = 8
        ROUTED_SCALE = 2.5
        HIDDEN = 128
        INTER = 64
        key = jax.random.key(seed)
        ks = jax.random.split(key, 7)
        B, S = (1, 256)
        return {'hidden_states': jax.random.normal(ks[0], (B, S, HIDDEN), dtype=jnp.float32), 'router_w': jax.random.normal(ks[1], (NUM_EXPERTS, HIDDEN), dtype=jnp.float32) * 0.02, 'expert_bias': jnp.zeros((NUM_EXPERTS,), dtype=jnp.float32), 'w_gate': jax.random.normal(ks[2], (NUM_EXPERTS, INTER, HIDDEN), dtype=jnp.float32) * 0.02, 'w_down': jax.random.normal(ks[3], (NUM_EXPERTS, HIDDEN, INTER), dtype=jnp.float32) * 0.02, 'w_gate_shared': jax.random.normal(ks[4], (INTER, HIDDEN), dtype=jnp.float32) * 0.02, 'w_down_shared': jax.random.normal(ks[5], (HIDDEN, INTER), dtype=jnp.float32) * 0.02}
    _L1_ffn_in = _L1_ffn_setup()
    _d = {'L0_attn_Q': _L0_attn_in['Q'], 'L0_attn_rot_w': _L0_attn_in['rot_w'], 'L0_attn_scale': _L0_attn_in['scale'], 'L0_attn_bias': _L0_attn_in['bias'], 'L0_ffn_expert_sel': _L0_ffn_in['expert_sel'], 'L0_ffn_keys': _L0_ffn_in['keys'], 'L0_ffn_values': _L0_ffn_in['values'], 'L0_ffn_route_scale': _L0_ffn_in['route_scale'], 'L1_attn_Wq': _L1_attn_in['Wq'], 'L1_attn_Wk': _L1_attn_in['Wk'], 'L1_attn_Wv': _L1_attn_in['Wv'], 'L1_attn_Wo': _L1_attn_in['Wo'], 'L1_attn_Wig': _L1_attn_in['Wig'], 'L1_attn_big': _L1_attn_in['big'], 'L1_attn_Wfg': _L1_attn_in['Wfg'], 'L1_attn_bfg': _L1_attn_in['bfg'], 'L1_attn_norm_w': _L1_attn_in['norm_w'], 'L1_attn_Wdown': _L1_attn_in['Wdown'], 'L1_ffn_router_w': _L1_ffn_in['router_w'], 'L1_ffn_expert_bias': _L1_ffn_in['expert_bias'], 'L1_ffn_w_gate': _L1_ffn_in['w_gate'], 'L1_ffn_w_down': _L1_ffn_in['w_down'], 'L1_ffn_w_gate_shared': _L1_ffn_in['w_gate_shared'], 'L1_ffn_w_down_shared': _L1_ffn_in['w_down_shared']}
    _x0 = _d['L0_attn_Q']
    _d['L0_attn_Q'] = jax.random.normal(jax.random.fold_in(jax.random.key(seed), 1), (4, 512, 128), dtype=_x0.dtype)
    del _x0
    return _d

def reference(L0_attn_Q, L0_attn_rot_w, L0_attn_scale, L0_attn_bias, L0_ffn_expert_sel, L0_ffn_keys, L0_ffn_values, L0_ffn_route_scale, L1_attn_Wq, L1_attn_Wk, L1_attn_Wv, L1_attn_Wo, L1_attn_Wig, L1_attn_big, L1_attn_Wfg, L1_attn_bfg, L1_attn_norm_w, L1_attn_Wdown, L1_ffn_router_w, L1_ffn_expert_bias, L1_ffn_w_gate, L1_ffn_w_down, L1_ffn_w_gate_shared, L1_ffn_w_down_shared):

    def _L0_attn_ref(Q, rot_w, scale, bias):
        import jax, jax.numpy as jnp
        import numpy as np
        B, S, D = (4, 256, 128)

        def givens_rotate(r, x):
            g = r.reshape(-1, 2)
            g = g / jnp.linalg.norm(g, axis=-1, keepdims=True)
            xp = x.reshape(x.shape[:-1] + (x.shape[-1] // 2, 2))
            c, s = (g[:, 0], g[:, 1])
            y0 = c * xp[..., 0] - s * xp[..., 1]
            y1 = c * xp[..., 1] + s * xp[..., 0]
            return jnp.stack([y0, y1], axis=-1).reshape(x.shape)
        q = givens_rotate(rot_w[0], Q)
        k = givens_rotate(rot_w[1], Q)
        v = givens_rotate(rot_w[2], Q)
        zeros = jnp.zeros(Q.shape[:-1] + (1,), Q.dtype)
        q = jnp.concatenate([zeros, q], axis=-1)[:, None]
        k = jnp.concatenate([zeros, k], axis=-1)[:, None]
        v = jnp.concatenate([zeros, v], axis=-1)[:, None]
        sgn = jnp.concatenate([-jnp.ones((1,), Q.dtype), jnp.ones((q.shape[-1] - 1,), Q.dtype)])
        cin = jnp.einsum('bhqd,bhkd->bhqk', q * sgn, k)
        attn = jax.nn.softmax((2.0 + 2.0 * cin) / scale + bias, axis=-1)
        ave = jnp.einsum('bhqk,bhkd->bhqd', attn, v)
        inner = jnp.sum(ave * ave * sgn, axis=-1, keepdims=True)
        denom = jnp.sqrt(jnp.clip(jnp.abs(inner), 1e-08, None))
        out = (ave / denom)[:, 0]
        return out[..., 1:]

    def _L0_ffn_ref(x, expert_sel, keys, values, route_scale):
        import jax, jax.numpy as jnp
        import numpy as np
        DMODEL = 128
        N_EXPERTS = 16
        EXPERT_SIZE = 32
        K = 4
        sel_logits = jnp.einsum('btd,ed->bte', x, expert_sel)
        sel_probs = jax.nn.sigmoid(sel_logits)
        _, sel_index = jax.lax.top_k(sel_probs, K)
        sel_val = jnp.take_along_axis(sel_probs, sel_index, axis=-1)
        sel_val = sel_val / jnp.clip(sel_val.sum(-1, keepdims=True), 1e-09)
        sel_val = sel_val * route_scale
        scores_all = jax.nn.relu(jnp.einsum('btd,edh->bteh', x, keys))
        values_all = jnp.einsum('bteh,ehv->btev', scores_all, values)
        sel_idx_exp = sel_index[..., None]
        selected = jnp.take_along_axis(values_all, sel_idx_exp, axis=2)
        out = (selected * sel_val[..., None]).sum(axis=2)
        return out

    def _L1_attn_ref(x, Wq, Wk, Wv, Wo, Wig, big, Wfg, bfg, norm_w, Wdown):
        import jax, jax.numpy as jnp
        import numpy as np
        E = 128
        NH = 4
        DH = E // NH
        GATE_SOFT_CAP = 15.0
        NORM_EPS = 1e-06
        BACKEND_EPS = 1e-06

        def soft_cap(x, cap):
            return cap * jnp.tanh(x / cap)

        def mlstm_parallel(q, k, v, ig, fg):
            q = q.transpose(0, 2, 1, 3)
            k = k.transpose(0, 2, 1, 3)
            v = v.transpose(0, 2, 1, 3)
            ig = ig.squeeze(-1).transpose(0, 2, 1)
            fg = fg.squeeze(-1).transpose(0, 2, 1)
            S = q.shape[2]
            log_fg = jax.nn.log_sigmoid(fg)
            lf_cum = jnp.cumsum(log_fg, axis=-1)
            fg_mat = lf_cum[..., :, None] - lf_cum[..., None, :]
            causal = jnp.tril(jnp.ones((S, S), dtype=bool))
            neg_inf = jnp.finfo(q.dtype).min
            log_D = jnp.where(causal, fg_mat + ig[..., None, :], neg_inf)
            m = jnp.max(log_D, axis=-1, keepdims=True)
            D = jnp.exp(log_D - m)
            scores = jnp.einsum('bhid,bhjd->bhij', q, k) / jnp.sqrt(jnp.float32(DH))
            C = scores * D
            n = jnp.maximum(jnp.abs(C.sum(axis=-1, keepdims=True)), jnp.exp(-m))
            h = jnp.einsum('bhij,bhjd->bhid', C, v) / (n + BACKEND_EPS)
            return h.transpose(0, 2, 1, 3)

        def multi_head_norm(h, w, eps):
            mu = h.mean(axis=-1, keepdims=True)
            var = ((h - mu) ** 2).mean(axis=-1, keepdims=True)
            return (h - mu) * jax.lax.rsqrt(var + eps) * w
        B, S, _ = x.shape
        q = (x @ Wq).reshape(B, S, NH, DH)
        k = (x @ Wk).reshape(B, S, NH, DH)
        v = (x @ Wv).reshape(B, S, NH, DH)
        o = x @ Wo
        ig = soft_cap(x @ Wig + big, GATE_SOFT_CAP)[..., None]
        fg = soft_cap(x @ Wfg + bfg, GATE_SOFT_CAP)[..., None]
        h = mlstm_parallel(q, k, v, ig, fg)
        hn = multi_head_norm(h, norm_w, NORM_EPS).reshape(B, S, -1)
        h_out = jax.nn.sigmoid(o) * hn
        return h_out @ Wdown

    def _L1_ffn_ref(hidden_states, router_w, expert_bias, w_gate, w_down, w_gate_shared, w_down_shared):
        import jax, jax.numpy as jnp
        import numpy as np
        NUM_EXPERTS = 160
        TOP_K = 8
        ROUTED_SCALE = 2.5
        HIDDEN = 128
        INTER = 64
        B, S, H = hidden_states.shape
        x = hidden_states.reshape(-1, H)
        T = x.shape[0]
        logits = x @ router_w.T + expert_bias[None, :]
        probs = jax.nn.sigmoid(logits)
        top_w, top_idx = jax.lax.top_k(probs, TOP_K)
        top_w = top_w / (jnp.sum(top_w, axis=-1, keepdims=True) + 1e-09)
        top_w = top_w * ROUTED_SCALE
        combine = jnp.zeros((T, NUM_EXPERTS), dtype=x.dtype)
        combine = combine.at[jnp.arange(T)[:, None], top_idx].set(top_w)
        h1 = jax.nn.silu(jnp.einsum('th,eih->eti', x, w_gate))
        h1w = h1 * combine.T[:, :, None]
        routed = jnp.einsum('eti,ehi->th', h1w, w_down)
        shared = jax.nn.silu(x @ w_gate_shared.T) @ w_down_shared.T
        return (routed + shared).reshape(B, S, H)
    x = L0_attn_Q
    xn = _layernorm(x, axis=-1)
    s = _L0_attn_ref(xn, L0_attn_rot_w, L0_attn_scale, L0_attn_bias)
    g = _silu(_L0_ffn_ref(xn, L0_ffn_expert_sel, L0_ffn_keys, L0_ffn_values, L0_ffn_route_scale))
    x = x + s * g
    xn = _layernorm(x, axis=-1)
    s = _L1_attn_ref(xn, L1_attn_Wq, L1_attn_Wk, L1_attn_Wv, L1_attn_Wo, L1_attn_Wig, L1_attn_big, L1_attn_Wfg, L1_attn_bfg, L1_attn_norm_w, L1_attn_Wdown)
    g = _silu(_L1_ffn_ref(xn, L1_ffn_router_w, L1_ffn_expert_bias, L1_ffn_w_gate, L1_ffn_w_down, L1_ffn_w_gate_shared, L1_ffn_w_down_shared))
    x = x + s * g
    return x

_drawn_inputs = setup_inputs


def setup_inputs(seed=0):
    import zlib

    import numpy as np

    out = dict(_drawn_inputs(seed))
    spreads = {'L1_attn_norm_w': (1.0, 0.6), 'L1_ffn_expert_bias': (0.0, 0.8)}
    factors = {'L0_attn_rot_w': 8.0,
     'L0_ffn_expert_sel': 8.0,
     'L0_ffn_keys': 8.0,
     'L0_ffn_values': 8.0,
     'L1_attn_Wq': 8.0,
     'L1_attn_Wk': 8.0,
     'L1_attn_Wv': 8.0,
     'L1_attn_Wo': 8.0,
     'L1_attn_Wig': 64.0,
     'L1_attn_big': 64.0,
     'L1_attn_Wfg': 64.0,
     'L1_attn_bfg': 64.0,
     'L1_attn_Wdown': 8.0,
     'L1_ffn_router_w': 8.0,
     'L1_ffn_w_gate': 8.0,
     'L1_ffn_w_down': 8.0,
     'L1_ffn_w_gate_shared': 8.0,
     'L1_ffn_w_down_shared': 8.0}
    for name, (base, spread) in spreads.items():
        noise = np.random.default_rng([zlib.crc32(name.encode()), seed]).standard_normal(out[name].shape)
        drawn = base * np.exp(spread * noise) if base else spread * noise
        out[name] = jnp.asarray(drawn.astype(out[name].dtype))
    for name, factor in factors.items():
        out[name] = (out[name] * factor).astype(out[name].dtype)
    return out
```

```python
import concourse.bass as bass
from concourse import mybir
from contextlib import ExitStack

F32 = mybir.dt.float32
F32R = mybir.dt.float32r
BF16 = mybir.dt.bfloat16
ALU = mybir.AluOpType
ACT = mybir.ActivationFunctionType
AX = mybir.AxisListType

P = 128
D = 128
B, S = 4, 512
TPB = S // P
NT = B * TPB
N = NT * P
LN_EPS = 1e-5

E0, H0, K0 = 16, 32, 4
EPC0 = P // H0
C0 = E0 // EPC0
R0 = C0 * 3 * EPC0
PAD0 = 8 - K0

NH, DH = 4, 32
DV = DH + 1
CAP = 15.0
NORM_EPS = 1e-6
BACKEND_EPS = 1e-6
E1, H1, K1 = 160, 64, 8
EPC1 = P // H1
C1 = E1 // EPC1
RPC = 3 * EPC1
ROUTED_SCALE = 2.5
TB = 120
NB = C1 * RPC // TB
MASKED = -30000.0

A_COLS = dict(ident=P, turn=P, ones=P, sel0=C0 * P, sel1=P, expert_sel=E0, keys=C0 * P, values=C0 * D,
              rot_c=3, rot_s=3, scale=1, bias=1, route_scale=1)
B_COLS = dict(masked=P, wv=D, wo=D, wk=D, wq=D, wig=32, wfg=32, router=E1, wdown=D, norm_w=D,
              expert_bias=E1, big=1, bfg=1, shared_gate=H1, shared_down=D, diag=NH * DV)


def places(cols):
    at, out = 0, {}
    for name, n in cols.items():
        out[name] = slice(at, at + n)
        at += n
    return out, at


A_AT, A_N = places(A_COLS)
B_AT, B_N = places(B_COLS)


def build(nc, x_in, a_in, b_in, w_in, x_out):
    x_rows = x_in.rearrange("(t p) d -> p t d", p=P)
    out_rows = x_out.rearrange("(t p) d -> p t d", p=P)
    comb_dram = nc.dram_tensor("combine_rows", (C1 * RPC, N), BF16, kind="Internal").ap()

    with ExitStack() as whole:
        def sem(name):
            return whole.enter_context(nc.semaphore(name))

        def chain(e, s):
            n = [0]

            def link(ins):
                n[0] += 1
                ins.then_inc(s, 1)
                e.wait_ge(s, n[0])
            return link

        def sb(name, shape, dt=F32, ctx=whole):
            return ctx.enter_context(nc.sbuf_tensor(name, shape, dt))

        bank = [whole.enter_context(nc.psum_tensor(f"bank{i}", [P, 512], F32)) for i in range(8)]

        A = sb("A", [P, A_N])
        Bw = sb("Bw", [P, B_N])
        a = {k: A[:, s] for k, s in A_AT.items()}
        w = {k: Bw[:, s] for k, s in B_AT.items()}
        X = sb("X", [P, NT, D])
        XT = sb("XT", [P, N])
        ident_bf = sb("ident_bf", [P, P], BF16)
        XH = sb("XH", [P, N], F32R)
        XL = sb("XL", [P, N], F32R)
        veps = sb("veps", [P, NT])
        rstd = sb("rstd", [P, NT])
        mv = sb("mv", [P, NT, 2])
        stats = sb("stats", [P, NT, 6])

        def norm_batch(e, link, b, Xn, std_asked, std_ready, xn_ready):
            ts = range(TPB * b, TPB * b + TPB)
            tb = slice(TPB * b, TPB * b + TPB)
            for t in ts:
                last = e.bn_stats(stats[:, t, :], X[:, t, :])
            link(last)
            for t in ts:
                last = e.bn_aggr(mv[:, t, :], stats[:, t, :])
            link(last)
            e.tensor_scalar(veps[:, tb], mv[:, tb, 1], LN_EPS, None, ALU.add).then_inc(std_asked, 1)
            e.wait_ge(std_ready, b + 1)
            link(e.reciprocal(rstd[:, tb], rstd[:, tb]))
            for t in ts:
                last = e.tensor_scalar(Xn[:, t, :], X[:, t, :], mv[:, t, 0:1], rstd[:, t:t + 1],
                                       ALU.subtract, ALU.mult)
            last.then_inc(xn_ready, 1)

        with ExitStack() as l0:
            Xn = sb("Xn", [P, NT, D], ctx=l0)
            QT = sb("QT", [P, N], ctx=l0)
            V = sb("V", [P, NT, D], ctx=l0)
            U = sb("U", [P, NT, D], ctx=l0)
            gate = sb("gate", [P, NT, D], ctx=l0)
            scaled = sb("scaled", [P, NT, D], ctx=l0)
            norm0 = sb("norm0", [P, NT], ctx=l0)
            comb0T = sb("comb0T", [R0, N], BF16, ctx=l0)
            sel0_bf = sb("sel0_bf", [R0, C0, P], BF16, ctx=l0)

            with ExitStack() as ph:
                rn = sb("rn", [P, 3], ctx=ph)
                rn2 = sb("rn2", [P, 3], ctx=ph)
                cs = sb("cs", [P, 3], ctx=ph)
                sn = sb("sn", [P, 3], ctx=ph)
                two = sb("two", [P, 1], ctx=ph)
                rt = sb("rt", [P, 3, P], ctx=ph)
                rot = sb("rot", [P, 3, P], ctx=ph)
                Mq = sb("Mq", [P, P], ctx=ph)
                ex = sb("ex", [P, NT * E0], ctx=ph)
                prob = sb("prob", [P, NT, E0 + PAD0], ctx=ph)
                zap = sb("zap", [P, NT, E0 + PAD0], ctx=ph)
                top = sb("top", [P, NT, 8], ctx=ph)
                take = sb("take", [P, NT, 8], ctx=ph)
                tot = sb("tot", [P, NT], ctx=ph)
                cw = sb("cw", [P, NT, E0], ctx=ph)
                cwr = sb("cwr", [P, NT, E0], ctx=ph)
                parts = sb("parts", [P, NT, R0], BF16, ctx=ph)

                x_loaded = [sem(f"x_loaded{b}") for b in range(B)]
                a_loaded, b_loaded = sem("a_loaded"), sem("b_loaded")
                dve_order, act_order = sem("dve_order_a"), sem("act_order_a")
                std_asked, std_ready, xn_ready = sem("std_asked"), sem("std_ready"), sem("xn_ready")
                xt_turned, xt_ready = sem("xt_turned"), sem("xt_ready")
                rot_asked, rot_ready, rot_made = sem("rot_asked"), sem("rot_ready"), sem("rot_made")
                rot_product, mq_ready = sem("rot_product"), sem("mq_ready")
                logits_ready, exp_ready, parts_ready = sem("logits_ready"), sem("exp_ready"), sem("parts_ready")
                v_made, v_ready, q_made, q_ready = sem("v_made"), sem("v_ready"), sem("q_made"), sem("q_ready")
                comb_turned, comb_ready, ident_ready = sem("comb_turned"), sem("comb_ready"), sem("ident_ready")
                block = ph.enter_context(nc.Block())

                @block.sync
                def _(e):
                    for b in range(B):
                        tb = slice(TPB * b, TPB * b + TPB)
                        e.dma_start(X[:, tb, :], x_rows[:, tb, :]).then_inc(x_loaded[b], 16)

                @block.scalar
                def _(e):
                    e.dma_start(A[:, :], a_in).then_inc(a_loaded, 16)
                    e.dma_start(Bw[:, :], b_in).then_inc(b_loaded, 16)
                    for b in range(B):
                        tb = slice(TPB * b, TPB * b + TPB)
                        e.wait_ge(std_asked, b + 1)
                        e.activation(rstd[:, tb], veps[:, tb], ACT.Sqrt).then_inc(std_ready, 1)
                        if b == 0:
                            e.wait_ge(rot_asked, 1)
                            e.activation(rn[:, :], rn2[:, :], ACT.Sqrt).then_inc(rot_ready, 1)
                    for b in range(B):
                        e.wait_ge(xt_turned, b + 1)
                        e.copy(XT[:, S * b:S * b + S], bank[b][:, :]).then_inc(xt_ready, 1)
                    e.wait_ge(logits_ready, 1)
                    e.activation(ex[:, :], bank[4][:, 0:NT * E0], ACT.Exp, scale=-1.0).then_inc(exp_ready, 1)
                    for b in range(B):
                        e.wait_ge(q_made, b + 1)
                        e.copy(QT[:, S * b:S * b + S], bank[b][:, :]).then_inc(q_ready, 1)
                    e.wait_ge(b_loaded, 16)

                @block.vector
                def _(e):
                    link = chain(e, dve_order)
                    e.wait_ge(a_loaded, 16)
                    e.tensor_copy(ident_bf[:, :], a["ident"]).then_inc(ident_ready, 1)
                    e.tensor_copy(sel0_bf[:, :, :], a["sel0"][0:R0, :].rearrange("r (c m) -> r c m", c=C0))
                    link(e.tensor_tensor(cs[:, :], a["rot_c"], a["rot_c"], ALU.mult))
                    link(e.tensor_tensor(sn[:, :], a["rot_s"], a["rot_s"], ALU.mult))
                    e.tensor_tensor(rn2[:, :], cs[:, :], sn[:, :], ALU.add).then_inc(rot_asked, 1)
                    for b in range(B):
                        e.wait_ge(x_loaded[b], 16)
                        norm_batch(e, link, b, Xn, std_asked, std_ready, xn_ready)
                        if b == 0:
                            e.wait_ge(rot_ready, 1)
                            e.reciprocal(two[:, :], a["scale"])
                            link(e.reciprocal(rn[:, :], rn[:, :]))
                            e.tensor_tensor(cs[:, :], a["rot_c"], rn[:, :], ALU.mult)
                            link(e.tensor_tensor(sn[:, :], a["rot_s"], rn[:, :], ALU.mult))
                            for i in range(3):
                                last = e.tensor_scalar(rt[:, i, :], a["turn"], sn[:, i:i + 1], None, ALU.mult)
                            link(last)
                            for i in range(3):
                                last = e.scalar_tensor_tensor(rot[:, i, :], a["ident"], cs[:, i:i + 1], rt[:, i, :],
                                                              ALU.mult, ALU.subtract if i == 2 else ALU.add)
                            last.then_inc(rot_made, 1)
                    e.wait_ge(rot_product, 1)
                    e.tensor_scalar(Mq[:, :], bank[5][:, 0:P], two[:, 0:1], 2.0, ALU.mult, ALU.mult).then_inc(mq_ready, 1)
                    e.wait_ge(exp_ready, 1)
                    link(e.tensor_scalar(ex[:, :], ex[:, :], 1.0, None, ALU.add))
                    for i in range(PAD0):
                        e.memset(prob[:, :, E0 + i:E0 + i + 1], -1.0 - i)
                        e.memset(take[:, :, K0 + i:K0 + i + 1], -1.0 - i)
                    link(e.reciprocal(prob[:, :, 0:E0], ex[:, :].rearrange("p (t e) -> p t e", e=E0)))
                    for t in range(NT):
                        last = e.max(top[:, t, :], prob[:, t, 0:E0])
                    link(last)
                    e.tensor_reduce(tot[:, :], top[:, :, 0:K0], AX.X, ALU.add)
                    link(e.tensor_copy(take[:, :, 0:K0], top[:, :, 0:K0]))
                    for t in range(NT):
                        last = e.match_replace(zap[:, t, :], take[:, t, :], prob[:, t, :], 0.0)
                    link(last)
                    link(e.tensor_scalar(tot[:, :], tot[:, :], 1e-9, None, ALU.max))
                    e.tensor_tensor(cw[:, :, :], prob[:, :, 0:E0], zap[:, :, 0:E0], ALU.subtract)
                    link(e.reciprocal(tot[:, :], tot[:, :]))
                    link(e.tensor_scalar(tot[:, :], tot[:, :], a["route_scale"], None, ALU.mult))
                    link(e.tensor_tensor(cw[:, :, :], cw[:, :, :],
                                         tot[:, :].rearrange("p (t o) -> p t o", o=1).to_broadcast([P, NT, E0]), ALU.mult))
                    pv = parts[:, :, :].rearrange("p t (c h e) -> p t c h e", c=C0, h=3)
                    cv = cw[:, :, :].rearrange("p t (c e) -> p t c e", c=C0)
                    rv = cwr[:, :, :].rearrange("p t (c e) -> p t c e", c=C0)
                    link(e.tensor_copy(pv[:, :, :, 0, :], cv))
                    link(e.tensor_tensor(rv, cv, pv[:, :, :, 0, :], ALU.subtract))
                    link(e.tensor_copy(pv[:, :, :, 1, :], rv))
                    e.tensor_tensor(pv[:, :, :, 2, :], rv, pv[:, :, :, 1, :], ALU.subtract).then_inc(parts_ready, 1)
                    for b in range(B):
                        e.wait_ge(v_made, b + 1)
                        e.tensor_copy(V[:, TPB * b:TPB * b + TPB, :],
                                      bank[4 + b][:, :].rearrange("p (t d) -> p t d", d=D)).then_inc(v_ready, 1)
                    for i in range(2):
                        e.wait_ge(comb_turned, i + 1)
                        e.tensor_copy(comb0T[:, i * (N // 2):(i + 1) * (N // 2)],
                                      bank[i][0:R0, :].bitcast(BF16)).then_inc(comb_ready, 1)

                @block.tensor
                def _(e):
                    e.wait_ge(a_loaded, 16)
                    for b in range(B):
                        e.wait_ge(xn_ready, b + 1)
                        for j in range(TPB):
                            last = e.transpose(bank[b][:, P * j:P * j + P], Xn[:, TPB * b + j, :], a["ident"])
                        last.then_inc(xt_turned, 1)
                        if b == 0:
                            e.wait_ge(rot_made, 1)
                            e.matmul(bank[5][:, 0:P], rot[:, 0, :], rot[:, 1, :], start=True, stop=True).then_inc(rot_product, 1)
                    for t in range(NT):
                        if t % TPB == 0:
                            e.wait_ge(xt_ready, t // TPB + 1)
                        last = e.matmul(bank[4][:, E0 * t:E0 * t + E0], XT[:, P * t:P * t + P], a["expert_sel"],
                                        start=True, stop=True)
                    last.then_inc(logits_ready, 1)
                    e.wait_ge(mq_ready, 1)
                    for b in range(B):
                        e.matmul(bank[b][:, :], Mq[:, :], XT[:, S * b:S * b + S], start=True, stop=True).then_inc(q_made, 1)
                    e.wait_ge(exp_ready, 1)
                    for b in range(B):
                        for j in range(TPB):
                            t = TPB * b + j
                            last = e.matmul(bank[4 + b][:, P * j:P * j + P], XT[:, P * t:P * t + P], rot[:, 2, :],
                                            start=True, stop=True)
                        last.then_inc(v_made, 1)
                    e.wait_ge(parts_ready, 1)
                    e.wait_ge(q_ready, 2)
                    for t in range(NT):
                        half, j = t // (NT // 2), t % (NT // 2)
                        last = e.transpose(bank[half][0:R0, :].bitcast(BF16)[:, P * j:P * j + P], parts[:, t, :],
                                           ident_bf[:, :])
                        if j == NT // 2 - 1:
                            last.then_inc(comb_turned, 1)

            with ExitStack() as ph:
                nmax = sb("nmax", [P, NT], ctx=ph)
                rows = sb("rows", [P, NT], ctx=ph)
                prb = sb("prb", [P, 2, S], ctx=ph)
                prT = sb("prT", [P, 2, S], ctx=ph)
                ss = sb("ss", [P, NT], ctx=ph)
                G0 = sb("G0", [P, 2, C0, S], ctx=ph)
                act0 = sb("act0", [P, 2, S], ctx=ph)
                scores_made, max_ready, probs_ready = sem("scores_made"), sem("max_ready"), sem("probs_ready")
                probs_turned, probsT_ready = sem("probs_turned"), sem("probsT_ready")
                u_made, u_ready = sem("u_made"), sem("u_ready")
                dve_order, act_order = sem("dve_order_b"), sem("act_order_b")
                h_made, b_made, act_ready, g_ready = sem("h0_made"), sem("b0_made"), sem("act0_ready"), sem("g0_ready")
                y_made, gate_ready, norm_asked = sem("y0_made"), sem("gate_ready"), sem("norm_asked")
                block = ph.enter_context(nc.Block())

                @block.tensor
                def _(e):
                    def scores(t):
                        if t >= 2:
                            e.wait_ge(probs_ready, t - 1)
                        b = t // TPB
                        e.matmul(bank[t % 2][:, :], QT[:, P * t:P * t + P], XT[:, S * b:S * b + S],
                                 start=True, stop=True).then_inc(scores_made, 1)

                    def turn(t):
                        e.wait_ge(probs_ready, t + 1)
                        if t >= 2:
                            e.wait_ge(probsT_ready, t - 1)
                        for j in range(TPB):
                            last = e.transpose(bank[2 + t % 2][:, P * j:P * j + P], prb[:, t % 2, P * j:P * j + P],
                                               a["ident"])
                        last.then_inc(probs_turned, 1)

                    def values(t):
                        e.wait_ge(probsT_ready, t + 1)
                        if t >= 2:
                            e.wait_ge(u_ready, t - 1)
                        b = t // TPB
                        for j in range(TPB):
                            last = e.matmul(bank[4 + t % 2][:, 0:D], prT[:, t % 2, P * j:P * j + P],
                                            V[:, TPB * b + j, :], start=(j == 0), stop=(j == TPB - 1))
                        last.then_inc(u_made, 1)

                    scores(0)
                    for t in range(NT + 1):
                        if t + 1 < NT:
                            scores(t + 1)
                        if t < NT:
                            turn(t)
                        if t >= 1:
                            values(t - 1)

                    def hidden(u):
                        g, c = u // C0, u % C0
                        if u >= 2:
                            e.wait_ge(act_ready, u - 1)
                            e.wait_ge(g_ready, u - 1)
                        elif u == 0:
                            e.wait_ge(u_ready, NT)
                        e.matmul(bank[u % 2][:, :], a["keys"][:, P * c:P * c + P], XT[:, S * g:S * g + S],
                                 start=True, stop=True).then_inc(h_made, 1)
                        e.matmul(bank[2 + u % 2][:, :], sel0_bf[:, c, :], comb0T[:, S * g:S * g + S],
                                 start=True, stop=True).then_inc(b_made, 1)

                    def down(g):
                        e.wait_ge(g_ready, C0 * g + C0)
                        for j in range(TPB):
                            for c in range(C0):
                                last = e.matmul(bank[4 + g][:, P * j:P * j + P], G0[:, g % 2, c, P * j:P * j + P],
                                                a["values"][:, P * c:P * c + P], start=(c == 0), stop=(c == C0 - 1))
                        last.then_inc(y_made, 1)

                    for u in range(B * C0):
                        hidden(u)
                        if u % C0 == 1 and u > C0:
                            down(u // C0 - 1)
                    down(B - 1)

                @block.vector
                def _(e):
                    link = chain(e, dve_order)

                    def row_max(t):
                        e.wait_ge(scores_made, t + 1)
                        link(e.tensor_reduce(nmax[:, t:t + 1], bank[t % 2][:, :], AX.X, ALU.max, negate=True))
                        e.tensor_scalar(nmax[:, t:t + 1], nmax[:, t:t + 1], a["bias"], a["bias"],
                                        ALU.subtract, ALU.add).then_inc(max_ready, 1)

                    def copy_turned(t):
                        e.wait_ge(probs_turned, t + 1)
                        if t >= 2:
                            e.wait_ge(u_made, t - 1)
                        e.tensor_copy(prT[:, t % 2, :], bank[2 + t % 2][:, :]).then_inc(probsT_ready, 1)

                    row_max(0)
                    for t in range(NT):
                        if t + 1 < NT:
                            row_max(t + 1)
                        copy_turned(t)
                    for u in range(B * C0):
                        g, c = u // C0, u % C0
                        e.wait_ge(b_made, u + 1)
                        e.wait_ge(act_ready, u + 1)
                        if c == 0 and g >= 2:
                            e.wait_ge(y_made, g - 1)
                        e.tensor_tensor(G0[:, g % 2, c, :], act0[:, u % 2, :], bank[2 + u % 2][:, :],
                                        ALU.mult).then_inc(g_ready, 1)
                    sq = prb[:, 0, :].rearrange("p (t d) -> p t d", d=D)
                    e.wait_ge(u_ready, NT)
                    for b in range(B):
                        tb = slice(TPB * b, TPB * b + TPB)
                        link(e.tensor_tensor(sq, U[:, tb, :], U[:, tb, :], ALU.mult))
                        link(e.tensor_reduce(ss[:, tb], sq, AX.X, ALU.add))
                    link(e.tensor_tensor(rows[:, :], rows[:, :], rows[:, :], ALU.mult))
                    e.scalar_tensor_tensor(norm0[:, :], rows[:, :], 1e-8, ss[:, :], ALU.mult, ALU.max).then_inc(norm_asked, 1)

                @block.scalar
                def _(e):
                    for t in range(NT):
                        e.wait_ge(max_ready, t + 1)
                        if t >= 2:
                            e.wait_ge(probs_turned, t - 1)
                        e.activation(prb[:, t % 2, :], bank[t % 2][:, :], ACT.Exp, bias=nmax[:, t:t + 1],
                                     accum_out=rows[:, t:t + 1]).then_inc(probs_ready, 1)
                        if t >= 1:
                            e.wait_ge(u_made, t)
                            e.copy(U[:, t - 1, :], bank[4 + (t - 1) % 2][:, 0:D]).then_inc(u_ready, 1)
                    e.wait_ge(u_made, NT)
                    e.copy(U[:, NT - 1, :], bank[4 + (NT - 1) % 2][:, 0:D]).then_inc(u_ready, 1)
                    for u in range(B * C0):
                        e.wait_ge(h_made, u + 1)
                        if u >= 2:
                            e.wait_ge(g_ready, u - 1)
                        e.activation(act0[:, u % 2, :], bank[u % 2][:, :], ACT.Relu).then_inc(act_ready, 1)
                    for b in range(B):
                        e.wait_ge(y_made, b + 1)
                        e.activation(gate[:, TPB * b:TPB * b + TPB, :],
                                     bank[4 + b][:, :].rearrange("p (t d) -> p t d", d=D), ACT.Silu).then_inc(gate_ready, 1)


            with ExitStack() as ph:
                norm_ready = sem("norm_ready")
                dve_order, act_order = sem("dve_order_c"), sem("act_order_c")
                std_asked, std_ready, xn_ready = sem("std_asked1"), sem("std_ready1"), sem("xn_ready1")
                xt_turned, xt_ready, xh_ready, xl_ready = sem("xt_turned1"), sem("xt_ready1"), sem("xh_ready"), sem("xl_ready")
                block = ph.enter_context(nc.Block())

                @block.scalar
                def _(e):
                    e.activation(norm0[:, :], norm0[:, :], ACT.Sqrt).then_inc(norm_ready, 1)
                    for b in range(B):
                        tb = slice(TPB * b, TPB * b + TPB)
                        e.wait_ge(std_asked, b + 1)
                        e.activation(rstd[:, tb], veps[:, tb], ACT.Sqrt).then_inc(std_ready, 1)
                    for b in range(B):
                        e.wait_ge(xt_turned, b + 1)
                        e.copy(XT[:, S * b:S * b + S], bank[b][:, :]).then_inc(xt_ready, 1)

                @block.vector
                def _(e):
                    link = chain(e, dve_order)
                    e.wait_ge(norm_ready, 1)
                    link(e.reciprocal(norm0[:, :], norm0[:, :]))
                    for b in range(B):
                        tb = slice(TPB * b, TPB * b + TPB)
                        for t in range(TPB * b, TPB * b + TPB):
                            last = e.scalar_tensor_tensor(scaled[:, t, :], U[:, t, :], norm0[:, t:t + 1], gate[:, t, :],
                                                          ALU.mult, ALU.mult)
                        link(last)
                        link(e.tensor_tensor(X[:, tb, :], X[:, tb, :], scaled[:, tb, :], ALU.add))
                        norm_batch(e, link, b, Xn, std_asked, std_ready, xn_ready)

                @block.tensor
                def _(e):
                    for b in range(B):
                        e.wait_ge(xn_ready, b + 1)
                        for j in range(TPB):
                            last = e.transpose(bank[b][:, P * j:P * j + P], Xn[:, TPB * b + j, :], a["ident"])
                        last.then_inc(xt_turned, 1)

                @block.gpsimd
                def _(e):
                    for b in range(B):
                        s = slice(S * b, S * b + S)
                        e.wait_ge(xt_ready, b + 1)
                        e.tensor_copy(XH[:, s], XT[:, s]).then_inc(xh_ready, 1)
                        e.wait_ge(xh_ready, b + 1)
                        e.tensor_tensor(XL[:, s], XT[:, s], XH[:, s].bitcast(F32), ALU.subtract).then_inc(xl_ready, 1)

        with ExitStack() as l1:
            S1 = sb("S1", [P, NT, D], ctx=l1)

            with ExitStack() as at:
                VA = sb("VA", [P, NT, NH, DV], ctx=at)
                K = sb("K", [P, NT, D], ctx=at)
                expO = sb("expO", [P, NT, D], ctx=at)
                qT = sb("qT", [P, N], ctx=at)
                kT = sb("kT", [P, N], ctx=at)
                O = sb("O", [P, NT, NH, DV], ctx=at)
                logits = sb("logits", [P, NT, E1], ctx=at)
                floor = sb("floor", [P, TPB, P], ctx=at)
                k_scale = sb("k_scale", [P, TPB, P], ctx=at)
                q_scale = sb("q_scale", [P, TPB - 1, P], ctx=at)
                decay = sb("decay", [P, TPB - 1, P], ctx=at)
                ah = sb("ah", [P, S], F32R, ctx=at)
                al = sb("al", [P, S], F32R, ctx=at)
                mh = sb("mh", [P, S], F32R, ctx=at)
                ml = sb("ml", [P, S], F32R, ctx=at)
                lane = sb("lane", [P, B, NH, P], F32R, ctx=at)
                masked_bf = sb("masked_bf", [P, TPB, P], BF16, ctx=at)

                with ExitStack() as ph:
                    g = {k: sb(f"g_{k}", [P, S], ctx=ph) for k in
                         ("ti", "tf", "x", "y", "u", "c", "ru", "ln", "lf", "a", "M", "m", "ones")}
                    bias15 = sb("bias15", [P, 2], ctx=ph)
                    Rdiag = sb("Rdiag", [P, TPB, P], ctx=ph)
                    R = sb("R", [P, TPB, P], ctx=ph)
                    proj_made, proj_read_v, proj_read_s = sem("proj_made"), sem("proj_read_v"), sem("proj_read_s")
                    router_made, router_read = sem("router_made"), sem("router_read")
                    qk_made, qk_read = sem("qk_made"), sem("qk_read")
                    gates_made, tanh_ready, bias_ready = sem("gates_made"), sem("tanh_ready"), sem("bias_ready")
                    abs_ready, y_ready, u_ready, ln_ready = sem("abs_ready"), sem("y_ready"), sem("u1_ready"), sem("ln_ready")
                    rows_ready, rows_turned, R_made, R_ready = sem("rows_ready"), sem("rows_turned"), sem("R_made"), sem("R_ready")
                    diff_ready, scales_ready = sem("diff_ready"), sem("scales_ready")
                    dve_order = sem("dve_order_d")
                    block = ph.enter_context(nc.Block())

                    @block.tensor
                    def _(e):
                        for i, name in enumerate(("wig", "wfg")):
                            for b in range(B):
                                last = e.matmul(bank[6 + i][32 * b:32 * b + 32, :], w[name], XT[:, S * b:S * b + S],
                                                start=True, stop=True)
                        last.then_inc(gates_made, 1)
                        for t in range(NT):
                            if t >= 2:
                                e.wait_ge(proj_read_v, t - 1)
                                e.wait_ge(proj_read_s, t - 1)
                                e.wait_ge(router_read, t - 1)
                            xt = XT[:, P * t:P * t + P]
                            wall = Bw[:, B_AT["wv"].start:B_AT["wk"].stop]
                            e.matmul(bank[t % 2][:, 0:3 * D], xt, wall, start=True, stop=True).then_inc(proj_made, 1)
                            e.matmul(bank[2 + t % 2][:, 0:E1], xt, w["router"], start=True, stop=True).then_inc(router_made, 1)
                            if t % 2 == 1:
                                i = t // 2
                                if i >= 2:
                                    e.wait_ge(qk_read, i - 1)
                                e.matmul(bank[4 + i % 2][:, :], w["wq" if i % 2 == 0 else "wk"],
                                         XT[:, S * (i // 2):S * (i // 2) + S], start=True, stop=True).then_inc(qk_made, 1)
                        e.wait_ge(rows_ready, 3)
                        e.wait_ge(proj_read_v, NT)
                        e.wait_ge(proj_read_s, NT)
                        e.wait_ge(router_read, NT)
                        for i, name in enumerate(("a", "M", "m")):
                            for j in range(TPB):
                                last = e.transpose(bank[i][:, P * j:P * j + P], g[name][:, P * j:P * j + P], a["ident"])
                        last.then_inc(rows_turned, 1)
                        e.wait_ge(R_made, 1)
                        for j in range(TPB):
                            last = e.matmul(bank[3][:, P * j:P * j + P], a["ones"], Rdiag[:, j, :], start=True, stop=True)
                        last.then_inc(rows_turned, 1)

                    @block.scalar
                    def _(e):
                        e.wait_ge(gates_made, 1)
                        e.wait_ge(bias_ready, 1)
                        e.activation(g["tf"][:, :], bank[7][:, :], ACT.Tanh, bias=bias15[:, 1:2], scale=1 / CAP).then_inc(tanh_ready, 1)
                        e.activation(g["ti"][:, :], bank[6][:, :], ACT.Tanh, bias=bias15[:, 0:1], scale=1 / CAP).then_inc(tanh_ready, 1)
                        e.wait_ge(abs_ready, 1)
                        e.activation(g["y"][:, :], g["y"][:, :], ACT.Exp, scale=-1.0).then_inc(y_ready, 1)
                        for t in range(NT):
                            e.wait_ge(proj_made, t + 1)
                            e.wait_ge(proj_read_v, t + 1)
                            e.activation(expO[:, t, :], bank[t % 2][:, D:2 * D], ACT.Exp, scale=-1.0)
                            e.copy(K[:, t, :], bank[t % 2][:, 2 * D:3 * D]).then_inc(proj_read_s, 1)
                            if t % 2 == 1:
                                i = t // 2
                                e.wait_ge(qk_made, i + 1)
                                dst = (qT, kT)[i % 2][:, S * (i // 2):S * (i // 2) + S]
                                if i % 2 == 0:
                                    e.mul(dst, bank[4][:, :], DH ** -0.5).then_inc(qk_read, 1)
                                else:
                                    e.copy(dst, bank[5][:, :]).then_inc(qk_read, 1)
                        e.wait_ge(u_ready, 1)
                        e.activation(g["ln"][:, :], g["u"][:, :], ACT.Ln).then_inc(ln_ready, 1)
                        e.wait_ge(rows_turned, 1)
                        e.activation(floor[:, :, :], bank[2][:, :].rearrange("p (j r) -> p j r", r=P), ACT.Exp, scale=-1.0)
                        e.wait_ge(rows_turned, 2)
                        e.copy(R[:, :, :], bank[3][:, :].rearrange("p (j r) -> p j r", r=P)).then_inc(R_ready, 1)
                        e.wait_ge(diff_ready, 3)
                        e.activation(k_scale[:, :, :], k_scale[:, :, :], ACT.Exp)
                        e.activation(q_scale[:, :, :], q_scale[:, :, :], ACT.Exp)
                        e.activation(decay[:, :, :], decay[:, :, :], ACT.Exp)

                    @block.vector
                    def _(e):
                        link = chain(e, dve_order)
                        e.tensor_scalar(bias15[:, :], Bw[:, B_AT["big"].start:B_AT["bfg"].stop], 1 / CAP, None,
                                        ALU.mult).then_inc(bias_ready, 1)
                        e.memset(VA[:, :, :, DH:DV], 1.0)
                        e.memset(g["ones"][:, :], 1.0)
                        e.tensor_copy(masked_bf[:, :, :],
                                      w["masked"].rearrange("p (o m) -> p o m", o=1).to_broadcast([P, TPB, P]))
                        e.wait_ge(tanh_ready, 2)
                        link(e.tensor_scalar(g["x"][:, :], g["tf"][:, :], CAP, None, ALU.mult))
                        e.scalar_tensor_tensor(g["y"][:, :], g["x"][:, :], -1.0, g["x"][:, :], ALU.mult, ALU.max).then_inc(abs_ready, 1)
                        e.tensor_scalar(g["ti"][:, :], g["ti"][:, :], CAP, None, ALU.mult)

                        def evacuate(t):
                            e.wait_ge(proj_made, t + 1)
                            e.tensor_copy(VA[:, t, :, 0:DH],
                                          bank[t % 2][:, 0:D].rearrange("p (h v) -> p h v", h=NH)).then_inc(proj_read_v, 1)
                            e.wait_ge(router_made, t + 1)
                            e.tensor_tensor(logits[:, t, :], bank[2 + t % 2][:, 0:E1], w["expert_bias"],
                                            ALU.add).then_inc(router_read, 1)
                        for t in range(2):
                            evacuate(t)
                        e.wait_ge(y_ready, 1)
                        e.tensor_scalar(g["u"][:, :], g["y"][:, :], 1.0, None, ALU.add).then_inc(u_ready, 1)
                        e.wait_ge(u_ready, 1)
                        link(e.scalar_tensor_tensor(g["c"][:, :], g["u"][:, :], 1.0, g["y"][:, :], ALU.subtract, ALU.subtract))
                        link(e.reciprocal(g["ru"][:, :], g["u"][:, :]))
                        link(e.tensor_tensor(g["c"][:, :], g["c"][:, :], g["ru"][:, :], ALU.mult))
                        link(e.scalar_tensor_tensor(g["x"][:, :], g["x"][:, :], 0.0, g["c"][:, :], ALU.min, ALU.add))
                        for t in range(2, NT):
                            evacuate(t)
                        e.wait_ge(ln_ready, 1)
                        link(e.tensor_tensor(g["x"][:, :], g["x"][:, :], g["ln"][:, :], ALU.subtract))
                        link(e.tensor_tensor_scan(g["lf"][:, :], g["ones"][:, :], g["x"][:, :], 0.0, ALU.mult, ALU.add))
                        e.tensor_tensor(g["a"][:, :], g["ti"][:, :], g["lf"][:, :], ALU.subtract).then_inc(rows_ready, 1)
                        e.wait_ge(rows_ready, 1)
                        e.tensor_tensor_scan(g["M"][:, :], g["a"][:, :], g["a"][:, :], -3e38, ALU.max, ALU.max).then_inc(rows_ready, 1)
                        e.wait_ge(rows_ready, 2)
                        e.tensor_tensor(g["m"][:, :], g["lf"][:, :], g["M"][:, :], ALU.add).then_inc(rows_ready, 1)
                        for j in range(TPB):
                            last = e.tensor_scalar(Rdiag[:, j, :], a["ident"], g["M"][:, P * j + P - 1:P * j + P], None, ALU.mult)
                        last.then_inc(R_made, 1)
                        e.tensor_copy(ah[:, :], g["a"][:, :])
                        link(e.tensor_scalar(mh[:, :], g["M"][:, :], -1.0, None, ALU.mult))
                        e.tensor_tensor(al[:, :], g["a"][:, :], ah[:, :].bitcast(F32), ALU.subtract)
                        e.scalar_tensor_tensor(ml[:, :], g["M"][:, :], -1.0, mh[:, :].bitcast(F32), ALU.mult, ALU.subtract)
                        e.tensor_copy(lane[:, :, :, :],
                                      a["ident"].rearrange("p (b r) -> p b r", b=B)[:, :, 0:NH]
                                      .rearrange("p b (h o) -> p b h o", o=1).to_broadcast([P, B, NH, P]))
                        e.wait_ge(R_ready, 1)
                        e.tensor_tensor(k_scale[:, :, :], bank[0][:, :].rearrange("p (j r) -> p j r", r=P), R[:, :, :],
                                        ALU.subtract).then_inc(diff_ready, 1)
                        e.tensor_tensor(q_scale[:, :, :], R[:, 0:TPB - 1, :],
                                        bank[1][:, P:S].rearrange("p (j r) -> p j r", r=P), ALU.subtract).then_inc(diff_ready, 1)
                        e.tensor_tensor(decay[:, :, :], R[:, 0:TPB - 1, :], R[:, 1:TPB, :], ALU.subtract).then_inc(diff_ready, 1)

                with ExitStack() as ph:
                    Dm = sb("Dm", [P, 2, S], ctx=ph)
                    CT = sb("CT", [P, 2, NH, S], ctx=ph)
                    KS = sb("KS", [P, 2, NH, DH], ctx=ph)
                    St = sb("St", [P, 2, NH, DV], ctx=ph)
                    inc = sb("inc", [P, NH, DV], ctx=ph)
                    part = sb("part", [P, NH, DV], ctx=ph)
                    d_made, d_ready, st_made, c_ready = sem("d_made"), sem("d_ready"), sem("st_made"), sem("c_ready")
                    ks_ready, kv_made, state_ready = sem("ks_ready"), sem("kv_made"), sem("state_ready")
                    inter_made, inter_read, intra_made, o_ready = sem("inter_made"), sem("inter_read"), sem("intra_made"), sem("o_ready")
                    dve_order = sem("dve_order_e")
                    block = ph.enter_context(nc.Block())
                    wide = NH * DV

                    @block.tensor
                    def _(e):
                        def unit(v):
                            b, h = v // NH, v % NH
                            if v >= 2:
                                e.wait_ge(d_ready, v - 1)
                                e.wait_ge(c_ready, v - 1)
                            dm, st = bank[v % 2], bank[2 + v % 2]
                            e.matmul(dm[:, :], lane[:, b, h, :], mh[:, :], start=True, stop=False)
                            e.matmul(dm[:, :], lane[:, b, h, :], ml[:, :], start=False, stop=False)
                            for j in range(TPB):
                                js = slice(P * j, P * j + P)
                                e.matmul(dm[:, js], ah[:, js], lane[:, b, h, :], start=False, stop=False, skip_group_check=True)
                                e.matmul(dm[:, js], al[:, js], lane[:, b, h, :], start=False, stop=False, skip_group_check=True)
                            e.matmul(dm[:, :], ident_bf[:, :], masked_bf[:, :, :], start=False, stop=True).then_inc(d_made, 1)
                            for j in range(TPB):
                                ts = slice(S * b + P * j, S * b + P * j + P)
                                hs = slice(DH * h, DH * h + DH)
                                last = e.matmul(st[:, P * j:P * j + P], kT[hs, ts], qT[hs, ts], start=True, stop=True)
                            last.then_inc(st_made, 1)

                        def tile(t):
                            b, j = t // TPB, t % TPB
                            n = (TPB - 1) * b + j
                            e.wait_ge(c_ready, NH * b + NH)
                            if t >= 2:
                                e.wait_ge(o_ready, t - 1)
                            for h in range(NH):
                                last = e.matmul(bank[4 + t % 2][:, DV * h:DV * h + DV], CT[:, b % 2, h, P * j:P * j + P],
                                                VA[:, t, h, :], start=True, stop=True)
                            last.then_inc(intra_made, 1)
                            if j < TPB - 1:
                                e.wait_ge(ks_ready, n + 1)
                                if n:
                                    e.wait_ge(state_ready, n)
                                e.matmul(bank[7][:, 0:wide], KS[:, n % 2, :, :], VA[:, t, :, :],
                                         start=True, stop=True).then_inc(kv_made, 1)
                            if j:
                                e.wait_ge(state_ready, n)
                                if n > 1:
                                    e.wait_ge(inter_read, n - 1)
                                e.matmul(bank[6][:, 0:wide], qT[:, P * t:P * t + P], St[:, (j - 1) % 2, :, :],
                                         start=True, stop=True).then_inc(inter_made, 1)

                        for v in range(NH):
                            unit(v)
                        for t in range(NT):
                            if t + NH < B * NH:
                                unit(t + NH)
                            tile(t)

                    @block.scalar
                    def _(e):
                        for v in range(B * NH):
                            e.wait_ge(d_made, v + 1)
                            if v >= 2:
                                e.wait_ge(c_ready, v - 1)
                            e.activation(Dm[:, v % 2, :], bank[v % 2][:, :], ACT.Exp).then_inc(d_ready, 1)

                    @block.vector
                    def _(e):
                        link = chain(e, dve_order)

                        def per_head(m, b, n):
                            return m[:, 32 * b:32 * b + NH].rearrange("p (h o) -> p h o", o=1).to_broadcast([P, NH, n])

                        def product(v):
                            b, h = v // NH, v % NH
                            e.wait_ge(d_ready, v + 1)
                            e.wait_ge(st_made, v + 1)
                            if b >= 2:
                                e.wait_ge(intra_made, NH * (b - 1))
                            e.tensor_tensor(CT[:, b % 2, h, :], Dm[:, v % 2, :], bank[2 + v % 2][:, :], ALU.mult).then_inc(c_ready, 1)

                        def tile(t):
                            b, j = t // TPB, t % TPB
                            n = (TPB - 1) * b + j
                            if j < TPB - 1:
                                if n >= 2:
                                    e.wait_ge(kv_made, n - 1)
                                e.tensor_tensor(KS[:, n % 2, :, :], K[:, t, :].rearrange("p (h d) -> p h d", h=NH),
                                                per_head(k_scale[:, j, :], b, DH), ALU.mult).then_inc(ks_ready, 1)
                            po = bank[4 + t % 2][:, 0:wide].rearrange("p (h d) -> p h d", h=NH)
                            pi = bank[6][:, 0:wide].rearrange("p (h d) -> p h d", h=NH)
                            if j:
                                e.wait_ge(inter_made, n)
                                e.tensor_tensor(part[:, :, :], pi, per_head(q_scale[:, j - 1, :], b, DV), ALU.mult).then_inc(inter_read, 1)
                                e.wait_ge(inter_read, n)
                                e.wait_ge(intra_made, t + 1)
                                e.tensor_tensor(O[:, t, :, :], part[:, :, :], po, ALU.add).then_inc(o_ready, 1)
                            else:
                                e.wait_ge(intra_made, t + 1)
                                e.tensor_copy(O[:, t, :, :], po).then_inc(o_ready, 1)
                            if j < TPB - 1:
                                e.wait_ge(kv_made, n + 1)
                                kv = bank[7][:, 0:wide].rearrange("p (h d) -> p h d", h=NH)
                                blocks = w["diag"].rearrange("p (h d) -> p h d", h=NH)
                                if j == 0:
                                    e.tensor_tensor(St[:, 0, :, :], kv, blocks, ALU.mult).then_inc(state_ready, 1)
                                    e.wait_ge(state_ready, n + 1)
                                else:
                                    e.tensor_tensor(inc[:, :, :], kv, blocks, ALU.mult)
                                    link(e.tensor_tensor(St[:, j % 2, :, :], St[:, (j - 1) % 2, :, :],
                                                         per_head(decay[:, j - 1, :], b, DV), ALU.mult))
                                    e.tensor_tensor(St[:, j % 2, :, :], St[:, j % 2, :, :], inc[:, :, :], ALU.add).then_inc(state_ready, 1)
                                    e.wait_ge(state_ready, n + 1)

                        for v in range(NH):
                            product(v)
                        for t in range(NT):
                            if t + NH < B * NH:
                                product(t + NH)
                            tile(t)

                with ExitStack() as ph:
                    pexp = sb("pexp", [P, NT, E1], ctx=ph)
                    zap = sb("zap1", [P, TPB, E1], ctx=ph)
                    top = sb("top1", [P, TPB, K1], ctx=ph)
                    tot = sb("tot1", [P, TPB], ctx=ph)
                    cw = sb("cw1", [P, TPB, E1], ctx=ph)
                    parts = sb("parts1", [P, 2, TPB, C1 * RPC], BF16, ctx=ph)
                    combT = sb("combT", [TB, 2, NB, S], BF16, ctx=ph)
                    dn = sb("dn", [P, NT, NH], ctx=ph)
                    mu = sb("mu", [P, NT, NH], ctx=ph)
                    var = sb("var", [P, NT, NH], ctx=ph)
                    hc = sb("hc", [P, NT, NH, DH], ctx=ph)
                    sq = sb("sq", [P, TPB, NH, DH], ctx=ph)
                    HT = sb("HT", [P, 2, S], ctx=ph)
                    pexp_ready, var_ready, std_ready = sem("pexp_ready"), sem("var_ready"), sem("head_std_ready")
                    parts_ready, comb_turned, comb_copied = sem("parts1_ready"), sem("comb1_turned"), sem("comb1_copied")
                    comb_stored = [sem(f"comb_stored{i}") for i in range(2)]
                    ho_ready, ho_turned, ht_ready, s_made = sem("ho_ready"), sem("ho_turned"), sem("ht_ready"), sem("s1_made")
                    dve_order = sem("dve_order_f")
                    block = ph.enter_context(nc.Block())

                    @block.sync
                    def _(e):
                        rows = comb_dram.rearrange("(k r) n -> r k n", r=TB)
                        for b in range(B):
                            e.wait_ge(comb_copied, b + 1)
                            e.dma_start(rows[:, :, S * b:S * b + S], combT[:, b % 2, :, :]).then_inc(comb_stored[b % 2], 16)
                        for i in range(2):
                            e.wait_ge(comb_stored[i], 16 * (B // 2))

                    @block.scalar
                    def _(e):
                        for b in range(B):
                            tb = slice(TPB * b, TPB * b + TPB)
                            e.activation(pexp[:, tb, :], logits[:, tb, :], ACT.Exp, scale=-1.0).then_inc(pexp_ready, 1)
                        for b in range(B):
                            tb = slice(TPB * b, TPB * b + TPB)
                            e.wait_ge(var_ready, b + 1)
                            e.activation(var[:, tb, :], var[:, tb, :], ACT.Sqrt).then_inc(std_ready, 1)
                        for b in range(B):
                            e.wait_ge(comb_turned, b + 1)
                            if b >= 2:
                                e.wait_ge(comb_stored[b % 2], 16)
                            for k in range(NB):
                                last = e.copy(combT[:, b % 2, k, :], bank[k][0:TB, 0:S // 2].bitcast(BF16))
                            last.then_inc(comb_copied, 1)
                            e.wait_ge(ho_turned, b + 1)
                            e.copy(HT[:, b % 2, :], bank[4 + b % 2][:, :]).then_inc(ht_ready, 1)
                            e.wait_ge(s_made, b + 1)
                            e.copy(S1[:, TPB * b:TPB * b + TPB, :],
                                   bank[6 + b % 2][:, :].rearrange("p (t d) -> p t d", d=D))

                    @block.vector
                    def _(e):
                        link = chain(e, dve_order)

                        def flat(m, tb):
                            return m[:, tb, :].rearrange("p t h -> p (t h)")

                        def spread(m, tb):
                            return m[:, tb, :].rearrange("p t (h o) -> p (t h) o", o=1).to_broadcast([P, TPB * NH, DH])

                        for b in range(B):
                            tb = slice(TPB * b, TPB * b + TPB)
                            th = hc[:, tb, :, :].rearrange("p t h d -> p (t h) d")
                            sums = O[:, tb, :, DH:DV].rearrange("p t h o -> p t (h o)")
                            vals = O[:, tb, :, 0:DH].rearrange("p t h d -> p (t h) d")
                            sqv = sq[:, :, :, :].rearrange("p t h d -> p (t h) d")
                            link(e.scalar_tensor_tensor(dn[:, tb, :], sums, -1.0, sums, ALU.mult, ALU.max))
                            link(e.tensor_tensor(dn[:, tb, :], dn[:, tb, :], floor[:, :, 32 * b:32 * b + NH], ALU.max))
                            link(e.tensor_scalar(flat(dn, tb), flat(dn, tb), BACKEND_EPS, None, ALU.add))
                            link(e.reciprocal(flat(dn, tb), flat(dn, tb)))
                            link(e.tensor_tensor(th, vals, spread(dn, tb), ALU.mult))
                            link(e.tensor_reduce(flat(mu, tb), th, AX.X, ALU.add))
                            link(e.tensor_scalar(flat(mu, tb), flat(mu, tb), 1 / DH, None, ALU.mult))
                            link(e.tensor_tensor(th, th, spread(mu, tb), ALU.subtract))
                            link(e.tensor_tensor(sqv, th, th, ALU.mult))
                            link(e.tensor_reduce(flat(var, tb), sqv, AX.X, ALU.add))
                            e.tensor_scalar(flat(var, tb), flat(var, tb), 1 / DH, NORM_EPS, ALU.mult, ALU.add).then_inc(var_ready, 1)
                        for b in range(B):
                            tb = slice(TPB * b, TPB * b + TPB)
                            e.wait_ge(pexp_ready, b + 1)
                            link(e.tensor_scalar(pexp[:, tb, :], pexp[:, tb, :], 1.0, None, ALU.add))
                            link(e.reciprocal(pexp[:, tb, :], pexp[:, tb, :]))
                            for j in range(TPB):
                                last = e.max(top[:, j, :], pexp[:, TPB * b + j, :])
                            link(last)
                            for j in range(TPB):
                                e.match_replace(zap[:, j, :], top[:, j, :], pexp[:, TPB * b + j, :], 0.0)
                            link(e.tensor_reduce(tot[:, :], top[:, :, :], AX.X, ALU.add))
                            link(e.tensor_scalar(tot[:, :], tot[:, :], 1e-9, None, ALU.add))
                            link(e.reciprocal(tot[:, :], tot[:, :]))
                            e.tensor_tensor(cw[:, :, :], pexp[:, tb, :], zap[:, :, :], ALU.subtract)
                            link(e.tensor_scalar(tot[:, :], tot[:, :], ROUTED_SCALE, None, ALU.mult))
                            link(e.tensor_tensor(cw[:, :, :], cw[:, :, :],
                                                 tot[:, :].rearrange("p (t o) -> p t o", o=1).to_broadcast([P, TPB, E1]), ALU.mult))
                            pv = parts[:, b % 2, :, :].rearrange("p t (c h e) -> p t c h e", c=C1, h=3)
                            cv = cw[:, :, :].rearrange("p t (c e) -> p t c e", c=C1)
                            if b >= 2:
                                e.wait_ge(comb_turned, b - 1)
                            link(e.tensor_copy(pv[:, :, :, 0, :], cv))
                            link(e.tensor_tensor(cv, cv, pv[:, :, :, 0, :], ALU.subtract))
                            link(e.tensor_copy(pv[:, :, :, 1, :], cv))
                            e.tensor_tensor(pv[:, :, :, 2, :], cv, pv[:, :, :, 1, :], ALU.subtract).then_inc(parts_ready, 1)
                            th = hc[:, tb, :, :].rearrange("p t h d -> p (t h) d")
                            rows = hc[:, tb, :, :].rearrange("p t h d -> p t (h d)")
                            e.wait_ge(std_ready, b + 1)
                            e.tensor_scalar(expO[:, tb, :], expO[:, tb, :], 1.0, None, ALU.add)
                            link(e.reciprocal(flat(var, tb), flat(var, tb)))
                            link(e.tensor_tensor(th, th, spread(var, tb), ALU.mult))
                            link(e.reciprocal(expO[:, tb, :], expO[:, tb, :]))
                            link(e.tensor_tensor(rows, rows, w["norm_w"].rearrange("p (o d) -> p o d", o=1)
                                                 .to_broadcast([P, TPB, D]), ALU.mult))
                            e.tensor_tensor(rows, rows, expO[:, tb, :], ALU.mult).then_inc(ho_ready, 1)

                    @block.tensor
                    def _(e):
                        for b in range(B):
                            e.wait_ge(parts_ready, b + 1)
                            if b:
                                e.wait_ge(comb_copied, b)
                            for k in range(NB):
                                for j in range(TPB):
                                    last = e.transpose(bank[k][0:TB, :].bitcast(BF16)[:, P * j:P * j + P],
                                                       parts[:, b % 2, j, TB * k:TB * k + TB], ident_bf[:, :])
                            last.then_inc(comb_turned, 1)
                            e.wait_ge(ho_ready, b + 1)
                            for j in range(TPB):
                                last = e.transpose(bank[4 + b % 2][:, P * j:P * j + P],
                                                   hc[:, TPB * b + j, :, :].rearrange("p h d -> p (h d)"), a["ident"])
                            last.then_inc(ho_turned, 1)
                            e.wait_ge(ht_ready, b + 1)
                            for j in range(TPB):
                                last = e.matmul(bank[6 + b % 2][:, P * j:P * j + P], HT[:, b % 2, P * j:P * j + P], w["wdown"],
                                                start=True, stop=True)
                            last.then_inc(s_made, 1)

            with ExitStack() as ph:
                G = N // S
                PAIR = 2 * G
                TURNS = C1 // 2
                LAG = 3
                zeros = sb("zeros", [P, P], ctx=ph)
                staged = sb("staged", [P, 2, 2 * P], ctx=ph)
                gate_hi = sb("gate_hi", [P, 2, P], F32R, ctx=ph)
                gate_lo = sb("gate_lo", [P, 2, P], F32R, ctx=ph)
                down_hi = sb("down_hi", [P, 2, P], F32R, ctx=ph)
                down_lo = sb("down_lo", [P, 2, P], F32R, ctx=ph)
                comb = sb("comb", [RPC, 2, N], BF16, ctx=ph)
                sel1_bf = sb("sel1_bf", [RPC, P], BF16, ctx=ph)
                act = sb("act", [P, 4, S], ctx=ph)
                hid = sb("hid", [P, 4, S], ctx=ph)
                hid_hi = sb("hid_hi", [P, 4, S], F32R, ctx=ph)
                hid_lo = sb("hid_lo", [P, 4, S], F32R, ctx=ph)
                shared = sb("shared", [H1, 2, S], ctx=ph)
                yT = sb("yT", [P, N], ctx=ph)
                res = sb("res", [P, NT, D], ctx=ph)
                staged_in = [sem(f"staged_in{i}") for i in range(2)]
                comb_in = [sem(f"comb_in{i}") for i in range(2)]
                gate_hi_ready, gate_ready = sem("gate_hi_ready"), sem("gate_parts_ready")
                down_hi_ready, down_ready = sem("down_hi_ready"), sem("down_parts_ready")
                zeros_ready, sel_ready, sh_made, sh_ready = sem("zeros_ready"), sem("sel_ready"), sem("sh_made"), sem("sh_ready")
                up_made, comb_made, act_ready = sem("up_made"), sem("comb_made"), sem("act1_ready")
                hid_ready, hi_ready, lo_ready, y_made = sem("hid_ready"), sem("hi_ready"), sem("lo_ready"), sem("y1_made")
                yt_ready, y_turned, res_ready, x_ready = sem("yt_ready"), sem("y_turned"), sem("res_ready"), sem("x_ready")
                stored = [sem(f"stored{b}") for b in range(B)]
                block = ph.enter_context(nc.Block())

                @block.sync
                def _(e):
                    def load(i, s, c):
                        e.dma_start(staged[:, s, :], w_in[c, :, :].rearrange("o p n -> (o p) n")).then_inc(staged_in[s], 16)

                    def load_comb(s, r):
                        e.dma_start(comb[:, s, :], comb_dram[r, :]).then_inc(comb_in[s], 16)

                    for s in range(2):
                        load(0, s, slice(s, s + 1))
                        load_comb(s, slice(RPC * s, RPC * s + RPC))
                    with e.Fori(1, TURNS) as i:
                        for s in range(2):
                            e.wait_ge(down_ready, i * 2 + (s - 1))
                            load(i, s, bass.ds(i * 2 + s, 1))
                            e.wait_ge(comb_made, i * PAIR + (G * s - G))
                            load_comb(s, bass.ds(i * (2 * RPC) + RPC * s, RPC))
                    for b in range(B):
                        tb = slice(TPB * b, TPB * b + TPB)
                        e.wait_ge(x_ready, b + 1)
                        e.dma_start(out_rows[:, tb, :], X[:, tb, :]).then_inc(stored[b], 16)
                    for b in range(B):
                        e.wait_ge(stored[b], 16)

                @block.gpsimd
                def _(e):
                    def split(i, s):
                        c = i * 2 + s
                        e.wait_ge(staged_in[s], i * 16 + 16)
                        if not (isinstance(i, int) and i == 0):
                            e.wait_ge(up_made, i * PAIR + (G * s - G))
                        e.tensor_tensor(gate_hi[:, s, :], staged[:, s, 0:P], zeros[:, :], ALU.subtract).then_inc(gate_hi_ready, 1)
                        e.wait_ge(gate_hi_ready, c + 1)
                        e.tensor_tensor(gate_lo[:, s, :], staged[:, s, 0:P], gate_hi[:, s, :].bitcast(F32),
                                        ALU.subtract).then_inc(gate_ready, 1)
                        if not (isinstance(i, int) and i == 0):
                            e.wait_ge(y_made, i * PAIR + (G * s - G))
                        e.tensor_tensor(down_hi[:, s, :], staged[:, s, P:2 * P], zeros[:, :], ALU.subtract).then_inc(down_hi_ready, 1)
                        e.wait_ge(down_hi_ready, c + 1)
                        e.tensor_tensor(down_lo[:, s, :], staged[:, s, P:2 * P], down_hi[:, s, :].bitcast(F32),
                                        ALU.subtract).then_inc(down_ready, 1)

                    e.memset(zeros[:, :], 0.0).then_inc(zeros_ready, 1)
                    e.wait_ge(zeros_ready, 1)
                    for s in range(2):
                        split(0, s)
                    with e.Fori(1, TURNS) as i:
                        for s in range(2):
                            split(i, s)

                @block.tensor
                def _(e):
                    for g in range(G):
                        if g >= 2:
                            e.wait_ge(sh_ready, g - 1)
                        e.matmul(bank[g % 2][0:H1, :], w["shared_gate"], XT[:, S * g:S * g + S],
                                 start=True, stop=True).then_inc(sh_made, 1)
                        if g:
                            e.wait_ge(sh_ready, g)
                            e.matmul(bank[3 + g][:, :], w["shared_down"][0:H1, :], shared[:, (g - 1) % 2, :],
                                     start=True, stop=False)
                    e.wait_ge(sh_ready, G)
                    e.matmul(bank[3 + G][:, :], w["shared_down"][0:H1, :], shared[:, (G - 1) % 2, :], start=True, stop=False)

                    def up(i, j):
                        s, g = (j // G) % 2, j % G
                        if g == 0:
                            e.wait_ge(gate_ready, i * 2 + (j // G + 1))
                        if not (isinstance(i, int) and i == 0 and j < 2):
                            e.wait_ge(act_ready, i * PAIR + (j - 1))
                        xs = slice(S * g, S * g + S)
                        e.matmul(bank[j % 2][:, :], gate_hi[:, s, :], XH[:, xs], start=True, stop=False)
                        e.matmul(bank[j % 2][:, :], gate_hi[:, s, :], XL[:, xs], start=False, stop=False)
                        e.matmul(bank[j % 2][:, :], gate_lo[:, s, :], XH[:, xs], start=False, stop=True).then_inc(up_made, 1)
                        if g == 0:
                            e.wait_ge(comb_in[s], i * 16 + 16 * (j // PAIR + 1))
                        if not (isinstance(i, int) and i == 0 and j < 2):
                            e.wait_ge(hid_ready, i * PAIR + (j - 1))
                        e.matmul(bank[2 + j % 2][:, :], sel1_bf[:, :], comb[:, s, xs], start=True, stop=True).then_inc(comb_made, 1)

                    def down(i, j, last=False):
                        s, g = (j // G) % 2, j % G
                        if g == 0:
                            e.wait_ge(down_ready, i * 2 + (j // G + 1))
                        e.wait_ge(lo_ready, i * PAIR + (j + 1))
                        y = bank[4 + g][:, :]
                        e.matmul(y, down_hi[:, s, :], hid_hi[:, j % 4, :], start=False, stop=False)
                        e.matmul(y, down_hi[:, s, :], hid_lo[:, j % 4, :], start=False, stop=False)
                        e.matmul(y, down_lo[:, s, :], hid_hi[:, j % 4, :], start=False, stop=last).then_inc(y_made, 1)

                    e.wait_ge(sel_ready, 1)
                    for j in range(LAG):
                        up(0, j)
                    with e.Fori(0, TURNS - 1) as i:
                        for j in range(PAIR):
                            down(i, j)
                            up(i, j + LAG)
                    for j in range(PAIR):
                        down(TURNS - 1, j, last=(j >= G))
                        if j + LAG < PAIR:
                            up(TURNS - 1, j + LAG)
                    for b in range(B):
                        e.wait_ge(yt_ready, b + 1)
                        for j in range(TPB):
                            last = e.transpose(bank[b][:, P * j:P * j + P], yT[:, S * b + P * j:S * b + P * j + P], a["ident"])
                        last.then_inc(y_turned, 1)

                @block.scalar
                def _(e):
                    for g in range(G):
                        e.wait_ge(sh_made, g + 1)
                        e.activation(shared[:, g % 2, :], bank[g % 2][0:H1, :], ACT.Silu).then_inc(sh_ready, 1)

                    def silu(i, j):
                        e.wait_ge(up_made, i * PAIR + (j + 1))
                        if not (isinstance(i, int) and i == 0 and j < 2):
                            e.wait_ge(hid_ready, i * PAIR + (j - 1))
                        e.activation(act[:, j % 4, :], bank[j % 2][:, :], ACT.Silu).then_inc(act_ready, 1)

                    def high(i, j):
                        e.wait_ge(hid_ready, i * PAIR + (j + 1))
                        e.copy(hid_hi[:, j % 4, :], hid[:, j % 4, :]).then_inc(hi_ready, 1)

                    silu(0, 0)
                    with e.Fori(0, TURNS - 1) as i:
                        for j in range(PAIR):
                            silu(i, j + 1)
                            high(i, j)
                    for j in range(PAIR):
                        if j + 1 < PAIR:
                            silu(TURNS - 1, j + 1)
                        high(TURNS - 1, j)
                    for b in range(B):
                        e.wait_ge(y_made, C1 * G - (B - 1) + b)
                        e.activation(yT[:, S * b:S * b + S], bank[4 + b][:, :], ACT.Silu).then_inc(yt_ready, 1)

                @block.vector
                def _(e):
                    e.tensor_copy(sel1_bf[:, :], a["sel1"][0:RPC, :]).then_inc(sel_ready, 1)

                    def weigh(i, j):
                        e.wait_ge(act_ready, i * PAIR + (j + 1))
                        e.wait_ge(comb_made, i * PAIR + (j + 1))
                        e.tensor_tensor(hid[:, j % 4, :], act[:, j % 4, :], bank[2 + j % 2][:, :], ALU.mult).then_inc(hid_ready, 1)

                    def low(i, j):
                        e.wait_ge(hi_ready, i * PAIR + (j + 1))
                        e.tensor_tensor(hid_lo[:, j % 4, :], hid[:, j % 4, :], hid_hi[:, j % 4, :].bitcast(F32),
                                        ALU.subtract).then_inc(lo_ready, 1)

                    weigh(0, 0)
                    with e.Fori(0, TURNS - 1) as i:
                        for j in range(PAIR):
                            weigh(i, j + 1)
                            low(i, j)
                    for j in range(PAIR):
                        if j + 1 < PAIR:
                            weigh(TURNS - 1, j + 1)
                        low(TURNS - 1, j)
                    for b in range(B):
                        tb = slice(TPB * b, TPB * b + TPB)
                        e.wait_ge(y_turned, b + 1)
                        e.tensor_tensor(res[:, tb, :], S1[:, tb, :], bank[b][:, :].rearrange("p (t d) -> p t d", d=D),
                                        ALU.mult).then_inc(res_ready, 1)
                        e.wait_ge(res_ready, b + 1)
                        e.tensor_tensor(X[:, tb, :], X[:, tb, :], res[:, tb, :], ALU.add).then_inc(x_ready, 1)


def kernel(**inputs):
    import numpy as np
    import concourse.bacc as bacc
    from concourse.bass_utils import run_bass_kernel_spmd

    i = {k: np.asarray(v) for k, v in inputs.items()}
    f = np.float32

    def rows(v):
        return np.tile(np.reshape(v, (1, -1)), (P, 1))

    def down(m, n=P):
        out = np.zeros((n,) + m.shape[1:], f)
        out[:m.shape[0]] = m
        return out

    turn = np.zeros((P, P), f)
    for k in range(0, P, 2):
        turn[k, k + 1], turn[k + 1, k] = -1, 1
    sel0 = np.zeros((P, C0, P), f)
    for r in range(R0):
        c, e = r // (3 * EPC0), r % EPC0
        sel0[r, c, H0 * e:H0 * e + H0] = 1
    sel1 = np.zeros((P, P), f)
    for r in range(RPC):
        e = r % EPC1
        sel1[r, H1 * e:H1 * e + H1] = 1
    masked = np.where(np.arange(P)[:, None] > np.arange(P)[None, :], MASKED, 0).astype(f)
    diag = np.zeros((P, NH, DV), f)
    for h in range(NH):
        diag[DH * h:DH * h + DH, h] = 1

    a = dict(ident=np.eye(P, dtype=f), turn=turn, ones=np.ones((P, P), f), sel0=sel0, sel1=sel1,
             expert_sel=i["L0_ffn_expert_sel"].T, keys=i["L0_ffn_keys"].transpose(1, 0, 2),
             values=i["L0_ffn_values"].reshape(C0, P, D).transpose(1, 0, 2),
             rot_c=np.repeat(i["L0_attn_rot_w"][:, 0::2], 2, axis=1).T,
             rot_s=np.repeat(i["L0_attn_rot_w"][:, 1::2], 2, axis=1).T,
             scale=rows(i["L0_attn_scale"]), bias=rows(i["L0_attn_bias"]), route_scale=rows(i["L0_ffn_route_scale"]))
    lanes = np.zeros((B, 32), f)

    def per_lane(v):
        out = lanes.copy()
        out[:, :NH] = v
        return out.reshape(P, 1)

    def per_col(m):
        out = np.zeros((P, 32), f)
        out[:, :NH] = m
        return out

    b = dict(masked=masked, wv=i["L1_attn_Wv"], wo=i["L1_attn_Wo"], wk=i["L1_attn_Wk"], wq=i["L1_attn_Wq"],
             wig=per_col(i["L1_attn_Wig"]), wfg=per_col(i["L1_attn_Wfg"]), router=i["L1_ffn_router_w"].T,
             wdown=i["L1_attn_Wdown"], norm_w=rows(i["L1_attn_norm_w"]), expert_bias=rows(i["L1_ffn_expert_bias"]),
             big=per_lane(i["L1_attn_big"]), bfg=per_lane(i["L1_attn_bfg"]),
             shared_gate=i["L1_ffn_w_gate_shared"].T, shared_down=down(i["L1_ffn_w_down_shared"].T), diag=diag)
    packed = {
        "x": i["L0_attn_Q"].reshape(N, D),
        "layer0": np.concatenate([a[k].reshape(P, n) for k, n in A_COLS.items()], axis=1),
        "layer1": np.concatenate([b[k].reshape(P, n) for k, n in B_COLS.items()], axis=1),
        "experts": np.concatenate([i["L1_ffn_w_gate"].reshape(C1, P, D).transpose(0, 2, 1),
                                   i["L1_ffn_w_down"].transpose(0, 2, 1).reshape(C1, P, D)], axis=2),
    }
    nc = bacc.Bacc("TRN2", target_bir_lowering=False, num_devices=1)
    arrays, args = {}, []
    for name, v in packed.items():
        v = np.ascontiguousarray(v)
        arrays[f"in_{name}"] = v
        args.append(nc.dram_tensor(f"in_{name}", v.shape, mybir.dt.from_np(v.dtype), kind="ExternalInput").ap())
    args.append(nc.dram_tensor("out", (N, D), F32, kind="ExternalOutput").ap())
    build(nc, *args)
    r = run_bass_kernel_spmd(nc, [arrays], core_ids=[0])
    return r.results[0]["out"].reshape(B, S, D)
```

```python
import concourse.bass as bass
from concourse import mybir
from contextlib import ExitStack

F32 = mybir.dt.float32
F32R = mybir.dt.float32r
BF16 = mybir.dt.bfloat16
ALU = mybir.AluOpType
ACT = mybir.ActivationFunctionType
AX = mybir.AxisListType

P = 128
D = 128
B, S = 4, 512
TPB = S // P
NT = B * TPB
N = NT * P
LN_EPS = 1e-5

E0, H0, K0 = 16, 32, 4
EPC0 = P // H0
C0 = E0 // EPC0
R0 = C0 * 3 * EPC0
PAD0 = 8 - K0

NH, DH = 4, 32
DV = DH + 1
CAP = 15.0
NORM_EPS = 1e-6
BACKEND_EPS = 1e-6
E1, H1, K1 = 160, 64, 8
EPC1 = P // H1
C1 = E1 // EPC1
ROUTED_SCALE = 2.5
TB = E1 // 2
NB = E1 // TB
MASKED = -30000.0

A_COLS = dict(ident=P, turn=P, ones=P, sel0=C0 * P, expert_sel=E0, keys=C0 * P, values=C0 * D,
              rot_c=3, rot_s=3, scale=1, bias=1, route_scale=1)
B_COLS = dict(masked=P, wv=D, wo=D, wk=D, wq=D, wig=32, wfg=32, router=E1, wdown=D, norm_w=D,
              expert_bias=E1, big=1, bfg=1, shared_gate=H1, shared_down=D, diag=NH * DV)


def places(cols):
    at, out = 0, {}
    for name, n in cols.items():
        out[name] = slice(at, at + n)
        at += n
    return out, at


A_AT, A_N = places(A_COLS)
B_AT, B_N = places(B_COLS)


def build(nc, x_in, a_in, b_in, w_in, x_out):
    x_rows = x_in.rearrange("(t p) d -> p t d", p=P)
    out_rows = x_out.rearrange("(t p) d -> p t d", p=P)
    comb_dram = nc.dram_tensor("combine_rows", (E1, N), F32, kind="Internal").ap()

    with ExitStack() as whole:
        def sem(name):
            return whole.enter_context(nc.semaphore(name))

        def chain(e, s):
            n = [0]

            def link(ins):
                n[0] += 1
                ins.then_inc(s, 1)
                e.wait_ge(s, n[0])
            return link

        def sb(name, shape, dt=F32, ctx=whole):
            return ctx.enter_context(nc.sbuf_tensor(name, shape, dt))

        bank = [whole.enter_context(nc.psum_tensor(f"bank{i}", [P, 512], F32)) for i in range(8)]

        A = sb("A", [P, A_N])
        Bw = sb("Bw", [P, B_N])
        a = {k: A[:, s] for k, s in A_AT.items()}
        w = {k: Bw[:, s] for k, s in B_AT.items()}
        X = sb("X", [P, NT, D])
        XT = sb("XT", [P, N])
        ident_bf = sb("ident_bf", [P, P], BF16)
        XH = sb("XH", [P, N], F32R)
        XL = sb("XL", [P, N], F32R)
        veps = sb("veps", [P, NT])
        rstd = sb("rstd", [P, NT])
        mv = sb("mv", [P, NT, 2])
        stats = sb("stats", [P, NT, 6])

        def norm_batch(e, link, b, Xn, std_asked, std_ready, xn_ready):
            ts = range(TPB * b, TPB * b + TPB)
            tb = slice(TPB * b, TPB * b + TPB)
            for t in ts:
                last = e.bn_stats(stats[:, t, :], X[:, t, :])
            link(last)
            for t in ts:
                last = e.bn_aggr(mv[:, t, :], stats[:, t, :])
            link(last)
            e.tensor_scalar(veps[:, tb], mv[:, tb, 1], LN_EPS, None, ALU.add).then_inc(std_asked, 1)
            e.wait_ge(std_ready, b + 1)
            link(e.reciprocal(rstd[:, tb], rstd[:, tb]))
            for t in ts:
                last = e.tensor_scalar(Xn[:, t, :], X[:, t, :], mv[:, t, 0:1], rstd[:, t:t + 1],
                                       ALU.subtract, ALU.mult)
            last.then_inc(xn_ready, 1)

        with ExitStack() as l0:
            Xn = sb("Xn", [P, NT, D], ctx=l0)
            QT = sb("QT", [P, N], ctx=l0)
            V = sb("V", [P, NT, D], ctx=l0)
            U = sb("U", [P, NT, D], ctx=l0)
            gate = sb("gate", [P, NT, D], ctx=l0)
            scaled = sb("scaled", [P, NT, D], ctx=l0)
            norm0 = sb("norm0", [P, NT], ctx=l0)
            comb0T = sb("comb0T", [R0, N], BF16, ctx=l0)
            sel0_bf = sb("sel0_bf", [R0, C0, P], BF16, ctx=l0)

            with ExitStack() as ph:
                rn = sb("rn", [P, 3], ctx=ph)
                rn2 = sb("rn2", [P, 3], ctx=ph)
                cs = sb("cs", [P, 3], ctx=ph)
                sn = sb("sn", [P, 3], ctx=ph)
                two = sb("two", [P, 1], ctx=ph)
                rt = sb("rt", [P, 3, P], ctx=ph)
                rot = sb("rot", [P, 3, P], ctx=ph)
                Mq = sb("Mq", [P, P], ctx=ph)
                ex = sb("ex", [P, NT * E0], ctx=ph)
                prob = sb("prob", [P, NT, E0 + PAD0], ctx=ph)
                zap = sb("zap", [P, NT, E0 + PAD0], ctx=ph)
                top = sb("top", [P, NT, 8], ctx=ph)
                take = sb("take", [P, NT, 8], ctx=ph)
                tot = sb("tot", [P, NT], ctx=ph)
                cw = sb("cw", [P, NT, E0], ctx=ph)
                cwr = sb("cwr", [P, NT, E0], ctx=ph)
                parts = sb("parts", [P, NT, R0], BF16, ctx=ph)

                x_loaded = [sem(f"x_loaded{b}") for b in range(B)]
                a_loaded, b_loaded = sem("a_loaded"), sem("b_loaded")
                dve_order, act_order = sem("dve_order_a"), sem("act_order_a")
                std_asked, std_ready, xn_ready = sem("std_asked"), sem("std_ready"), sem("xn_ready")
                xt_turned, xt_ready = sem("xt_turned"), sem("xt_ready")
                rot_asked, rot_ready, rot_made = sem("rot_asked"), sem("rot_ready"), sem("rot_made")
                rot_product, mq_ready = sem("rot_product"), sem("mq_ready")
                logits_ready, exp_ready, parts_ready = sem("logits_ready"), sem("exp_ready"), sem("parts_ready")
                v_made, v_ready, q_made, q_ready = sem("v_made"), sem("v_ready"), sem("q_made"), sem("q_ready")
                comb_turned, comb_ready, ident_ready = sem("comb_turned"), sem("comb_ready"), sem("ident_ready")
                block = ph.enter_context(nc.Block())

                @block.sync
                def _(e):
                    for b in range(B):
                        tb = slice(TPB * b, TPB * b + TPB)
                        e.dma_start(X[:, tb, :], x_rows[:, tb, :]).then_inc(x_loaded[b], 16)

                @block.scalar
                def _(e):
                    e.dma_start(A[:, :], a_in).then_inc(a_loaded, 16)
                    e.dma_start(Bw[:, :], b_in).then_inc(b_loaded, 16)
                    for b in range(B):
                        tb = slice(TPB * b, TPB * b + TPB)
                        e.wait_ge(std_asked, b + 1)
                        e.activation(rstd[:, tb], veps[:, tb], ACT.Sqrt).then_inc(std_ready, 1)
                        if b == 0:
                            e.wait_ge(rot_asked, 1)
                            e.activation(rn[:, :], rn2[:, :], ACT.Sqrt).then_inc(rot_ready, 1)
                    for b in range(B):
                        e.wait_ge(xt_turned, b + 1)
                        e.copy(XT[:, S * b:S * b + S], bank[b][:, :]).then_inc(xt_ready, 1)
                    e.wait_ge(logits_ready, 1)
                    e.activation(ex[:, :], bank[4][:, 0:NT * E0], ACT.Exp, scale=-1.0).then_inc(exp_ready, 1)
                    for b in range(B):
                        e.wait_ge(q_made, b + 1)
                        e.copy(QT[:, S * b:S * b + S], bank[b][:, :]).then_inc(q_ready, 1)
                    e.wait_ge(b_loaded, 16)

                @block.vector
                def _(e):
                    link = chain(e, dve_order)
                    e.wait_ge(a_loaded, 16)
                    e.tensor_copy(ident_bf[:, :], a["ident"]).then_inc(ident_ready, 1)
                    e.tensor_copy(sel0_bf[:, :, :], a["sel0"][0:R0, :].rearrange("r (c m) -> r c m", c=C0))
                    link(e.tensor_tensor(cs[:, :], a["rot_c"], a["rot_c"], ALU.mult))
                    link(e.tensor_tensor(sn[:, :], a["rot_s"], a["rot_s"], ALU.mult))
                    e.tensor_tensor(rn2[:, :], cs[:, :], sn[:, :], ALU.add).then_inc(rot_asked, 1)
                    for b in range(B):
                        e.wait_ge(x_loaded[b], 16)
                        norm_batch(e, link, b, Xn, std_asked, std_ready, xn_ready)
                        if b == 0:
                            e.wait_ge(rot_ready, 1)
                            e.reciprocal(two[:, :], a["scale"])
                            link(e.reciprocal(rn[:, :], rn[:, :]))
                            e.tensor_tensor(cs[:, :], a["rot_c"], rn[:, :], ALU.mult)
                            link(e.tensor_tensor(sn[:, :], a["rot_s"], rn[:, :], ALU.mult))
                            for i in range(3):
                                last = e.tensor_scalar(rt[:, i, :], a["turn"], sn[:, i:i + 1], None, ALU.mult)
                            link(last)
                            for i in range(3):
                                last = e.scalar_tensor_tensor(rot[:, i, :], a["ident"], cs[:, i:i + 1], rt[:, i, :],
                                                              ALU.mult, ALU.subtract if i == 2 else ALU.add)
                            last.then_inc(rot_made, 1)
                    e.wait_ge(rot_product, 1)
                    e.tensor_scalar(Mq[:, :], bank[5][:, 0:P], two[:, 0:1], 2.0, ALU.mult, ALU.mult).then_inc(mq_ready, 1)
                    e.wait_ge(exp_ready, 1)
                    link(e.tensor_scalar(ex[:, :], ex[:, :], 1.0, None, ALU.add))
                    for i in range(PAD0):
                        e.memset(prob[:, :, E0 + i:E0 + i + 1], -1.0 - i)
                        e.memset(take[:, :, K0 + i:K0 + i + 1], -1.0 - i)
                    link(e.reciprocal(prob[:, :, 0:E0], ex[:, :].rearrange("p (t e) -> p t e", e=E0)))
                    for t in range(NT):
                        last = e.max(top[:, t, :], prob[:, t, 0:E0])
                    link(last)
                    e.tensor_reduce(tot[:, :], top[:, :, 0:K0], AX.X, ALU.add)
                    link(e.tensor_copy(take[:, :, 0:K0], top[:, :, 0:K0]))
                    for t in range(NT):
                        last = e.match_replace(zap[:, t, :], take[:, t, :], prob[:, t, :], 0.0)
                    link(last)
                    link(e.tensor_scalar(tot[:, :], tot[:, :], 1e-9, None, ALU.max))
                    e.tensor_tensor(cw[:, :, :], prob[:, :, 0:E0], zap[:, :, 0:E0], ALU.subtract)
                    link(e.reciprocal(tot[:, :], tot[:, :]))
                    link(e.tensor_scalar(tot[:, :], tot[:, :], a["route_scale"], None, ALU.mult))
                    link(e.tensor_tensor(cw[:, :, :], cw[:, :, :],
                                         tot[:, :].rearrange("p (t o) -> p t o", o=1).to_broadcast([P, NT, E0]), ALU.mult))
                    pv = parts[:, :, :].rearrange("p t (c h e) -> p t c h e", c=C0, h=3)
                    cv = cw[:, :, :].rearrange("p t (c e) -> p t c e", c=C0)
                    rv = cwr[:, :, :].rearrange("p t (c e) -> p t c e", c=C0)
                    link(e.tensor_copy(pv[:, :, :, 0, :], cv))
                    link(e.tensor_tensor(rv, cv, pv[:, :, :, 0, :], ALU.subtract))
                    link(e.tensor_copy(pv[:, :, :, 1, :], rv))
                    e.tensor_tensor(pv[:, :, :, 2, :], rv, pv[:, :, :, 1, :], ALU.subtract).then_inc(parts_ready, 1)
                    for b in range(B):
                        e.wait_ge(v_made, b + 1)
                        e.tensor_copy(V[:, TPB * b:TPB * b + TPB, :],
                                      bank[4 + b][:, :].rearrange("p (t d) -> p t d", d=D)).then_inc(v_ready, 1)
                    for i in range(2):
                        e.wait_ge(comb_turned, i + 1)
                        e.tensor_copy(comb0T[:, i * (N // 2):(i + 1) * (N // 2)],
                                      bank[i][0:R0, :].bitcast(BF16)).then_inc(comb_ready, 1)

                @block.tensor
                def _(e):
                    e.wait_ge(a_loaded, 16)
                    for b in range(B):
                        e.wait_ge(xn_ready, b + 1)
                        for j in range(TPB):
                            last = e.transpose(bank[b][:, P * j:P * j + P], Xn[:, TPB * b + j, :], a["ident"])
                        last.then_inc(xt_turned, 1)
                        if b == 0:
                            e.wait_ge(rot_made, 1)
                            e.matmul(bank[5][:, 0:P], rot[:, 0, :], rot[:, 1, :], start=True, stop=True).then_inc(rot_product, 1)
                    for t in range(NT):
                        if t % TPB == 0:
                            e.wait_ge(xt_ready, t // TPB + 1)
                        last = e.matmul(bank[4][:, E0 * t:E0 * t + E0], XT[:, P * t:P * t + P], a["expert_sel"],
                                        start=True, stop=True)
                    last.then_inc(logits_ready, 1)
                    e.wait_ge(mq_ready, 1)
                    for b in range(B):
                        e.matmul(bank[b][:, :], Mq[:, :], XT[:, S * b:S * b + S], start=True, stop=True).then_inc(q_made, 1)
                    e.wait_ge(exp_ready, 1)
                    for b in range(B):
                        for j in range(TPB):
                            t = TPB * b + j
                            last = e.matmul(bank[4 + b][:, P * j:P * j + P], XT[:, P * t:P * t + P], rot[:, 2, :],
                                            start=True, stop=True)
                        last.then_inc(v_made, 1)
                    e.wait_ge(parts_ready, 1)
                    e.wait_ge(q_ready, 2)
                    for t in range(NT):
                        half, j = t // (NT // 2), t % (NT // 2)
                        last = e.transpose(bank[half][0:R0, :].bitcast(BF16)[:, P * j:P * j + P], parts[:, t, :],
                                           ident_bf[:, :])
                        if j == NT // 2 - 1:
                            last.then_inc(comb_turned, 1)

            with ExitStack() as ph:
                nmax = sb("nmax", [P, NT], ctx=ph)
                rows = sb("rows", [P, NT], ctx=ph)
                prb = sb("prb", [P, 2, S], ctx=ph)
                prT = sb("prT", [P, 2, S], ctx=ph)
                ss = sb("ss", [P, NT], ctx=ph)
                G0 = sb("G0", [P, 2, C0, S], ctx=ph)
                act0 = sb("act0", [P, 2, S], ctx=ph)
                scores_made, max_ready, probs_ready = sem("scores_made"), sem("max_ready"), sem("probs_ready")
                probs_turned, probsT_ready = sem("probs_turned"), sem("probsT_ready")
                u_made, u_ready = sem("u_made"), sem("u_ready")
                dve_order, act_order = sem("dve_order_b"), sem("act_order_b")
                h_made, b_made, act_ready, g_ready = sem("h0_made"), sem("b0_made"), sem("act0_ready"), sem("g0_ready")
                y_made, gate_ready, norm_asked = sem("y0_made"), sem("gate_ready"), sem("norm_asked")
                block = ph.enter_context(nc.Block())

                @block.tensor
                def _(e):
                    def scores(t):
                        if t >= 2:
                            e.wait_ge(probs_ready, t - 1)
                        b = t // TPB
                        e.matmul(bank[t % 2][:, :], QT[:, P * t:P * t + P], XT[:, S * b:S * b + S],
                                 start=True, stop=True).then_inc(scores_made, 1)

                    def turn(t):
                        e.wait_ge(probs_ready, t + 1)
                        if t >= 2:
                            e.wait_ge(probsT_ready, t - 1)
                        for j in range(TPB):
                            last = e.transpose(bank[2 + t % 2][:, P * j:P * j + P], prb[:, t % 2, P * j:P * j + P],
                                               a["ident"])
                        last.then_inc(probs_turned, 1)

                    def values(t):
                        e.wait_ge(probsT_ready, t + 1)
                        if t >= 2:
                            e.wait_ge(u_ready, t - 1)
                        b = t // TPB
                        for j in range(TPB):
                            last = e.matmul(bank[4 + t % 2][:, 0:D], prT[:, t % 2, P * j:P * j + P],
                                            V[:, TPB * b + j, :], start=(j == 0), stop=(j == TPB - 1))
                        last.then_inc(u_made, 1)

                    scores(0)
                    for t in range(NT + 1):
                        if t + 1 < NT:
                            scores(t + 1)
                        if t < NT:
                            turn(t)
                        if t >= 1:
                            values(t - 1)

                    def hidden(u):
                        g, c = u // C0, u % C0
                        if u >= 2:
                            e.wait_ge(act_ready, u - 1)
                            e.wait_ge(g_ready, u - 1)
                        elif u == 0:
                            e.wait_ge(u_ready, NT)
                        e.matmul(bank[u % 2][:, :], a["keys"][:, P * c:P * c + P], XT[:, S * g:S * g + S],
                                 start=True, stop=True).then_inc(h_made, 1)
                        e.matmul(bank[2 + u % 2][:, :], sel0_bf[:, c, :], comb0T[:, S * g:S * g + S],
                                 start=True, stop=True).then_inc(b_made, 1)

                    def down(g):
                        e.wait_ge(g_ready, C0 * g + C0)
                        for j in range(TPB):
                            for c in range(C0):
                                last = e.matmul(bank[4 + g][:, P * j:P * j + P], G0[:, g % 2, c, P * j:P * j + P],
                                                a["values"][:, P * c:P * c + P], start=(c == 0), stop=(c == C0 - 1))
                        last.then_inc(y_made, 1)

                    for u in range(B * C0):
                        hidden(u)
                        if u % C0 == 1 and u > C0:
                            down(u // C0 - 1)
                    down(B - 1)

                @block.vector
                def _(e):
                    link = chain(e, dve_order)

                    def row_max(t):
                        e.wait_ge(scores_made, t + 1)
                        link(e.tensor_reduce(nmax[:, t:t + 1], bank[t % 2][:, :], AX.X, ALU.max, negate=True))
                        e.tensor_scalar(nmax[:, t:t + 1], nmax[:, t:t + 1], a["bias"], a["bias"],
                                        ALU.subtract, ALU.add).then_inc(max_ready, 1)

                    def copy_turned(t):
                        e.wait_ge(probs_turned, t + 1)
                        if t >= 2:
                            e.wait_ge(u_made, t - 1)
                        e.tensor_copy(prT[:, t % 2, :], bank[2 + t % 2][:, :]).then_inc(probsT_ready, 1)

                    row_max(0)
                    for t in range(NT):
                        if t + 1 < NT:
                            row_max(t + 1)
                        copy_turned(t)
                    for u in range(B * C0):
                        g, c = u // C0, u % C0
                        e.wait_ge(b_made, u + 1)
                        e.wait_ge(act_ready, u + 1)
                        if c == 0 and g >= 2:
                            e.wait_ge(y_made, g - 1)
                        e.tensor_tensor(G0[:, g % 2, c, :], act0[:, u % 2, :], bank[2 + u % 2][:, :],
                                        ALU.mult).then_inc(g_ready, 1)
                    sq = prb[:, 0, :].rearrange("p (t d) -> p t d", d=D)
                    e.wait_ge(u_ready, NT)
                    for b in range(B):
                        tb = slice(TPB * b, TPB * b + TPB)
                        link(e.tensor_tensor(sq, U[:, tb, :], U[:, tb, :], ALU.mult))
                        link(e.tensor_reduce(ss[:, tb], sq, AX.X, ALU.add))
                    link(e.tensor_tensor(rows[:, :], rows[:, :], rows[:, :], ALU.mult))
                    e.scalar_tensor_tensor(norm0[:, :], rows[:, :], 1e-8, ss[:, :], ALU.mult, ALU.max).then_inc(norm_asked, 1)

                @block.scalar
                def _(e):
                    for t in range(NT):
                        e.wait_ge(max_ready, t + 1)
                        if t >= 2:
                            e.wait_ge(probs_turned, t - 1)
                        e.activation(prb[:, t % 2, :], bank[t % 2][:, :], ACT.Exp, bias=nmax[:, t:t + 1],
                                     accum_out=rows[:, t:t + 1]).then_inc(probs_ready, 1)
                        if t >= 1:
                            e.wait_ge(u_made, t)
                            e.copy(U[:, t - 1, :], bank[4 + (t - 1) % 2][:, 0:D]).then_inc(u_ready, 1)
                    e.wait_ge(u_made, NT)
                    e.copy(U[:, NT - 1, :], bank[4 + (NT - 1) % 2][:, 0:D]).then_inc(u_ready, 1)
                    for u in range(B * C0):
                        e.wait_ge(h_made, u + 1)
                        if u >= 2:
                            e.wait_ge(g_ready, u - 1)
                        e.activation(act0[:, u % 2, :], bank[u % 2][:, :], ACT.Relu).then_inc(act_ready, 1)
                    for b in range(B):
                        e.wait_ge(y_made, b + 1)
                        e.activation(gate[:, TPB * b:TPB * b + TPB, :],
                                     bank[4 + b][:, :].rearrange("p (t d) -> p t d", d=D), ACT.Silu).then_inc(gate_ready, 1)


            with ExitStack() as ph:
                norm_ready = sem("norm_ready")
                dve_order, act_order = sem("dve_order_c"), sem("act_order_c")
                std_asked, std_ready, xn_ready = sem("std_asked1"), sem("std_ready1"), sem("xn_ready1")
                xt_turned, xt_ready, xh_ready, xl_ready = sem("xt_turned1"), sem("xt_ready1"), sem("xh_ready"), sem("xl_ready")
                block = ph.enter_context(nc.Block())

                @block.scalar
                def _(e):
                    e.activation(norm0[:, :], norm0[:, :], ACT.Sqrt).then_inc(norm_ready, 1)
                    for b in range(B):
                        tb = slice(TPB * b, TPB * b + TPB)
                        e.wait_ge(std_asked, b + 1)
                        e.activation(rstd[:, tb], veps[:, tb], ACT.Sqrt).then_inc(std_ready, 1)
                    for b in range(B):
                        e.wait_ge(xt_turned, b + 1)
                        e.copy(XT[:, S * b:S * b + S], bank[b][:, :]).then_inc(xt_ready, 1)

                @block.vector
                def _(e):
                    link = chain(e, dve_order)
                    e.wait_ge(norm_ready, 1)
                    link(e.reciprocal(norm0[:, :], norm0[:, :]))
                    for b in range(B):
                        tb = slice(TPB * b, TPB * b + TPB)
                        for t in range(TPB * b, TPB * b + TPB):
                            last = e.scalar_tensor_tensor(scaled[:, t, :], U[:, t, :], norm0[:, t:t + 1], gate[:, t, :],
                                                          ALU.mult, ALU.mult)
                        link(last)
                        link(e.tensor_tensor(X[:, tb, :], X[:, tb, :], scaled[:, tb, :], ALU.add))
                        norm_batch(e, link, b, Xn, std_asked, std_ready, xn_ready)

                @block.tensor
                def _(e):
                    for b in range(B):
                        e.wait_ge(xn_ready, b + 1)
                        for j in range(TPB):
                            last = e.transpose(bank[b][:, P * j:P * j + P], Xn[:, TPB * b + j, :], a["ident"])
                        last.then_inc(xt_turned, 1)

                @block.gpsimd
                def _(e):
                    for b in range(B):
                        s = slice(S * b, S * b + S)
                        e.wait_ge(xt_ready, b + 1)
                        e.tensor_copy(XH[:, s], XT[:, s]).then_inc(xh_ready, 1)
                        e.wait_ge(xh_ready, b + 1)
                        e.tensor_tensor(XL[:, s], XT[:, s], XH[:, s].bitcast(F32), ALU.subtract).then_inc(xl_ready, 1)

        with ExitStack() as l1:
            S1 = sb("S1", [P, NT, D], ctx=l1)

            with ExitStack() as at:
                VA = sb("VA", [P, NT, NH, DV], ctx=at)
                K = sb("K", [P, NT, D], ctx=at)
                og = sb("og", [P, NT, D], ctx=at)
                qT = sb("qT", [P, N], ctx=at)
                kT = sb("kT", [P, N], ctx=at)
                O = sb("O", [P, NT, NH, DV], ctx=at)
                logits = sb("logits", [P, NT, E1], ctx=at)
                floor = sb("floor", [P, TPB, P], ctx=at)
                k_scale = sb("k_scale", [P, TPB, P], ctx=at)
                q_scale = sb("q_scale", [P, TPB - 1, P], ctx=at)
                decay = sb("decay", [P, TPB - 1, P], ctx=at)
                aT = sb("aT", [P, TPB, P], ctx=at)
                prob = sb("prob1", [P, NT, E1], ctx=at)
                dn = sb("dn", [P, NT, NH], ctx=at)
                mu = sb("mu", [P, NT, NH], ctx=at)
                var = sb("var", [P, NT, NH], ctx=at)
                sq = sb("sq", [P, TPB, NH, DH], ctx=at)

                def flat(m, tb):
                    return m[:, tb, :].rearrange("p t h -> p (t h)")

                def spread(m, tb):
                    return m[:, tb, :].rearrange("p t (h o) -> p (t h) o", o=1).to_broadcast([P, TPB * NH, DH])

                def head_sums(e, link, b):
                    tb = slice(TPB * b, TPB * b + TPB)
                    sums = O[:, tb, :, DH:DV].rearrange("p t h o -> p t (h o)")
                    vals = O[:, tb, :, 0:DH].rearrange("p t h d -> p (t h) d")
                    link(e.scalar_tensor_tensor(dn[:, tb, :], sums, -1.0, sums, ALU.mult, ALU.max))
                    link(e.tensor_tensor(dn[:, tb, :], dn[:, tb, :], floor[:, :, 32 * b:32 * b + NH], ALU.max))
                    link(e.tensor_scalar(flat(dn, tb), flat(dn, tb), BACKEND_EPS, None, ALU.add))
                    link(e.reciprocal(flat(dn, tb), flat(dn, tb)))
                    link(e.tensor_tensor(vals, vals, spread(dn, tb), ALU.mult))
                    link(e.tensor_reduce(flat(mu, tb), vals, AX.X, ALU.add))
                    link(e.tensor_scalar(flat(mu, tb), flat(mu, tb), 1 / DH, None, ALU.mult))

                def head_vars(e, link, b, var_ready):
                    tb = slice(TPB * b, TPB * b + TPB)
                    vals = O[:, tb, :, 0:DH].rearrange("p t h d -> p (t h) d")
                    sqv = sq[:, :, :, :].rearrange("p t h d -> p (t h) d")
                    link(e.tensor_tensor(vals, vals, spread(mu, tb), ALU.subtract))
                    link(e.tensor_tensor(sqv, vals, vals, ALU.mult))
                    link(e.tensor_reduce(flat(var, tb), sqv, AX.X, ALU.add))
                    e.tensor_scalar(flat(var, tb), flat(var, tb), 1 / DH, NORM_EPS, ALU.mult, ALU.add).then_inc(var_ready, 1)
                mh = sb("mh", [P, S], F32R, ctx=at)
                ml = sb("ml", [P, S], F32R, ctx=at)
                lane = sb("lane", [P, B, NH, P], F32R, ctx=at)
                masked_bf = sb("masked_bf", [P, TPB, P], BF16, ctx=at)

                with ExitStack() as ph:
                    g = {k: sb(f"g_{k}", [P, S], ctx=ph) for k in
                         ("ti", "tf", "x", "y", "u", "c", "ru", "ln", "lf", "a", "M", "m", "ones")}
                    bias15 = sb("bias15", [P, 2], ctx=ph)
                    Rdiag = sb("Rdiag", [P, TPB, P], ctx=ph)
                    R = sb("R", [P, TPB, P], ctx=ph)
                    proj_made, proj_read_v, proj_read_s = sem("proj_made"), sem("proj_read_v"), sem("proj_read_s")
                    router_made, router_read = sem("router_made"), sem("router_read")
                    qk_made, qk_read = sem("qk_made"), sem("qk_read")
                    gates_made, tanh_ready, bias_ready = sem("gates_made"), sem("tanh_ready"), sem("bias_ready")
                    abs_ready, y_ready, u_ready, ln_ready = sem("abs_ready"), sem("y_ready"), sem("u1_ready"), sem("ln_ready")
                    rows_ready, rows_turned, R_made, R_ready = sem("rows_ready"), sem("rows_turned"), sem("R_made"), sem("R_ready")
                    diff_ready, scales_ready = sem("diff_ready"), sem("scales_ready")
                    dve_order, prob_ready = sem("dve_order_d"), sem("prob_ready")
                    block = ph.enter_context(nc.Block())

                    @block.tensor
                    def _(e):
                        for i, name in enumerate(("wig", "wfg")):
                            for b in range(B):
                                last = e.matmul(bank[6 + i][32 * b:32 * b + 32, :], w[name], XT[:, S * b:S * b + S],
                                                start=True, stop=True)
                        last.then_inc(gates_made, 1)
                        for t in range(NT):
                            if t >= 2:
                                e.wait_ge(proj_read_v, t - 1)
                                e.wait_ge(proj_read_s, t - 1)
                                e.wait_ge(router_read, t - 1)
                            xt = XT[:, P * t:P * t + P]
                            wall = Bw[:, B_AT["wv"].start:B_AT["wk"].stop]
                            e.matmul(bank[t % 2][:, 0:3 * D], xt, wall, start=True, stop=True).then_inc(proj_made, 1)
                            e.matmul(bank[2 + t % 2][:, 0:E1], xt, w["router"], start=True, stop=True).then_inc(router_made, 1)
                            if t % 2 == 1:
                                i = t // 2
                                if i >= 2:
                                    e.wait_ge(qk_read, i - 1)
                                e.matmul(bank[4 + i % 2][:, :], w["wq" if i % 2 == 0 else "wk"],
                                         XT[:, S * (i // 2):S * (i // 2) + S], start=True, stop=True).then_inc(qk_made, 1)
                        e.wait_ge(rows_ready, 3)
                        e.wait_ge(proj_read_v, NT)
                        e.wait_ge(proj_read_s, NT)
                        e.wait_ge(router_read, NT)
                        for i, name in enumerate(("a", "M", "m")):
                            for j in range(TPB):
                                last = e.transpose(bank[i][:, P * j:P * j + P], g[name][:, P * j:P * j + P], a["ident"])
                        last.then_inc(rows_turned, 1)
                        e.wait_ge(R_made, 1)
                        for j in range(TPB):
                            last = e.matmul(bank[3][:, P * j:P * j + P], a["ones"], Rdiag[:, j, :], start=True, stop=True)
                        last.then_inc(rows_turned, 1)

                    @block.scalar
                    def _(e):
                        e.wait_ge(gates_made, 1)
                        e.wait_ge(bias_ready, 1)
                        e.activation(g["tf"][:, :], bank[7][:, :], ACT.Tanh, bias=bias15[:, 1:2], scale=1 / CAP).then_inc(tanh_ready, 1)
                        e.activation(g["ti"][:, :], bank[6][:, :], ACT.Tanh, bias=bias15[:, 0:1], scale=1 / CAP).then_inc(tanh_ready, 1)
                        for t in range(NT):
                            if t and t % TPB == 0:
                                tb = slice(t - TPB, t)
                                e.wait_ge(router_read, t)
                                e.activation(prob[:, tb, :], logits[:, tb, :], ACT.Sigmoid)
                            e.wait_ge(proj_made, t + 1)
                            e.wait_ge(proj_read_v, t + 1)
                            e.activation(og[:, t, :], bank[t % 2][:, D:2 * D], ACT.Sigmoid)
                            e.copy(K[:, t, :], bank[t % 2][:, 2 * D:3 * D]).then_inc(proj_read_s, 1)
                            if t % 2 == 1:
                                i = t // 2
                                e.wait_ge(qk_made, i + 1)
                                dst = (qT, kT)[i % 2][:, S * (i // 2):S * (i // 2) + S]
                                if i % 2 == 0:
                                    e.mul(dst, bank[4][:, :], DH ** -0.5).then_inc(qk_read, 1)
                                else:
                                    e.copy(dst, bank[5][:, :]).then_inc(qk_read, 1)
                        e.wait_ge(router_read, NT)
                        e.activation(prob[:, NT - TPB:NT, :], logits[:, NT - TPB:NT, :], ACT.Sigmoid).then_inc(prob_ready, 1)
                        e.wait_ge(abs_ready, 1)
                        e.activation(g["y"][:, :], g["y"][:, :], ACT.Exp, scale=-1.0).then_inc(y_ready, 1)
                        e.wait_ge(prob_ready, 1)
                        for b in range(B):
                            tb = slice(TPB * b, TPB * b + TPB)
                            e.activation(logits[:, tb, :], logits[:, tb, :], ACT.Exp, scale=-1.0)
                        e.wait_ge(u_ready, 1)
                        e.activation(g["ln"][:, :], g["u"][:, :], ACT.Ln).then_inc(ln_ready, 1)
                        e.wait_ge(rows_turned, 1)
                        e.activation(floor[:, :, :], bank[2][:, :].rearrange("p (j r) -> p j r", r=P), ACT.Exp, scale=-1.0)
                        e.wait_ge(rows_turned, 2)
                        e.copy(R[:, :, :], bank[3][:, :].rearrange("p (j r) -> p j r", r=P)).then_inc(R_ready, 1)
                        e.wait_ge(diff_ready, 3)
                        e.activation(k_scale[:, :, :], k_scale[:, :, :], ACT.Exp)
                        e.activation(q_scale[:, :, :], q_scale[:, :, :], ACT.Exp)
                        e.activation(decay[:, :, :], decay[:, :, :], ACT.Exp)

                    @block.vector
                    def _(e):
                        link = chain(e, dve_order)
                        e.tensor_scalar(bias15[:, :], Bw[:, B_AT["big"].start:B_AT["bfg"].stop], 1 / CAP, None,
                                        ALU.mult).then_inc(bias_ready, 1)
                        e.memset(VA[:, :, :, DH:DV], 1.0)
                        e.memset(g["ones"][:, :], 1.0)
                        e.tensor_copy(masked_bf[:, :, :],
                                      w["masked"].rearrange("p (o m) -> p o m", o=1).to_broadcast([P, TPB, P]))
                        e.wait_ge(tanh_ready, 2)
                        link(e.tensor_scalar(g["x"][:, :], g["tf"][:, :], CAP, None, ALU.mult))
                        e.scalar_tensor_tensor(g["y"][:, :], g["x"][:, :], -1.0, g["x"][:, :], ALU.mult, ALU.max).then_inc(abs_ready, 1)
                        e.tensor_scalar(g["ti"][:, :], g["ti"][:, :], CAP, None, ALU.mult)

                        def evacuate(t):
                            e.wait_ge(proj_made, t + 1)
                            e.tensor_copy(VA[:, t, :, 0:DH],
                                          bank[t % 2][:, 0:D].rearrange("p (h v) -> p h v", h=NH)).then_inc(proj_read_v, 1)
                            e.wait_ge(router_made, t + 1)
                            e.tensor_tensor(logits[:, t, :], bank[2 + t % 2][:, 0:E1], w["expert_bias"],
                                            ALU.add).then_inc(router_read, 1)
                        for t in range(2):
                            evacuate(t)
                        for t in range(2, NT):
                            evacuate(t)
                        e.wait_ge(y_ready, 1)
                        e.tensor_scalar(g["u"][:, :], g["y"][:, :], 1.0, None, ALU.add).then_inc(u_ready, 1)
                        e.wait_ge(u_ready, 1)
                        link(e.scalar_tensor_tensor(g["c"][:, :], g["u"][:, :], 1.0, g["y"][:, :], ALU.subtract, ALU.subtract))
                        link(e.reciprocal(g["ru"][:, :], g["u"][:, :]))
                        link(e.tensor_tensor(g["c"][:, :], g["c"][:, :], g["ru"][:, :], ALU.mult))
                        link(e.scalar_tensor_tensor(g["x"][:, :], g["x"][:, :], 0.0, g["c"][:, :], ALU.min, ALU.add))
                        e.wait_ge(ln_ready, 1)
                        link(e.tensor_tensor(g["x"][:, :], g["x"][:, :], g["ln"][:, :], ALU.subtract))
                        link(e.tensor_tensor_scan(g["lf"][:, :], g["ones"][:, :], g["x"][:, :], 0.0, ALU.mult, ALU.add))
                        e.tensor_tensor(g["a"][:, :], g["ti"][:, :], g["lf"][:, :], ALU.subtract).then_inc(rows_ready, 1)
                        e.wait_ge(rows_ready, 1)
                        e.tensor_tensor_scan(g["M"][:, :], g["a"][:, :], g["a"][:, :], -3e38, ALU.max, ALU.max).then_inc(rows_ready, 1)
                        e.wait_ge(rows_ready, 2)
                        e.tensor_tensor(g["m"][:, :], g["lf"][:, :], g["M"][:, :], ALU.add).then_inc(rows_ready, 1)
                        for j in range(TPB):
                            last = e.tensor_scalar(Rdiag[:, j, :], a["ident"], g["M"][:, P * j + P - 1:P * j + P], None, ALU.mult)
                        last.then_inc(R_made, 1)
                        link(e.tensor_scalar(mh[:, :], g["M"][:, :], -1.0, None, ALU.mult))
                        e.scalar_tensor_tensor(ml[:, :], g["M"][:, :], -1.0, mh[:, :].bitcast(F32), ALU.mult, ALU.subtract)
                        e.tensor_copy(lane[:, :, :, :],
                                      a["ident"].rearrange("p (b r) -> p b r", b=B)[:, :, 0:NH]
                                      .rearrange("p b (h o) -> p b h o", o=1).to_broadcast([P, B, NH, P]))
                        e.wait_ge(R_ready, 1)
                        e.tensor_copy(aT[:, :, :], bank[0][:, :].rearrange("p (j r) -> p j r", r=P))
                        e.tensor_tensor(k_scale[:, :, :], bank[0][:, :].rearrange("p (j r) -> p j r", r=P), R[:, :, :],
                                        ALU.subtract).then_inc(diff_ready, 1)
                        e.tensor_tensor(q_scale[:, :, :], R[:, 0:TPB - 1, :],
                                        bank[1][:, P:S].rearrange("p (j r) -> p j r", r=P), ALU.subtract).then_inc(diff_ready, 1)
                        e.tensor_tensor(decay[:, :, :], R[:, 0:TPB - 1, :], R[:, 1:TPB, :], ALU.subtract).then_inc(diff_ready, 1)

                with ExitStack() as ph:
                    Dm = sb("Dm", [P, 2, S], ctx=ph)
                    CT = sb("CT", [P, 2, NH, S], ctx=ph)
                    KS = sb("KS", [P, 2, NH, DH], ctx=ph)
                    St = sb("St", [P, 2, NH, DV], ctx=ph)
                    inc = sb("inc", [P, NH, DV], ctx=ph)
                    part = sb("part", [P, NH, DV], ctx=ph)
                    top = sb("top1", [P, TPB, K1], ctx=ph)
                    tot = sb("tot1", [P, TPB], ctx=ph)
                    zap = sb("zap1", [P, TPB, E1], ctx=ph)
                    cw_ready = sem("cw_ready")
                    d_made, d_ready, st_made, c_ready = sem("d_made"), sem("d_ready"), sem("st_made"), sem("c_ready")
                    ks_ready, kv_made, state_ready = sem("ks_ready"), sem("kv_made"), sem("state_ready")
                    inter_made, inter_read, intra_made, o_ready = sem("inter_made"), sem("inter_read"), sem("intra_made"), sem("o_ready")
                    dve_order, var_ready = sem("dve_order_e"), sem("var_ready")
                    block = ph.enter_context(nc.Block())
                    wide = NH * DV

                    @block.tensor
                    def _(e):
                        def unit(v):
                            b, h = v // NH, v % NH
                            if v >= 2:
                                e.wait_ge(d_ready, v - 1)
                                e.wait_ge(c_ready, v - 1)
                            dm, st = bank[v % 2], bank[2 + v % 2]
                            e.matmul(dm[:, :], lane[:, b, h, :], mh[:, :], start=True, stop=False)
                            e.matmul(dm[:, :], lane[:, b, h, :], ml[:, :], start=False, stop=False)
                            e.matmul(dm[:, :], ident_bf[:, :], masked_bf[:, :, :], start=False, stop=True).then_inc(d_made, 1)
                            for j in range(TPB):
                                ts = slice(S * b + P * j, S * b + P * j + P)
                                hs = slice(DH * h, DH * h + DH)
                                last = e.matmul(st[:, P * j:P * j + P], kT[hs, ts], qT[hs, ts], start=True, stop=True)
                            last.then_inc(st_made, 1)

                        def tile(t):
                            b, j = t // TPB, t % TPB
                            n = (TPB - 1) * b + j
                            e.wait_ge(c_ready, NH * b + NH)
                            if t >= 2:
                                e.wait_ge(o_ready, t - 1)
                            for h in range(NH):
                                last = e.matmul(bank[4 + t % 2][:, DV * h:DV * h + DV], CT[:, b % 2, h, P * j:P * j + P],
                                                VA[:, t, h, :], start=True, stop=True)
                            last.then_inc(intra_made, 1)
                            if j < TPB - 1:
                                e.wait_ge(ks_ready, n + 1)
                                if n:
                                    e.wait_ge(state_ready, n)
                                e.matmul(bank[7][:, 0:wide], KS[:, n % 2, :, :], VA[:, t, :, :],
                                         start=True, stop=True).then_inc(kv_made, 1)
                            if j:
                                e.wait_ge(state_ready, n)
                                if n > 1:
                                    e.wait_ge(inter_read, n - 1)
                                e.matmul(bank[6][:, 0:wide], qT[:, P * t:P * t + P], St[:, (j - 1) % 2, :, :],
                                         start=True, stop=True).then_inc(inter_made, 1)

                        for v in range(NH):
                            unit(v)
                        for t in range(NT):
                            if t + NH < B * NH:
                                unit(t + NH)
                            tile(t)

                    @block.scalar
                    def _(e):
                        for v in range(B * NH):
                            e.wait_ge(d_made, v + 1)
                            if v >= 2:
                                e.wait_ge(c_ready, v - 1)
                            b, h = v // NH, v % NH
                            for j in range(TPB):
                                js = slice(P * j, P * j + P)
                                last = e.activation(Dm[:, v % 2, js], bank[v % 2][:, js], ACT.Exp,
                                                    bias=aT[:, j, 32 * b + h:32 * b + h + 1])
                            last.then_inc(d_ready, 1)

                    @block.vector
                    def _(e):
                        link = chain(e, dve_order)

                        def per_head(m, b, n):
                            return m[:, 32 * b:32 * b + NH].rearrange("p (h o) -> p h o", o=1).to_broadcast([P, NH, n])

                        def product(v):
                            b, h = v // NH, v % NH
                            e.wait_ge(d_ready, v + 1)
                            e.wait_ge(st_made, v + 1)
                            if b >= 2:
                                e.wait_ge(intra_made, NH * (b - 1))
                            e.tensor_tensor(CT[:, b % 2, h, :], Dm[:, v % 2, :], bank[2 + v % 2][:, :], ALU.mult).then_inc(c_ready, 1)

                        def tile(t):
                            b, j = t // TPB, t % TPB
                            n = (TPB - 1) * b + j
                            if j < TPB - 1:
                                if n >= 2:
                                    e.wait_ge(kv_made, n - 1)
                                e.tensor_tensor(KS[:, n % 2, :, :], K[:, t, :].rearrange("p (h d) -> p h d", h=NH),
                                                per_head(k_scale[:, j, :], b, DH), ALU.mult).then_inc(ks_ready, 1)
                            po = bank[4 + t % 2][:, 0:wide].rearrange("p (h d) -> p h d", h=NH)
                            pi = bank[6][:, 0:wide].rearrange("p (h d) -> p h d", h=NH)
                            if j:
                                e.wait_ge(inter_made, n)
                                e.tensor_tensor(part[:, :, :], pi, per_head(q_scale[:, j - 1, :], b, DV), ALU.mult).then_inc(inter_read, 1)
                                e.wait_ge(inter_read, n)
                                e.wait_ge(intra_made, t + 1)
                                e.tensor_tensor(O[:, t, :, :], part[:, :, :], po, ALU.add).then_inc(o_ready, 1)
                            else:
                                e.wait_ge(intra_made, t + 1)
                                e.tensor_copy(O[:, t, :, :], po).then_inc(o_ready, 1)
                            if j < TPB - 1:
                                e.wait_ge(kv_made, n + 1)
                                kv = bank[7][:, 0:wide].rearrange("p (h d) -> p h d", h=NH)
                                blocks = w["diag"].rearrange("p (h d) -> p h d", h=NH)
                                if j == 0:
                                    e.tensor_tensor(St[:, 0, :, :], kv, blocks, ALU.mult).then_inc(state_ready, 1)
                                    e.wait_ge(state_ready, n + 1)
                                else:
                                    e.tensor_tensor(inc[:, :, :], kv, blocks, ALU.mult)
                                    link(e.tensor_tensor(St[:, j % 2, :, :], St[:, (j - 1) % 2, :, :],
                                                         per_head(decay[:, j - 1, :], b, DV), ALU.mult))
                                    e.tensor_tensor(St[:, j % 2, :, :], St[:, j % 2, :, :], inc[:, :, :], ALU.add).then_inc(state_ready, 1)
                                    e.wait_ge(state_ready, n + 1)

                        def route(b, step):
                            tb = slice(TPB * b, TPB * b + TPB)
                            if step == 0:
                                link(e.tensor_scalar(logits[:, tb, :], logits[:, tb, :], -1.0, -1.0, ALU.mult, ALU.add))
                                for j in range(TPB):
                                    last = e.max(top[:, j, :], logits[:, TPB * b + j, :])
                                link(last)
                            elif step == 1:
                                for j in range(TPB):
                                    last = e.match_replace(zap[:, j, :], top[:, j, :], logits[:, TPB * b + j, :], 1.0)
                                link(last)
                                link(e.scalar_tensor_tensor(prob[:, tb, :], zap[:, :, :], 0.0, prob[:, tb, :],
                                                            ALU.is_gt, ALU.mult))
                            elif step == 2:
                                link(e.tensor_reduce(tot[:, :], prob[:, tb, :], AX.X, ALU.add))
                                link(e.tensor_scalar(tot[:, :], tot[:, :], 1e-9, None, ALU.add))
                                link(e.reciprocal(tot[:, :], tot[:, :]))
                                link(e.tensor_scalar(tot[:, :], tot[:, :], ROUTED_SCALE, None, ALU.mult))
                                e.tensor_tensor(prob[:, tb, :], prob[:, tb, :],
                                                tot[:, :].rearrange("p (t o) -> p t o", o=1).to_broadcast([P, TPB, E1]),
                                                ALU.mult).then_inc(cw_ready, 1)

                        for v in range(NH):
                            product(v)
                        for t in range(NT):
                            b, j = t // TPB, t % TPB
                            if t + NH < B * NH:
                                product(t + NH)
                            tile(t)
                            route(b, j)
                            if b and j == 1:
                                head_sums(e, link, b - 1)
                            if b and j == 3:
                                head_vars(e, link, b - 1, var_ready)
                        head_sums(e, link, B - 1)
                        head_vars(e, link, B - 1, var_ready)

                    @block.gpsimd
                    def _(e):
                        e.tensor_tensor(og[:, :, :], og[:, :, :], w["norm_w"].rearrange("p (o d) -> p o d", o=1)
                                        .to_broadcast([P, NT, D]), ALU.mult)

                with ExitStack() as ph:
                    combT = sb("combT", [TB, 2, NB, S], ctx=ph)
                    ho = sb("ho", [P, NT, D], ctx=ph)
                    HT = sb("HT", [P, 2, S], ctx=ph)
                    std_ready = sem("head_std_ready")
                    comb_turned, comb_copied = sem("comb1_turned"), sem("comb1_copied")
                    comb_stored = [sem(f"comb_stored{i}") for i in range(2)]
                    ho_ready, ho_turned, ht_ready, s_made = sem("ho_ready"), sem("ho_turned"), sem("ht_ready"), sem("s1_made")
                    dve_order, s_read = sem("dve_order_f"), sem("s_read")
                    block = ph.enter_context(nc.Block())

                    @block.sync
                    def _(e):
                        rows = comb_dram.rearrange("(k r) n -> r k n", r=TB)
                        for b in range(B):
                            e.wait_ge(comb_copied, b + 1)
                            e.dma_start(rows[:, :, S * b:S * b + S], combT[:, b % 2, :, :]).then_inc(comb_stored[b % 2], 16)
                        for i in range(2):
                            e.wait_ge(comb_stored[i], 16 * (B // 2))

                    @block.scalar
                    def _(e):
                        e.activation(var[:, :, :], var[:, :, :], ACT.Sqrt).then_inc(std_ready, 1)
                        for b in range(B):
                            e.wait_ge(comb_turned, b + 1)
                            if b >= 2:
                                e.wait_ge(comb_stored[b % 2], 16)
                            for k in range(NB):
                                last = e.copy(combT[:, b % 2, k, :], bank[NB * (b % 2) + k][0:TB, :])
                            last.then_inc(comb_copied, 1)
                            e.wait_ge(ho_turned, b + 1)
                            e.copy(HT[:, b % 2, :], bank[4 + b % 2][:, :]).then_inc(ht_ready, 1)

                    @block.vector
                    def _(e):
                        link = chain(e, dve_order)
                        e.wait_ge(std_ready, 1)
                        link(e.reciprocal(var[:, :, :], var[:, :, :]))
                        for b in range(B):
                            tb = slice(TPB * b, TPB * b + TPB)
                            vals = O[:, tb, :, 0:DH].rearrange("p t h d -> p (t h) d")
                            hv = ho[:, tb, :].rearrange("p t (h d) -> p (t h) d", h=NH)
                            link(e.tensor_tensor(hv, vals, spread(var, tb), ALU.mult))
                            e.tensor_tensor(ho[:, tb, :], ho[:, tb, :], og[:, tb, :], ALU.mult).then_inc(ho_ready, 1)
                        for b in range(B):
                            e.wait_ge(s_made, b + 1)
                            e.tensor_copy(S1[:, TPB * b:TPB * b + TPB, :],
                                          bank[6 + b % 2][:, :].rearrange("p (t d) -> p t d", d=D)).then_inc(s_read, 1)

                    @block.tensor
                    def _(e):
                        for b in range(B):
                            if b >= 2:
                                e.wait_ge(comb_copied, b - 1)
                            for k in range(NB):
                                for j in range(TPB):
                                    last = e.transpose(bank[NB * (b % 2) + k][0:TB, P * j:P * j + P],
                                                       prob[:, TPB * b + j, TB * k:TB * k + TB], a["ident"])
                            last.then_inc(comb_turned, 1)
                            e.wait_ge(ho_ready, b + 1)
                            for j in range(TPB):
                                last = e.transpose(bank[4 + b % 2][:, P * j:P * j + P], ho[:, TPB * b + j, :], a["ident"])
                            last.then_inc(ho_turned, 1)
                            e.wait_ge(ht_ready, b + 1)
                            if b >= 2:
                                e.wait_ge(s_read, b - 1)
                            for j in range(TPB):
                                last = e.matmul(bank[6 + b % 2][:, P * j:P * j + P], HT[:, b % 2, P * j:P * j + P], w["wdown"],
                                                start=True, stop=True)
                            last.then_inc(s_made, 1)

            with ExitStack() as ph:
                G = N // S
                PAIR = 2 * G
                TURNS = C1 // 2
                LAG = 6
                LEAD = 2
                zeros = sb("zeros", [P, P], ctx=ph)
                RING = PAIR
                staged = sb("staged", [P, 2, 2 * P], ctx=ph)
                gate_hi = sb("gate_hi", [P, 2, P], F32R, ctx=ph)
                gate_lo = sb("gate_lo", [P, 2, P], F32R, ctx=ph)
                down_hi = sb("down_hi", [P, 2, P], F32R, ctx=ph)
                down_lo = sb("down_lo", [P, 2, P], F32R, ctx=ph)
                comb = sb("comb", [P, 2, N], ctx=ph)
                act = sb("act", [P, 4, S], ctx=ph)
                hid = sb("hid", [P, RING, S], ctx=ph)
                hid_hi = sb("hid_hi", [P, RING, S], F32R, ctx=ph)
                hid_lo = sb("hid_lo", [P, RING, S], F32R, ctx=ph)
                shared = sb("shared", [H1, 2, S], ctx=ph)
                yT = sb("yT", [P, N], ctx=ph)
                res = sb("res", [P, NT, D], ctx=ph)
                staged_in = [sem(f"staged_in{i}") for i in range(2)]
                HALVES, GPH = 2, G // 2
                comb_in = [[sem(f"comb_in{i}_{h}") for h in range(HALVES)] for i in range(2)]
                gate_hi_ready, gate_ready = sem("gate_hi_ready"), sem("gate_parts_ready")
                down_hi_ready, down_ready = sem("down_hi_ready"), sem("down_parts_ready")
                zeros_ready, sh_made, sh_ready = sem("zeros_ready"), sem("sh_made"), sem("sh_ready")
                up_made, act_ready = sem("up_made"), sem("act1_ready")
                hid_ready, hi_ready, lo_ready, y_made = sem("hid_ready"), sem("hi_ready"), sem("lo_ready"), sem("y1_made")
                yt_ready, y_turned, res_ready, x_ready = sem("yt_ready"), sem("y_turned"), sem("res_ready"), sem("x_ready")
                stored = [sem(f"stored{b}") for b in range(B)]
                block = ph.enter_context(nc.Block())

                @block.sync
                def _(e):
                    def load(s, c):
                        e.dma_start(staged[:, s, :], w_in[c, :, :].rearrange("o p n -> (o p) n")).then_inc(staged_in[s], 16)

                    def load_comb(s, h, first):
                        cols = slice(S * GPH * h, S * GPH * (h + 1))
                        for x in range(EPC1):
                            e.dma_start(comb[H1 * x:H1 * x + H1, s, cols],
                                        comb_dram[bass.ds(first + x, 1), cols].to_broadcast([H1, S * GPH])
                                        ).then_inc(comb_in[s][h], 16)

                    for s in range(2):
                        load(s, slice(s, s + 1))
                        for h in range(HALVES):
                            load_comb(s, h, EPC1 * s)
                    with e.Fori(1, TURNS) as i:
                        for s in range(2):
                            e.wait_ge(down_ready, i * 2 + (s - 1))
                            load(s, bass.ds(i * 2 + s, 1))
                            for h in range(HALVES):
                                e.wait_ge(hid_ready, i * PAIR + (G * s - PAIR + GPH * (h + 1)))
                                load_comb(s, h, i * (2 * EPC1) + EPC1 * s)
                    for b in range(B):
                        tb = slice(TPB * b, TPB * b + TPB)
                        e.wait_ge(x_ready, b + 1)
                        e.dma_start(out_rows[:, tb, :], X[:, tb, :]).then_inc(stored[b], 16)
                    for b in range(B):
                        e.wait_ge(stored[b], 16)

                @block.gpsimd
                def _(e):
                    def split(i, s):
                        c = i * 2 + s
                        e.wait_ge(staged_in[s], i * 16 + 16)
                        if not (isinstance(i, int) and i == 0):
                            e.wait_ge(up_made, i * PAIR + (G * s - G))
                        e.tensor_tensor(gate_hi[:, s, :], staged[:, s, 0:P], zeros[:, :], ALU.subtract).then_inc(gate_hi_ready, 1)
                        e.wait_ge(gate_hi_ready, c + 1)
                        e.tensor_tensor(gate_lo[:, s, :], staged[:, s, 0:P], gate_hi[:, s, :].bitcast(F32),
                                        ALU.subtract).then_inc(gate_ready, 1)
                        if not (isinstance(i, int) and i == 0):
                            e.wait_ge(y_made, i * PAIR + (G * s - G))
                        e.tensor_tensor(down_hi[:, s, :], staged[:, s, P:2 * P], zeros[:, :], ALU.subtract).then_inc(down_hi_ready, 1)
                        e.wait_ge(down_hi_ready, c + 1)
                        e.tensor_tensor(down_lo[:, s, :], staged[:, s, P:2 * P], down_hi[:, s, :].bitcast(F32),
                                        ALU.subtract).then_inc(down_ready, 1)

                    e.memset(zeros[:, :], 0.0).then_inc(zeros_ready, 1)
                    e.wait_ge(zeros_ready, 1)
                    for s in range(2):
                        split(0, s)
                    with e.Fori(1, TURNS) as i:
                        for s in range(2):
                            split(i, s)

                @block.tensor
                def _(e):
                    for g in range(G):
                        if g >= 2:
                            e.wait_ge(sh_ready, g - 1)
                        e.matmul(bank[g % 2][0:H1, :], w["shared_gate"], XT[:, S * g:S * g + S],
                                 start=True, stop=True).then_inc(sh_made, 1)
                        if g:
                            e.wait_ge(sh_ready, g)
                            e.matmul(bank[3 + g][:, :], w["shared_down"][0:H1, :], shared[:, (g - 1) % 2, :],
                                     start=True, stop=False)
                    e.wait_ge(sh_ready, G)
                    e.matmul(bank[3 + G][:, :], w["shared_down"][0:H1, :], shared[:, (G - 1) % 2, :], start=True, stop=False)

                    def up(i, j):
                        s, g = (j // G) % 2, j % G
                        if g == 0:
                            e.wait_ge(gate_ready, i * 2 + (j // G + 1))
                        if not (isinstance(i, int) and i == 0 and j < 4):
                            e.wait_ge(act_ready, i * PAIR + (j - 3))
                        xs = slice(S * g, S * g + S)
                        e.matmul(bank[j % 4][:, :], gate_hi[:, s, :], XH[:, xs], start=True, stop=False)
                        e.matmul(bank[j % 4][:, :], gate_hi[:, s, :], XL[:, xs], start=False, stop=False)
                        e.matmul(bank[j % 4][:, :], gate_lo[:, s, :], XH[:, xs], start=False, stop=True).then_inc(up_made, 1)

                    def down(i, j, last=False):
                        s, g = (j // G) % 2, j % G
                        if g == 0:
                            e.wait_ge(down_ready, i * 2 + (j // G + 1))
                        e.wait_ge(lo_ready, i * PAIR + (j + 1))
                        y = bank[4 + g][:, :]
                        e.matmul(y, down_hi[:, s, :], hid_hi[:, j % RING, :], start=False, stop=False)
                        e.matmul(y, down_hi[:, s, :], hid_lo[:, j % RING, :], start=False, stop=False)
                        e.matmul(y, down_lo[:, s, :], hid_hi[:, j % RING, :], start=False, stop=last).then_inc(y_made, 1)

                    for j in range(LAG):
                        up(0, j)
                    with e.Fori(0, TURNS - 1) as i:
                        for j in range(PAIR):
                            down(i, j)
                            up(i, j + LAG)
                    for j in range(PAIR):
                        down(TURNS - 1, j, last=(j >= G))
                        if j + LAG < PAIR:
                            up(TURNS - 1, j + LAG)
                    for b in range(B):
                        e.wait_ge(yt_ready, b + 1)
                        for j in range(TPB):
                            last = e.transpose(bank[b][:, P * j:P * j + P], yT[:, S * b + P * j:S * b + P * j + P], a["ident"])
                        last.then_inc(y_turned, 1)

                @block.scalar
                def _(e):
                    for g in range(G):
                        e.wait_ge(sh_made, g + 1)
                        e.activation(shared[:, g % 2, :], bank[g % 2][0:H1, :], ACT.Silu).then_inc(sh_ready, 1)

                    def silu(i, j):
                        e.wait_ge(up_made, i * PAIR + (j + 1))
                        if not (isinstance(i, int) and i == 0 and j < 2):
                            e.wait_ge(hid_ready, i * PAIR + (j - 1))
                        e.activation(act[:, j % 4, :], bank[j % 4][:, :], ACT.Silu).then_inc(act_ready, 1)

                    def high(i, j):
                        e.wait_ge(hid_ready, i * PAIR + (j + 1))
                        e.copy(hid_hi[:, j % RING, :], hid[:, j % RING, :]).then_inc(hi_ready, 1)

                    for j in range(LEAD):
                        silu(0, j)
                    with e.Fori(0, TURNS - 1) as i:
                        for j in range(PAIR):
                            silu(i, j + LEAD)
                            high(i, j)
                    for j in range(PAIR):
                        if j + LEAD < PAIR:
                            silu(TURNS - 1, j + LEAD)
                        high(TURNS - 1, j)
                    for b in range(B):
                        e.wait_ge(y_made, C1 * G - (B - 1) + b)
                        e.activation(yT[:, S * b:S * b + S], bank[4 + b][:, :], ACT.Silu).then_inc(yt_ready, 1)

                @block.vector
                def _(e):
                    def weigh(i, j):
                        e.wait_ge(act_ready, i * PAIR + (j + 1))
                        s, g = (j // G) % 2, j % G
                        if g % GPH == 0:
                            e.wait_ge(comb_in[s][g // GPH], (i + j // PAIR) * (16 * EPC1) + 16 * EPC1)
                        e.tensor_tensor(hid[:, j % RING, :], act[:, j % 4, :], comb[:, s, S * g:S * g + S], ALU.mult).then_inc(hid_ready, 1)

                    def low(i, j):
                        e.wait_ge(hi_ready, i * PAIR + (j + 1))
                        e.tensor_tensor(hid_lo[:, j % RING, :], hid[:, j % RING, :], hid_hi[:, j % RING, :].bitcast(F32),
                                        ALU.subtract).then_inc(lo_ready, 1)

                    for j in range(LEAD):
                        weigh(0, j)
                    with e.Fori(0, TURNS - 1) as i:
                        for j in range(PAIR):
                            weigh(i, j + LEAD)
                            low(i, j)
                    for j in range(PAIR):
                        if j + LEAD < PAIR:
                            weigh(TURNS - 1, j + LEAD)
                        low(TURNS - 1, j)
                    for b in range(B):
                        tb = slice(TPB * b, TPB * b + TPB)
                        e.wait_ge(y_turned, b + 1)
                        e.tensor_tensor(res[:, tb, :], S1[:, tb, :], bank[b][:, :].rearrange("p (t d) -> p t d", d=D),
                                        ALU.mult).then_inc(res_ready, 1)
                        e.wait_ge(res_ready, b + 1)
                        e.tensor_tensor(X[:, tb, :], X[:, tb, :], res[:, tb, :], ALU.add).then_inc(x_ready, 1)


def kernel(**inputs):
    import numpy as np
    import concourse.bacc as bacc
    from concourse.bass_utils import run_bass_kernel_spmd

    i = {k: np.asarray(v) for k, v in inputs.items()}
    f = np.float32

    def rows(v):
        return np.tile(np.reshape(v, (1, -1)), (P, 1))

    def down(m, n=P):
        out = np.zeros((n,) + m.shape[1:], f)
        out[:m.shape[0]] = m
        return out

    turn = np.zeros((P, P), f)
    for k in range(0, P, 2):
        turn[k, k + 1], turn[k + 1, k] = -1, 1
    sel0 = np.zeros((P, C0, P), f)
    for r in range(R0):
        c, e = r // (3 * EPC0), r % EPC0
        sel0[r, c, H0 * e:H0 * e + H0] = 1
    masked = np.where(np.arange(P)[:, None] > np.arange(P)[None, :], MASKED, 0).astype(f)
    diag = np.zeros((P, NH, DV), f)
    for h in range(NH):
        diag[DH * h:DH * h + DH, h] = 1

    a = dict(ident=np.eye(P, dtype=f), turn=turn, ones=np.ones((P, P), f), sel0=sel0,
             expert_sel=i["L0_ffn_expert_sel"].T, keys=i["L0_ffn_keys"].transpose(1, 0, 2),
             values=i["L0_ffn_values"].reshape(C0, P, D).transpose(1, 0, 2),
             rot_c=np.repeat(i["L0_attn_rot_w"][:, 0::2], 2, axis=1).T,
             rot_s=np.repeat(i["L0_attn_rot_w"][:, 1::2], 2, axis=1).T,
             scale=rows(i["L0_attn_scale"]), bias=rows(i["L0_attn_bias"]), route_scale=rows(i["L0_ffn_route_scale"]))
    lanes = np.zeros((B, 32), f)

    def per_lane(v):
        out = lanes.copy()
        out[:, :NH] = v
        return out.reshape(P, 1)

    def per_col(m):
        out = np.zeros((P, 32), f)
        out[:, :NH] = m
        return out

    b = dict(masked=masked, wv=i["L1_attn_Wv"], wo=i["L1_attn_Wo"], wk=i["L1_attn_Wk"], wq=i["L1_attn_Wq"],
             wig=per_col(i["L1_attn_Wig"]), wfg=per_col(i["L1_attn_Wfg"]), router=i["L1_ffn_router_w"].T,
             wdown=i["L1_attn_Wdown"], norm_w=rows(i["L1_attn_norm_w"]), expert_bias=rows(i["L1_ffn_expert_bias"]),
             big=per_lane(i["L1_attn_big"]), bfg=per_lane(i["L1_attn_bfg"]),
             shared_gate=i["L1_ffn_w_gate_shared"].T, shared_down=down(i["L1_ffn_w_down_shared"].T), diag=diag)
    packed = {
        "x": i["L0_attn_Q"].reshape(N, D),
        "layer0": np.concatenate([a[k].reshape(P, n) for k, n in A_COLS.items()], axis=1),
        "layer1": np.concatenate([b[k].reshape(P, n) for k, n in B_COLS.items()], axis=1),
        "experts": np.concatenate([i["L1_ffn_w_gate"].reshape(C1, P, D).transpose(0, 2, 1),
                                   i["L1_ffn_w_down"].transpose(0, 2, 1).reshape(C1, P, D)], axis=2),
    }
    nc = bacc.Bacc("TRN2", target_bir_lowering=False, num_devices=1)
    arrays, args = {}, []
    for name, v in packed.items():
        v = np.ascontiguousarray(v)
        arrays[f"in_{name}"] = v
        args.append(nc.dram_tensor(f"in_{name}", v.shape, mybir.dt.from_np(v.dtype), kind="ExternalInput").ap())
    args.append(nc.dram_tensor("out", (N, D), F32, kind="ExternalOutput").ap())
    build(nc, *args)
    r = run_bass_kernel_spmd(nc, [arrays], core_ids=[0])
    return r.results[0]["out"].reshape(B, S, D)
```

```python
import concourse.bass as bass
from concourse import mybir
from contextlib import ExitStack

F32 = mybir.dt.float32
F32R = mybir.dt.float32r
BF16 = mybir.dt.bfloat16
I32 = mybir.dt.int32
ALU = mybir.AluOpType
ACT = mybir.ActivationFunctionType
AX = mybir.AxisListType

P = 128
D = 128
B, S = 4, 512
TPB = S // P
NT = B * TPB
N = NT * P
LN_EPS = 1e-5

E0, H0, K0 = 16, 32, 4
EPC0 = P // H0
C0 = E0 // EPC0
R0 = C0 * 3 * EPC0
PAD0 = 8 - K0

NH, DH = 4, 32
DV = DH + 1
CAP = 15.0
NORM_EPS = 1e-6
BACKEND_EPS = 1e-6
E1, H1, K1 = 160, 64, 8
EPC1 = P // H1
C1 = E1 // EPC1
ROUTED_SCALE = 2.5
TB = E1 // 2
NB = E1 // TB
MASKED = -30000.0

A_COLS = dict(ident=P, turn=P, rot_c=3, rot_s=3, scale=1, bias=1, route_scale=1, expert_sel=E0,
              ones=P, sel0=C0 * P, keys=C0 * P, values=C0 * D)
B_COLS = dict(masked=P, wv=D, wo=D, wk=D, wq=D, wig=32, wfg=32, router=E1, wdown=D, norm_w=D,
              expert_bias=E1, big=1, bfg=1, shared_gate=H1, shared_down=D, diag=NH * DV, lane=NH)


def places(cols):
    at, out = 0, {}
    for name, n in cols.items():
        out[name] = slice(at, at + n)
        at += n
    return out, at


A_AT, A_N = places(A_COLS)
B_AT, B_N = places(B_COLS)


def build(nc, x_in, a_in, b_in, w_in, x_out):
    x_rows = x_in.rearrange("(t p) d -> p t d", p=P)
    out_rows = x_out.rearrange("(t p) d -> p t d", p=P)
    comb_dram = nc.dram_tensor("combine_rows", (E1, N), F32, kind="Internal").ap()

    with ExitStack() as whole:
        def sem(name):
            return whole.enter_context(nc.semaphore(name))

        def chain(e, s):
            n = [0]

            def link(ins):
                n[0] += 1
                ins.then_inc(s, 1)
                e.wait_ge(s, n[0])
            return link

        def sb(name, shape, dt=F32, ctx=whole):
            return ctx.enter_context(nc.sbuf_tensor(name, shape, dt))

        bank = [whole.enter_context(nc.psum_tensor(f"bank{i}", [P, 512], F32)) for i in range(8)]

        A = sb("A", [P, A_N])
        Bw = sb("Bw", [P, B_N])
        a = {k: A[:, s] for k, s in A_AT.items()}
        w = {k: Bw[:, s] for k, s in B_AT.items()}
        X = sb("X", [P, NT, D])
        XT = sb("XT", [P, N])
        ident_bf = sb("ident_bf", [P, P], BF16)
        still = sb("still", [P, S], BF16)
        XH = sb("XH", [P, N], F32R)
        XL = sb("XL", [P, N], F32R)
        veps = sb("veps", [P, NT])
        rstd = sb("rstd", [P, NT])
        mv = sb("mv", [P, NT, 2])
        stats = sb("stats", [P, NT, 6])

        def keep_warm(e, bk, n):
            for _ in range(n):
                e.matmul(bank[bk][:, :], still[:, 0:P], still[:, :], start=True, stop=True)

        def norm_stats(e, link, b):
            ts = range(TPB * b, TPB * b + TPB)
            tb = slice(TPB * b, TPB * b + TPB)
            for t in ts:
                last = e.bn_stats(stats[:, t, :], X[:, t, :])
            link(last)
            for t in ts:
                last = e.bn_aggr(mv[:, t, :], stats[:, t, :])
            link(last)
            return e.tensor_scalar(veps[:, tb], mv[:, tb, 1], LN_EPS, None, ALU.add)

        def norm_apply(e, b, Xn, xn_ready):
            for t in range(TPB * b, TPB * b + TPB):
                last = e.tensor_scalar(Xn[:, t, :], X[:, t, :], mv[:, t, 0:1], rstd[:, t:t + 1],
                                       ALU.subtract, ALU.mult)
            last.then_inc(xn_ready, 1)

        def root_seed(e, link, out, v):
            link(e.tensor_scalar(out.bitcast(I32), v.bitcast(I32), 1, None, ALU.logical_shift_right))
            return e.tensor_scalar(out.bitcast(I32), out.bitcast(I32), -1.0, float(0x5F3759DF), ALU.mult, ALU.add)

        def root_refine(e, link, y, v, tmp):
            for step in range(3):
                link(e.tensor_tensor(tmp, y, y, ALU.mult))
                link(e.tensor_tensor(tmp, tmp, v, ALU.mult))
                link(e.tensor_scalar(tmp, tmp, -0.5, 1.5, ALU.mult, ALU.add))
                last = e.tensor_tensor(y, y, tmp, ALU.mult)
                if step < 2:
                    link(last)
            return last

        with ExitStack() as l0:
            Xn = sb("Xn", [P, NT, D], ctx=l0)
            QH = sb("QH", [P, N], F32R, ctx=l0)
            QL = sb("QL", [P, N], F32R, ctx=l0)
            keys_hi = sb("keys_hi", [P, C0 * P], F32R, ctx=l0)
            keys_lo = sb("keys_lo", [P, C0 * P], F32R, ctx=l0)
            V = sb("V", [P, NT, D], ctx=l0)
            U = sb("U", [P, NT, D], ctx=l0)
            gate = sb("gate", [P, NT, D], ctx=l0)
            scaled = sb("scaled", [P, NT, D], ctx=l0)
            norm0 = sb("norm0", [P, NT], ctx=l0)
            ex = sb("ex", [P, NT * E0], ctx=l0)
            comb0T = sb("comb0T", [R0, N], BF16, ctx=l0)
            sel0_bf = sb("sel0_bf", [R0, C0, P], BF16, ctx=l0)

            with ExitStack() as ph:
                rn = sb("rn", [P, 3], ctx=ph)
                rn2 = sb("rn2", [P, 3], ctx=ph)
                cs = sb("cs", [P, 3], ctx=ph)
                sn = sb("sn", [P, 3], ctx=ph)
                two = sb("two", [P, 1], ctx=ph)
                rt = sb("rt", [P, 3, P], ctx=ph)
                rot = sb("rot", [P, 3, P], ctx=ph)
                Mq = sb("Mq", [P, P], ctx=ph)
                x_loaded = [sem(f"x_loaded{b}") for b in range(B)]
                a_loaded, a_rest_loaded, b_loaded = sem("a_loaded"), sem("a_rest_loaded"), sem("b_loaded")
                early = A_AT["ones"].start
                dve_order = sem("dve_order_a")
                std_asked, std_ready, xn_ready = sem("std_asked"), sem("std_ready"), sem("xn_ready")
                xt_turned, xt_ready = sem("xt_turned"), sem("xt_ready")
                rot_asked, rot_ready, rot_made = sem("rot_asked"), sem("rot_ready"), sem("rot_made")
                rot_product, mq_ready = sem("rot_product"), sem("mq_ready")
                logits_ready, exp_ready = sem("logits_ready"), sem("exp_ready")
                v_made, v_ready, q_made, q_ready = sem("v_made"), sem("v_ready"), sem("q_made"), sem("q_ready")
                keys_ready, xh_ready = sem("keys_ready"), sem("xh_ready0")
                still_ready = sem("still_ready")
                block = ph.enter_context(nc.Block())

                @block.sync
                def _(e):
                    for b in range(B):
                        tb = slice(TPB * b, TPB * b + TPB)
                        e.dma_start(X[:, tb, :], x_rows[:, tb, :]).then_inc(x_loaded[b], 16)

                @block.scalar
                def _(e):
                    e.dma_start(A[:, 0:early], a_in[:, 0:early]).then_inc(a_loaded, 16)
                    e.dma_start(A[:, early:A_N], a_in[:, early:A_N]).then_inc(a_rest_loaded, 16)
                    e.dma_start(Bw[:, :], b_in).then_inc(b_loaded, 16)

                    def turned(b):
                        e.wait_ge(xt_turned, b + 1)
                        e.copy(XT[:, S * b:S * b + S], bank[b][:, :]).then_inc(xt_ready, 1)

                    e.wait_ge(rot_asked, 1)
                    e.activation(rn[:, :], rn2[:, :], ACT.Sqrt).then_inc(rot_ready, 1)
                    for b in range(B):
                        tb = slice(TPB * b, TPB * b + TPB)
                        e.wait_ge(std_asked, b + 1)
                        e.activation(rstd[:, tb], veps[:, tb], ACT.Sqrt).then_inc(std_ready, 1)
                        if b:
                            turned(b - 1)
                    turned(B - 1)
                    e.wait_ge(logits_ready, B)
                    e.activation(ex[:, :], bank[4][:, 0:NT * E0], ACT.Exp, scale=-1.0).then_inc(exp_ready, 1)
                    for b in range(B):
                        e.wait_ge(q_made, b + 1)
                        e.copy(QH[:, S * b:S * b + S], bank[b][:, :]).then_inc(q_ready, 1)
                    e.wait_ge(b_loaded, 16)

                @block.gpsimd
                def _(e):
                    e.memset(still[:, :], 0.0).then_inc(still_ready, 1)
                    e.wait_ge(a_rest_loaded, 16)
                    e.tensor_copy(keys_hi[:, :], a["keys"]).then_inc(keys_ready, 1)
                    e.wait_ge(keys_ready, 1)
                    e.tensor_tensor(keys_lo[:, :], a["keys"], keys_hi[:, :].bitcast(F32), ALU.subtract)
                    e.tensor_copy(sel0_bf[:, :, :], a["sel0"][0:R0, :].rearrange("r (c m) -> r c m", c=C0))
                    for b in range(B):
                        s = slice(S * b, S * b + S)
                        e.wait_ge(xt_ready, b + 1)
                        e.tensor_copy(XH[:, s], XT[:, s]).then_inc(xh_ready, 1)
                        e.wait_ge(xh_ready, b + 1)
                        e.tensor_tensor(XL[:, s], XT[:, s], XH[:, s].bitcast(F32), ALU.subtract)

                @block.vector
                def _(e):
                    link = chain(e, dve_order)
                    e.wait_ge(a_loaded, 16)
                    e.tensor_copy(ident_bf[:, :], a["ident"])
                    link(e.tensor_tensor(cs[:, :], a["rot_c"], a["rot_c"], ALU.mult))
                    link(e.tensor_tensor(sn[:, :], a["rot_s"], a["rot_s"], ALU.mult))
                    e.tensor_tensor(rn2[:, :], cs[:, :], sn[:, :], ALU.add).then_inc(rot_asked, 1)
                    for b in range(B):
                        e.wait_ge(x_loaded[b], 16)
                        norm_stats(e, link, b).then_inc(std_asked, 1)
                        if b:
                            e.wait_ge(std_ready, b)
                            link(e.reciprocal(rstd[:, TPB * (b - 1):TPB * b], rstd[:, TPB * (b - 1):TPB * b]))
                            norm_apply(e, b - 1, Xn, xn_ready)
                        if b == 0:
                            e.wait_ge(rot_ready, 1)
                            e.reciprocal(two[:, :], a["scale"])
                            link(e.reciprocal(rn[:, :], rn[:, :]))
                            e.tensor_tensor(cs[:, :], a["rot_c"], rn[:, :], ALU.mult)
                            link(e.tensor_tensor(sn[:, :], a["rot_s"], rn[:, :], ALU.mult))
                            for i in range(3):
                                last = e.tensor_scalar(rt[:, i, :], a["turn"], sn[:, i:i + 1], None, ALU.mult)
                            link(last)
                            for i in range(3):
                                last = e.scalar_tensor_tensor(rot[:, i, :], a["ident"], cs[:, i:i + 1], rt[:, i, :],
                                                              ALU.mult, ALU.subtract if i == 2 else ALU.add)
                            last.then_inc(rot_made, 1)
                    e.wait_ge(std_ready, B)
                    link(e.reciprocal(rstd[:, TPB * (B - 1):NT], rstd[:, TPB * (B - 1):NT]))
                    norm_apply(e, B - 1, Xn, xn_ready)
                    e.wait_ge(rot_product, 1)
                    e.tensor_scalar(Mq[:, :], bank[5][:, 0:P], two[:, 0:1], 2.0, ALU.mult, ALU.mult).then_inc(mq_ready, 1)
                    for b in range(B):
                        e.wait_ge(q_ready, b + 1)
                        e.tensor_tensor(QL[:, S * b:S * b + S], bank[b][:, :], QH[:, S * b:S * b + S].bitcast(F32), ALU.subtract)
                    for b in range(B):
                        e.wait_ge(v_made, b + 1)
                        e.tensor_copy(V[:, TPB * b:TPB * b + TPB, :],
                                      bank[4 + b][:, :].rearrange("p (t d) -> p t d", d=D)).then_inc(v_ready, 1)
                @block.tensor
                def _(e):
                    e.wait_ge(still_ready, 1)
                    keep_warm(e, 7, 20)
                    e.wait_ge(a_loaded, 16)

                    def logits(b):
                        e.wait_ge(xt_ready, b + 1)
                        for t in range(TPB * b, TPB * b + TPB):
                            last = e.matmul(bank[4][:, E0 * t:E0 * t + E0], XT[:, P * t:P * t + P], a["expert_sel"],
                                            start=True, stop=True)
                        last.then_inc(logits_ready, 1)

                    e.wait_ge(rot_made, 1)
                    e.matmul(bank[5][:, 0:P], rot[:, 0, :], rot[:, 1, :], start=True, stop=True).then_inc(rot_product, 1)
                    for b in range(B):
                        e.wait_ge(xn_ready, b + 1)
                        for j in range(TPB):
                            last = e.transpose(bank[b][:, P * j:P * j + P], Xn[:, TPB * b + j, :], a["ident"])
                        last.then_inc(xt_turned, 1)
                        if b:
                            logits(b - 1)
                        keep_warm(e, 7, 5)
                    logits(B - 1)
                    e.wait_ge(mq_ready, 1)
                    for b in range(B):
                        e.matmul(bank[b][:, :], Mq[:, :], XT[:, S * b:S * b + S], start=True, stop=True).then_inc(q_made, 1)
                    e.wait_ge(exp_ready, 1)
                    for b in range(B):
                        for j in range(TPB):
                            t = TPB * b + j
                            last = e.matmul(bank[4 + b][:, P * j:P * j + P], XT[:, P * t:P * t + P], rot[:, 2, :],
                                            start=True, stop=True)
                        last.then_inc(v_made, 1)

            with ExitStack() as ph:
                nmax = sb("nmax", [P, NT], ctx=ph)
                rows = sb("rows", [P, NT], ctx=ph)
                prb = sb("prb", [P, 2, S], ctx=ph)
                prT = sb("prT", [P, 2, S], ctx=ph)
                ss = sb("ss", [P, NT], ctx=ph)
                root_tmp = sb("root_tmp", [P, TPB], ctx=ph)
                G0 = sb("G0", [P, 2, C0, S], ctx=ph)
                act0 = sb("act0", [P, 4, S], ctx=ph)
                scores_made, max_ready, probs_ready = sem("scores_made"), sem("max_ready"), sem("probs_ready")
                probs_turned, probsT_ready = sem("probs_turned"), sem("probsT_ready")
                u_made, u_ready = sem("u_made"), sem("u_ready")
                dve_order, pool_order = sem("dve_order_b"), sem("pool_order_b")
                h_made, b_made, act_ready, g_ready = sem("h0_made"), sem("b0_made"), sem("act0_ready"), sem("g0_ready")
                y_made, gate_ready = sem("y0_made"), sem("gate_ready")
                norm_asked, norm_ready = sem("norm_asked"), sem("norm_ready")
                std_asked, std_ready, xn_ready = sem("std_asked1"), sem("std_ready1"), sem("xn_ready1")
                xt_turned, xt_ready = sem("xt_turned1"), sem("xt_ready1")
                SCORES = (0, 1, 7)
                SPREAD = (2, 3, 7)
                APPLIED_BY_POOL = 2
                prob = sb("prob", [P, NT, E0 + PAD0], ctx=ph)
                zap = sb("zap", [P, NT, E0 + PAD0], ctx=ph)
                top = sb("top", [P, NT, 8], ctx=ph)
                take = sb("take", [P, NT, 8], ctx=ph)
                tot = sb("tot", [P, NT], ctx=ph)
                cw = sb("cw", [P, NT, E0], ctx=ph)
                cwr = sb("cwr", [P, NT, E0], ctx=ph)
                parts = sb("parts", [P, NT, R0], BF16, ctx=ph)
                parts_ready, comb_turned, comb_ready = sem("parts_ready"), sem("comb_turned"), sem("comb_ready")
                routed = sem("routed")
                ROWS_AT, TURN_AT, TURNED_AT = 5, (10, 12), (11, 13)
                STEP_AT = dict(down=5, gate=6, add=7, stats=9, apply=12, turn=15, copy=16)
                LAST = C0 * (B - 1) + STEP_AT["copy"] + 1

                def beside(u, *steps):
                    return [(g, k) for g in range(B) for k in steps if u == C0 * g + STEP_AT[k]]
                block = ph.enter_context(nc.Block())

                @block.tensor
                def _(e):
                    def scores(t):
                        if t >= 3:
                            e.wait_ge(probs_ready, t - 2)
                        b = t // TPB
                        ts, bs = slice(P * t, P * t + P), slice(S * b, S * b + S)
                        bk = bank[SCORES[t % 3]]
                        e.matmul(bk[:, :], QH[:, ts], XH[:, bs], start=True, stop=False)
                        e.matmul(bk[:, :], QH[:, ts], XL[:, bs], start=False, stop=False)
                        e.matmul(bk[:, :], QL[:, ts], XH[:, bs], start=False, stop=True).then_inc(scores_made, 1)

                    def turn(t):
                        e.wait_ge(probs_ready, t + 1)
                        if t >= 2:
                            e.wait_ge(probsT_ready, t - 1)
                        for j in range(TPB):
                            last = e.transpose(bank[2 + t % 2][:, P * j:P * j + P], prb[:, t % 2, P * j:P * j + P],
                                               a["ident"])
                        last.then_inc(probs_turned, 1)

                    def values(t):
                        e.wait_ge(probsT_ready, t + 1)
                        if t >= 2:
                            e.wait_ge(u_ready, t - 1)
                        b = t // TPB
                        for j in range(TPB):
                            last = e.matmul(bank[4 + t % 2][:, 0:D], prT[:, t % 2, P * j:P * j + P],
                                            V[:, TPB * b + j, :], start=(j == 0), stop=(j == TPB - 1))
                        last.then_inc(u_made, 1)

                    def turn_parts(half):
                        if half == 0:
                            e.wait_ge(parts_ready, 1)
                        else:
                            e.wait_ge(comb_ready, 1)
                        for j in range(NT // 2):
                            last = e.transpose(bank[6][0:R0, :].bitcast(BF16)[:, P * j:P * j + P],
                                               parts[:, NT // 2 * half + j, :], ident_bf[:, :])
                        last.then_inc(comb_turned, 1)

                    scores(0)
                    scores(1)
                    for t in range(NT + 1):
                        if t + 2 < NT:
                            scores(t + 2)
                        if t < NT:
                            turn(t)
                        if t >= 1:
                            values(t - 1)
                        if t in TURN_AT:
                            turn_parts(TURN_AT.index(t))

                    def hidden(u):
                        g, c = u // C0, u % C0
                        if u >= 2:
                            e.wait_ge(act_ready, u - 1)
                        elif u == 0:
                            e.wait_ge(probs_ready, NT)
                            e.wait_ge(probsT_ready, NT)
                            e.wait_ge(comb_ready, 2)
                        ks, gs = slice(P * c, P * c + P), slice(S * g, S * g + S)
                        e.matmul(bank[u % 2][:, :], keys_hi[:, ks], XH[:, gs], start=True, stop=False)
                        e.matmul(bank[u % 2][:, :], keys_hi[:, ks], XL[:, gs], start=False, stop=False)
                        e.matmul(bank[u % 2][:, :], keys_lo[:, ks], XH[:, gs], start=False, stop=True).then_inc(h_made, 1)
                        if u >= 3:
                            e.wait_ge(g_ready, u - 2)
                        e.matmul(bank[SPREAD[u % 3]][:, :], sel0_bf[:, c, :], comb0T[:, S * g:S * g + S],
                                 start=True, stop=True).then_inc(b_made, 1)

                    def down(g):
                        e.wait_ge(g_ready, C0 * g + C0)
                        if g >= 2:
                            e.wait_ge(gate_ready, g - 1)
                        else:
                            e.wait_ge(u_ready, NT)
                        for j in range(TPB):
                            for c in range(C0):
                                last = e.matmul(bank[4 + g % 2][:, P * j:P * j + P], G0[:, g % 2, c, P * j:P * j + P],
                                                a["values"][:, P * c:P * c + P], start=(c == 0), stop=(c == C0 - 1))
                        last.then_inc(y_made, 1)

                    def turn_norm(b):
                        e.wait_ge(xn_ready, b + 1)
                        if b:
                            e.wait_ge(xt_ready, b)
                        for j in range(TPB):
                            last = e.transpose(bank[6][:, P * j:P * j + P], Xn[:, TPB * b + j, :], a["ident"])
                        last.then_inc(xt_turned, 1)

                    for u in range(LAST):
                        if u < B * C0:
                            hidden(u)
                        for g, step in beside(u, "turn", "down"):
                            (down if step == "down" else turn_norm)(g)
                            if g == B - 2 and step == "turn" or g == B - 1 and step == "down":
                                keep_warm(e, 0, 20)

                @block.vector
                def _(e):
                    link = chain(e, dve_order)

                    def row_max(t):
                        e.wait_ge(scores_made, t + 1)
                        link(e.tensor_reduce(nmax[:, t:t + 1], bank[SCORES[t % 3]][:, :], AX.X, ALU.max, negate=True))
                        e.tensor_scalar(nmax[:, t:t + 1], nmax[:, t:t + 1], a["bias"], a["bias"],
                                        ALU.subtract, ALU.add).then_inc(max_ready, 1)

                    def finish(b, step):
                        tb = slice(TPB * b, TPB * b + TPB)
                        if step == "root_of_rows":
                            sq = scaled[:, tb, :]
                            e.wait_ge(u_ready, TPB * b + TPB)
                            e.tensor_tensor(rows[:, tb], rows[:, tb], rows[:, tb], ALU.mult)
                            link(e.tensor_tensor(sq, U[:, tb, :], U[:, tb, :], ALU.mult))
                            link(e.tensor_reduce(ss[:, tb], sq, AX.X, ALU.add))
                            link(e.scalar_tensor_tensor(ss[:, tb], rows[:, tb], 1e-8, ss[:, tb], ALU.mult, ALU.max))
                            root_seed(e, link, norm0[:, tb], ss[:, tb]).then_inc(norm_asked, 1)
                        elif step == "add":
                            e.wait_ge(norm_ready, b + 1)
                            e.wait_ge(gate_ready, b + 1)
                            for t in range(TPB * b, TPB * b + TPB):
                                last = e.scalar_tensor_tensor(scaled[:, t, :], U[:, t, :], norm0[:, t:t + 1], gate[:, t, :],
                                                              ALU.mult, ALU.mult)
                            link(last)
                            link(e.tensor_tensor(X[:, tb, :], X[:, tb, :], scaled[:, tb, :], ALU.add))
                        elif step == "stats":
                            link(norm_stats(e, link, b))
                            root_seed(e, link, rstd[:, tb], veps[:, tb]).then_inc(std_asked, 1)

                    def apply(b):
                        if b >= APPLIED_BY_POOL:
                            e.wait_ge(std_ready, b + 1)
                            norm_apply(e, b, Xn, xn_ready)

                    def route(step):
                        if step == 0:
                            link(e.tensor_scalar(ex[:, :], ex[:, :], 1.0, None, ALU.add))
                            for i in range(PAD0):
                                e.memset(prob[:, :, E0 + i:E0 + i + 1], -1.0 - i)
                                e.memset(take[:, :, K0 + i:K0 + i + 1], -1.0 - i)
                        elif step == 1:
                            link(e.reciprocal(prob[:, :, 0:E0], ex[:, :].rearrange("p (t e) -> p t e", e=E0)))
                        elif step == 2:
                            for t in range(NT):
                                last = e.max(top[:, t, :], prob[:, t, 0:E0])
                            link(last)
                        elif step == 3:
                            e.tensor_reduce(tot[:, :], top[:, :, 0:K0], AX.X, ALU.add)
                            link(e.tensor_copy(take[:, :, 0:K0], top[:, :, 0:K0]))
                            link(e.tensor_scalar(tot[:, :], tot[:, :], 1e-9, None, ALU.max))
                            link(e.reciprocal(tot[:, :], tot[:, :]))
                            link(e.tensor_scalar(tot[:, :], tot[:, :], a["route_scale"], None, ALU.mult))
                        elif step == 4:
                            for t in range(NT):
                                last = e.match_replace(zap[:, t, :], take[:, t, :], prob[:, t, :], 0.0)
                            last.then_inc(routed, 1)

                    row_max(0)
                    row_max(1)
                    for t in range(TPB * (B - 1) + ROWS_AT + 1):
                        if t + 2 < NT:
                            row_max(t + 2)
                        route(t)
                        if t in TURNED_AT:
                            half = TURNED_AT.index(t)
                            e.wait_ge(comb_turned, half + 1)
                            e.tensor_copy(comb0T[:, half * (N // 2):(half + 1) * (N // 2)],
                                          bank[6][0:R0, :].bitcast(BF16)).then_inc(comb_ready, 1)
                        if t >= ROWS_AT and (t - ROWS_AT) % TPB == 0:
                            finish((t - ROWS_AT) // TPB, "root_of_rows")

                    def weigh(u):
                        g, c = u // C0, u % C0
                        e.wait_ge(b_made, u + 1)
                        e.wait_ge(act_ready, u + 1)
                        if c == 0 and g >= 2:
                            e.wait_ge(y_made, g - 1)
                        e.tensor_tensor(G0[:, g % 2, c, :], act0[:, u % 4, :], bank[SPREAD[u % 3]][:, :],
                                        ALU.mult).then_inc(g_ready, 1)

                    for u in range(LAST):
                        if u < B * C0:
                            weigh(u)
                        for g, step in beside(u, "apply", "add", "stats"):
                            apply(g) if step == "apply" else finish(g, step)

                @block.scalar
                def _(e):
                    def gate_of(g):
                        e.wait_ge(y_made, g + 1)
                        e.activation(gate[:, TPB * g:TPB * g + TPB, :],
                                     bank[4 + g % 2][:, :].rearrange("p (t d) -> p t d", d=D), ACT.Silu).then_inc(gate_ready, 1)

                    def turned(b):
                        e.wait_ge(xt_turned, b + 1)
                        e.copy(XT[:, S * b:S * b + S], bank[6][:, :]).then_inc(xt_ready, 1)

                    def exponent(t):
                        e.wait_ge(max_ready, t + 1)
                        if t >= 2:
                            e.wait_ge(probs_turned, t - 1)
                        e.activation(prb[:, t % 2, :], bank[SCORES[t % 3]][:, :], ACT.Exp, bias=nmax[:, t:t + 1],
                                     accum_out=rows[:, t:t + 1]).then_inc(probs_ready, 1)

                    def copy_turned(t):
                        e.wait_ge(probs_turned, t + 1)
                        if t >= 2:
                            e.wait_ge(u_made, t - 1)
                        e.copy(prT[:, t % 2, :], bank[2 + t % 2][:, :]).then_inc(probsT_ready, 1)

                    exponent(0)
                    for t in range(NT + 1):
                        if t + 1 < NT:
                            exponent(t + 1)
                        if t < NT:
                            copy_turned(t)
                        if t >= 1:
                            e.wait_ge(u_made, t)
                            e.copy(U[:, t - 1, :], bank[4 + (t - 1) % 2][:, 0:D]).then_inc(u_ready, 1)

                    for u in range(LAST):
                        if u < B * C0:
                            e.wait_ge(h_made, u + 1)
                            if u >= 4:
                                e.wait_ge(g_ready, u - 3)
                            e.activation(act0[:, u % 4, :], bank[u % 2][:, :], ACT.Relu).then_inc(act_ready, 1)
                        for g, step in beside(u, "copy", "gate"):
                            (gate_of if step == "gate" else turned)(g)

                @block.gpsimd
                def _(e):
                    link = chain(e, pool_order)
                    pv = parts[:, :, :].rearrange("p t (c h e) -> p t c h e", c=C0, h=3)
                    cv = cw[:, :, :].rearrange("p t (c e) -> p t c e", c=C0)
                    rv = cwr[:, :, :].rearrange("p t (c e) -> p t c e", c=C0)
                    e.wait_ge(routed, 1)
                    link(e.tensor_tensor(cw[:, :, :], prob[:, :, 0:E0], zap[:, :, 0:E0], ALU.subtract))
                    link(e.tensor_tensor(cw[:, :, :], cw[:, :, :],
                                         tot[:, :].rearrange("p (t o) -> p t o", o=1).to_broadcast([P, NT, E0]), ALU.mult))
                    link(e.tensor_copy(pv[:, :, :, 0, :], cv))
                    link(e.tensor_tensor(rv, cv, pv[:, :, :, 0, :], ALU.subtract))
                    link(e.tensor_copy(pv[:, :, :, 1, :], rv))
                    e.tensor_tensor(pv[:, :, :, 2, :], rv, pv[:, :, :, 1, :], ALU.subtract).then_inc(parts_ready, 1)
                    for b in range(B):
                        tb = slice(TPB * b, TPB * b + TPB)
                        e.wait_ge(norm_asked, b + 1)
                        root_refine(e, link, norm0[:, tb], ss[:, tb], root_tmp[:, :]).then_inc(norm_ready, 1)
                        e.wait_ge(norm_ready, b + 1)
                    for b in range(B):
                        tb = slice(TPB * b, TPB * b + TPB)
                        e.wait_ge(std_asked, b + 1)
                        root_refine(e, link, rstd[:, tb], veps[:, tb], root_tmp[:, :]).then_inc(std_ready, 1)
                        e.wait_ge(std_ready, b + 1)
                        if b < APPLIED_BY_POOL:
                            norm_apply(e, b, Xn, xn_ready)

        with ExitStack() as l1:
            S1 = sb("S1", [P, NT, D], ctx=l1)

            G = N // S
            PAIR = 2 * G
            TURNS = C1 // 2
            HALVES, GPH = 2, G // 2
            zeros = sb("zeros", [P, P], ctx=l1)
            staged = sb("staged", [P, 2, 2 * P], ctx=l1)
            gate_hi = sb("gate_hi", [P, 2, P], F32R, ctx=l1)
            gate_lo = sb("gate_lo", [P, 2, P], F32R, ctx=l1)
            down_hi = sb("down_hi", [P, 2, P], F32R, ctx=l1)
            down_lo = sb("down_lo", [P, 2, P], F32R, ctx=l1)
            comb = sb("comb", [P, 2, N], ctx=l1)
            shared = sb("shared", [H1, G, S], ctx=l1)
            staged_in = [sem(f"staged_in{i}") for i in range(2)]
            comb_in = [[sem(f"comb_in{i}_{h}") for h in range(HALVES)] for i in range(2)]
            gate_hi_ready, gate_ready = sem("gate_hi_ready"), sem("gate_parts_ready")
            down_hi_ready, down_ready = sem("down_hi_ready"), sem("down_parts_ready")
            zeros_ready, up_made, y_made = sem("zeros_ready"), sem("up_made"), sem("y1_made")

            def load_chunk(e, s, c):
                e.dma_start(staged[:, s, :], w_in[c, :, :].rearrange("o p n -> (o p) n")).then_inc(staged_in[s], 16)

            def load_comb(e, s, h, first):
                cols = slice(S * GPH * h, S * GPH * (h + 1))
                for x in range(EPC1):
                    e.dma_start(comb[H1 * x:H1 * x + H1, s, cols],
                                comb_dram[bass.ds(first + x, 1), cols].to_broadcast([H1, S * GPH])
                                ).then_inc(comb_in[s][h], 16)

            def split(e, i, s):
                c = i * 2 + s
                e.wait_ge(staged_in[s], i * 16 + 16)
                if not (isinstance(i, int) and i == 0):
                    e.wait_ge(up_made, i * PAIR + (G * s - G))
                e.tensor_tensor(gate_hi[:, s, :], staged[:, s, 0:P], zeros[:, :], ALU.subtract).then_inc(gate_hi_ready, 1)
                e.wait_ge(gate_hi_ready, c + 1)
                e.tensor_tensor(gate_lo[:, s, :], staged[:, s, 0:P], gate_hi[:, s, :].bitcast(F32),
                                ALU.subtract).then_inc(gate_ready, 1)
                if not (isinstance(i, int) and i == 0):
                    e.wait_ge(y_made, i * PAIR + (G * s - G))
                e.tensor_tensor(down_hi[:, s, :], staged[:, s, P:2 * P], zeros[:, :], ALU.subtract).then_inc(down_hi_ready, 1)
                e.wait_ge(down_hi_ready, c + 1)
                e.tensor_tensor(down_lo[:, s, :], staged[:, s, P:2 * P], down_hi[:, s, :].bitcast(F32),
                                ALU.subtract).then_inc(down_ready, 1)

            with ExitStack() as at:
                VA = sb("VA", [P, NT, NH, DV], ctx=at)
                K = sb("K", [P, NT, D], ctx=at)
                og = sb("og", [P, NT, D], ctx=at)
                qT = sb("qT", [P, N], ctx=at)
                kT = sb("kT", [P, N], ctx=at)
                O = sb("O", [P, NT, NH, DV], ctx=at)
                logits = sb("logits", [P, NT, E1], ctx=at)
                floor = sb("floor", [P, TPB, P], ctx=at)
                k_scale = sb("k_scale", [P, TPB, P], ctx=at)
                q_scale = sb("q_scale", [P, TPB - 1, P], ctx=at)
                decay = sb("decay", [P, TPB - 1, P], ctx=at)
                aT = sb("aT", [P, TPB, P], ctx=at)
                prob = sb("prob1", [P, NT, E1], ctx=at)
                dn = sb("dn", [P, NT, NH], ctx=at)
                mu = sb("mu", [P, NT, NH], ctx=at)
                var = sb("var", [P, NT, NH], ctx=at)
                sq = sb("sq", [P, TPB, NH, DH], ctx=at)

                def flat(m, tb):
                    return m[:, tb, :].rearrange("p t h -> p (t h)")

                def spread(m, tb):
                    return m[:, tb, :].rearrange("p t (h o) -> p (t h) o", o=1).to_broadcast([P, TPB * NH, DH])

                def values_of(b):
                    return O[:, TPB * b:TPB * b + TPB, :, 0:DH].rearrange("p t h d -> p (t h) d")

                sqv = sq[:, :, :, :].rearrange("p t h d -> p (t h) d")

                def head_divisors(e, link, b):
                    tb = slice(TPB * b, TPB * b + TPB)
                    sums = O[:, tb, :, DH:DV].rearrange("p t h o -> p t (h o)")
                    link(e.scalar_tensor_tensor(dn[:, tb, :], sums, -1.0, sums, ALU.mult, ALU.max))
                    link(e.tensor_tensor(dn[:, tb, :], dn[:, tb, :], floor[:, :, 32 * b:32 * b + NH], ALU.max))
                    link(e.tensor_scalar(flat(dn, tb), flat(dn, tb), BACKEND_EPS, None, ALU.add))
                    return e.reciprocal(flat(dn, tb), flat(dn, tb))

                def head_divide(e, b):
                    tb = slice(TPB * b, TPB * b + TPB)
                    return e.tensor_tensor(values_of(b), values_of(b), spread(dn, tb), ALU.mult)

                def head_means(e, link, b):
                    tb = slice(TPB * b, TPB * b + TPB)
                    link(e.tensor_reduce(flat(mu, tb), values_of(b), AX.X, ALU.add))
                    return e.tensor_scalar(flat(mu, tb), flat(mu, tb), 1 / DH, None, ALU.mult)

                def head_center(e, b):
                    tb = slice(TPB * b, TPB * b + TPB)
                    return e.tensor_tensor(values_of(b), values_of(b), spread(mu, tb), ALU.subtract)

                def head_squares(e, b):
                    return e.tensor_tensor(sqv, values_of(b), values_of(b), ALU.mult)

                def head_vars(e, link, b):
                    tb = slice(TPB * b, TPB * b + TPB)
                    link(e.tensor_reduce(flat(var, tb), sqv, AX.X, ALU.add))
                    return e.tensor_scalar(flat(var, tb), flat(var, tb), 1 / DH, NORM_EPS, ALU.mult, ALU.add)
                mh = sb("mh", [P, S], F32R, ctx=at)
                ml = sb("ml", [P, S], F32R, ctx=at)
                ones_r = sb("ones_r", [P, P], F32R, ctx=at)
                mh_own, ml_own = (comb[:, i, :].bitcast(F32R).rearrange("p (j h n) -> p j h n", j=TPB, h=NH)
                                  for i in range(2))
                masked_bf = sb("masked_bf", [P, TPB, P], BF16, ctx=at)

                with ExitStack() as ph:
                    g = {k: sb(f"g_{k}", [P, S], ctx=ph) for k in
                         ("ti", "tf", "x", "y", "u", "c", "ru", "ln", "lf", "a", "M", "m", "ones")}
                    bias15 = sb("bias15", [P, 2], ctx=ph)
                    Rdiag = sb("Rdiag", [P, TPB, P], ctx=ph)
                    R = sb("R", [P, TPB, P], ctx=ph)
                    proj_made, proj_read_v, proj_read_s = sem("proj_made"), sem("proj_read_v"), sem("proj_read_s")
                    router_made, router_read = sem("router_made"), sem("router_read")
                    qk_made, qk_read = sem("qk_made"), sem("qk_read")
                    gates_made, tanh_ready, bias_ready = sem("gates_made"), sem("tanh_ready"), sem("bias_ready")
                    abs_ready, y_ready, u_ready, ln_ready = sem("abs_ready"), sem("y_ready"), sem("u1_ready"), sem("ln_ready")
                    rows_ready, rows_turned, R_made, R_ready = sem("rows_ready"), sem("rows_turned"), sem("R_made"), sem("R_ready")
                    diff_ready = sem("diff_ready")
                    dve_order, prob_ready = sem("dve_order_d"), sem("prob_ready")
                    router_exp_ready, xh_ready = sem("router_exp_ready"), sem("xh_ready")
                    ru_ready, aT_ready, m_copied = sem("ru_ready"), sem("aT_ready"), sem("m_copied")
                    FIRST = 2
                    TURN_1, TURN_2 = 9, 12
                    block = ph.enter_context(nc.Block())

                    @block.tensor
                    def _(e):
                        def gates():
                            for i, name in enumerate(("wig", "wfg")):
                                for b in range(B):
                                    last = e.matmul(bank[6 + i][32 * b:32 * b + 32, :], w[name], XT[:, S * b:S * b + S],
                                                    start=True, stop=True)
                            last.then_inc(gates_made, 1)

                        def turn_rows(bk, name):
                            for j in range(TPB):
                                last = e.transpose(bank[bk][:, P * j:P * j + P], g[name][:, P * j:P * j + P], a["ident"])
                            return last

                        for t in range(NT):
                            if t >= 2:
                                e.wait_ge(proj_read_v, t - 1)
                                e.wait_ge(proj_read_s, t - 1)
                                e.wait_ge(router_read, t - 1)
                            xt = XT[:, P * t:P * t + P]
                            wall = Bw[:, B_AT["wv"].start:B_AT["wk"].stop]
                            e.matmul(bank[t % 2][:, 0:3 * D], xt, wall, start=True, stop=True).then_inc(proj_made, 1)
                            e.matmul(bank[2 + t % 2][:, 0:E1], xt, w["router"], start=True, stop=True).then_inc(router_made, 1)
                            if t % 2 == 1:
                                i = t // 2
                                if i >= 2:
                                    e.wait_ge(qk_read, i - 1)
                                e.matmul(bank[4 + i % 2][:, :], w["wq" if i % 2 == 0 else "wk"],
                                         XT[:, S * (i // 2):S * (i // 2) + S], start=True, stop=True).then_inc(qk_made, 1)
                            if t == FIRST - 1:
                                gates()
                            if t == TURN_1:
                                e.wait_ge(rows_ready, 3)
                                turn_rows(6, "a")
                                turn_rows(7, "m").then_inc(rows_turned, 1)
                            if t == TURN_2:
                                e.wait_ge(aT_ready, 1)
                                turn_rows(6, "M")
                                e.wait_ge(m_copied, 1)
                                e.wait_ge(R_made, 1)
                                for j in range(TPB):
                                    last = e.matmul(bank[7][:, P * j:P * j + P], a["ones"], Rdiag[:, j, :], start=True, stop=True)
                                last.then_inc(rows_turned, 1)
                        e.wait_ge(qk_read, NT // 2)
                        keep_warm(e, 4, 24)

                    @block.scalar
                    def _(e):
                        def gate_functions():
                            e.wait_ge(gates_made, 1)
                            e.wait_ge(bias_ready, 1)
                            e.activation(g["tf"][:, :], bank[7][:, :], ACT.Tanh, bias=bias15[:, 1:2], scale=1 / CAP).then_inc(tanh_ready, 1)
                            e.activation(g["ti"][:, :], bank[6][:, :], ACT.Tanh, bias=bias15[:, 0:1], scale=1 / CAP).then_inc(tanh_ready, 1)
                            e.wait_ge(abs_ready, 1)
                            e.activation(g["y"][:, :], g["ru"][:, :], ACT.Exp, scale=-1.0).then_inc(y_ready, 1)
                            e.wait_ge(u_ready, 1)
                            e.activation(g["ln"][:, :], g["u"][:, :], ACT.Ln).then_inc(ln_ready, 1)
                            e.wait_ge(y_ready, 1)
                            e.activation(g["ru"][:, :], g["ru"][:, :], ACT.Sigmoid).then_inc(ru_ready, 1)

                        for t in range(NT):
                            if t and t % TPB == 0:
                                tb = slice(t - TPB, t)
                                e.wait_ge(router_read, t)
                                e.activation(prob[:, tb, :], logits[:, tb, :], ACT.Sigmoid)
                            e.wait_ge(proj_made, t + 1)
                            e.wait_ge(proj_read_v, t + 1)
                            e.activation(og[:, t, :], bank[t % 2][:, D:2 * D], ACT.Sigmoid)
                            e.copy(K[:, t, :], bank[t % 2][:, 2 * D:3 * D]).then_inc(proj_read_s, 1)
                            if t % 2 == 1:
                                i = t // 2
                                e.wait_ge(qk_made, i + 1)
                                dst = (qT, kT)[i % 2][:, S * (i // 2):S * (i // 2) + S]
                                if i % 2 == 0:
                                    e.mul(dst, bank[4][:, :], DH ** -0.5).then_inc(qk_read, 1)
                                else:
                                    e.copy(dst, bank[5][:, :]).then_inc(qk_read, 1)
                            if t == FIRST - 1:
                                gate_functions()
                            if t == TURN_1 + 1:
                                e.wait_ge(rows_turned, 1)
                                e.copy(floor[:, :, :], bank[7][:, :].rearrange("p (j r) -> p j r", r=P)).then_inc(m_copied, 1)
                            if t == TURN_2 + 1:
                                e.wait_ge(rows_turned, 2)
                                e.copy(R[:, :, :], bank[7][:, :].rearrange("p (j r) -> p j r", r=P)).then_inc(R_ready, 1)
                        e.wait_ge(router_read, NT)
                        e.activation(prob[:, NT - TPB:NT, :], logits[:, NT - TPB:NT, :], ACT.Sigmoid).then_inc(prob_ready, 1)
                        e.wait_ge(prob_ready, 1)
                        for b in range(B):
                            tb = slice(TPB * b, TPB * b + TPB)
                            e.activation(logits[:, tb, :], logits[:, tb, :], ACT.Exp, scale=-1.0).then_inc(router_exp_ready, 1)
                        e.wait_ge(m_copied, 1)
                        e.activation(floor[:, :, :], floor[:, :, :], ACT.Exp, scale=-1.0)
                        e.wait_ge(diff_ready, 3)
                        e.activation(k_scale[:, :, :], k_scale[:, :, :], ACT.Exp)
                        e.activation(q_scale[:, :, :], q_scale[:, :, :], ACT.Exp)
                        e.activation(decay[:, :, :], decay[:, :, :], ACT.Exp)

                    @block.vector
                    def _(e):
                        link = chain(e, dve_order)
                        e.tensor_scalar(bias15[:, :], Bw[:, B_AT["big"].start:B_AT["bfg"].stop], 1 / CAP, None,
                                        ALU.mult).then_inc(bias_ready, 1)
                        e.memset(VA[:, :, :, DH:DV], 1.0)
                        e.memset(g["ones"][:, :], 1.0)
                        e.tensor_copy(masked_bf[:, :, :],
                                      w["masked"].rearrange("p (o m) -> p o m", o=1).to_broadcast([P, TPB, P]))
                        def evacuate(t):
                            e.wait_ge(proj_made, t + 1)
                            e.tensor_copy(VA[:, t, :, 0:DH],
                                          bank[t % 2][:, 0:D].rearrange("p (h v) -> p h v", h=NH)).then_inc(proj_read_v, 1)
                            e.wait_ge(router_made, t + 1)
                            e.tensor_tensor(logits[:, t, :], bank[2 + t % 2][:, 0:E1], w["expert_bias"],
                                            ALU.add).then_inc(router_read, 1)

                        for t in range(FIRST):
                            evacuate(t)
                        e.wait_ge(tanh_ready, 2)
                        link(e.tensor_scalar(g["x"][:, :], g["tf"][:, :], CAP, None, ALU.mult))
                        e.scalar_tensor_tensor(g["ru"][:, :], g["x"][:, :], -1.0, g["x"][:, :], ALU.mult, ALU.max).then_inc(abs_ready, 1)
                        e.tensor_scalar(g["ti"][:, :], g["ti"][:, :], CAP, None, ALU.mult)
                        e.wait_ge(y_ready, 1)
                        e.tensor_scalar(g["u"][:, :], g["y"][:, :], 1.0, None, ALU.add).then_inc(u_ready, 1)
                        e.wait_ge(u_ready, 1)
                        evacuate(2)
                        link(e.scalar_tensor_tensor(g["c"][:, :], g["u"][:, :], 1.0, g["y"][:, :], ALU.subtract, ALU.subtract))
                        evacuate(3)
                        e.wait_ge(ru_ready, 1)
                        link(e.tensor_tensor(g["c"][:, :], g["c"][:, :], g["ru"][:, :], ALU.mult))
                        link(e.scalar_tensor_tensor(g["x"][:, :], g["x"][:, :], 0.0, g["c"][:, :], ALU.min, ALU.add))
                        e.wait_ge(ln_ready, 1)
                        link(e.tensor_tensor(g["x"][:, :], g["x"][:, :], g["ln"][:, :], ALU.subtract))
                        evacuate(4)
                        link(e.tensor_tensor_scan(g["lf"][:, :], g["ones"][:, :], g["x"][:, :], 0.0, ALU.mult, ALU.add))
                        evacuate(5)
                        e.tensor_tensor(g["a"][:, :], g["ti"][:, :], g["lf"][:, :], ALU.subtract).then_inc(rows_ready, 1)
                        e.wait_ge(rows_ready, 1)
                        evacuate(6)
                        e.tensor_tensor_scan(g["M"][:, :], g["a"][:, :], g["a"][:, :], -3e38, ALU.max, ALU.max).then_inc(rows_ready, 1)
                        e.wait_ge(rows_ready, 2)
                        evacuate(7)
                        e.tensor_tensor(g["m"][:, :], g["lf"][:, :], g["M"][:, :], ALU.add).then_inc(rows_ready, 1)
                        evacuate(8)
                        for j in range(TPB):
                            last = e.tensor_scalar(Rdiag[:, j, :], a["ident"], g["M"][:, P * j + P - 1:P * j + P], None, ALU.mult)
                        last.then_inc(R_made, 1)
                        for t in range(9, NT):
                            evacuate(t)
                            if t == 9:
                                link(e.tensor_scalar(mh[:, :], g["M"][:, :], -1.0, None, ALU.mult))
                            if t == TURN_1 + 1:
                                e.wait_ge(rows_turned, 1)
                                e.tensor_copy(aT[:, :, :], bank[6][:, :].rearrange("p (j r) -> p j r", r=P)).then_inc(aT_ready, 1)
                            if t == 11:
                                link(e.scalar_tensor_tensor(ml[:, :], g["M"][:, :], -1.0, mh[:, :].bitcast(F32),
                                                            ALU.mult, ALU.subtract))
                            if t == 12:
                                e.tensor_copy(ones_r[:, :], a["ones"])
                        e.wait_ge(R_ready, 1)
                        e.wait_ge(aT_ready, 1)
                        e.tensor_tensor(k_scale[:, :, :], aT[:, :, :], R[:, :, :], ALU.subtract).then_inc(diff_ready, 1)
                        e.tensor_tensor(q_scale[:, :, :], R[:, 0:TPB - 1, :],
                                        bank[6][:, P:S].rearrange("p (j r) -> p j r", r=P), ALU.subtract).then_inc(diff_ready, 1)
                        e.tensor_tensor(decay[:, :, :], R[:, 0:TPB - 1, :], R[:, 1:TPB, :], ALU.subtract).then_inc(diff_ready, 1)

                        def own(j):
                            own_head = w["lane"].rearrange("p (h o) -> p h o", o=1).to_broadcast([P, NH, P])
                            for whole_m, m_own in ((mh, mh_own), (ml, ml_own)):
                                e.tensor_tensor(m_own[:, j, :, :],
                                                       whole_m[:, P * j:P * j + P].bitcast(F32)
                                                       .rearrange("p (o n) -> p o n", o=1).to_broadcast([P, NH, P]),
                                                       own_head, ALU.mult)

                        for j in range(TPB):
                            own(j)

                    @block.gpsimd
                    def _(e):
                        for b in range(B):
                            s = slice(S * b, S * b + S)
                            e.tensor_copy(XH[:, s], XT[:, s]).then_inc(xh_ready, 1)
                            e.wait_ge(xh_ready, b + 1)
                            e.tensor_tensor(XL[:, s], XT[:, s], XH[:, s].bitcast(F32), ALU.subtract)
                        for b in range(B):
                            tb = slice(TPB * b, TPB * b + TPB)
                            e.wait_ge(router_exp_ready, b + 1)
                            e.tensor_scalar(logits[:, tb, :], logits[:, tb, :], -1.0, -1.0, ALU.mult, ALU.add)

                with ExitStack() as ph:
                    AHEAD = 4
                    Dm = sb("Dm", [P, 2, NH, P], ctx=ph)
                    CT = sb("CT", [P, 2, NH, P], ctx=ph)
                    qb = sb("qb", [P, AHEAD, NH, P], ctx=ph)
                    KS = sb("KS", [P, AHEAD, NH, DH], ctx=ph)
                    St = sb("St", [P, 2, NH, DV], ctx=ph)
                    inc = sb("inc", [P, NH, DV], ctx=ph)
                    part = sb("part", [P, NH, DV], ctx=ph)
                    top = sb("top1", [P, TPB, K1], ctx=ph)
                    tot = sb("tot1", [P, B, TPB], ctx=ph)
                    zap = sb("zap1", [P, TPB, E1], ctx=ph)
                    d_made, d_ready, st_made, c_ready = sem("d_made"), sem("d_ready"), sem("st_made"), sem("c_ready")
                    ks_ready, kv_made, state_ready = sem("ks_ready"), sem("kv_made"), sem("state_ready")
                    inter_made, inter_read, intra_made, o_ready = sem("inter_made"), sem("inter_read"), sem("intra_made"), sem("o_ready")
                    dve_order = sem("dve_order_e")
                    qb_ready = sem("qb_ready")
                    div_ready, divided, mean_ready = sem("div_ready"), sem("divided"), sem("mean_ready")
                    centered, squares_ready, tot_ready = sem("centered"), sem("squares_ready"), sem("tot_ready")
                    block = ph.enter_context(nc.Block())
                    wide = NH * DV

                    @block.tensor
                    def _(e):
                        def unit(t):
                            b, j = t // TPB, t % TPB
                            if t >= 2:
                                e.wait_ge(d_ready, t - 1)
                            rows = slice(32 * b, 32 * b + 32)
                            dm, st = bank[t % 2], bank[2 + t % 2]
                            e.matmul(dm[:, :], ones_r[rows, :], mh_own[rows, j, :, :], start=True, stop=False)
                            e.matmul(dm[:, :], ones_r[rows, :], ml_own[rows, j, :, :], start=False, stop=False)
                            e.matmul(dm[:, :], ident_bf[:, :], masked_bf[:, :, :], start=False, stop=True).then_inc(d_made, 1)
                            if t >= 2:
                                e.wait_ge(c_ready, t - 1)
                            e.wait_ge(qb_ready, t + 1)
                            e.matmul(st[:, :], kT[:, P * t:P * t + P], qb[:, t % AHEAD, :, :], start=True, stop=True).then_inc(st_made, 1)

                        def tile(t):
                            b, j = t // TPB, t % TPB
                            n = (TPB - 1) * b + j
                            e.wait_ge(c_ready, t + 1)
                            if t >= 2:
                                e.wait_ge(o_ready, t - 1)
                            for h in range(NH):
                                last = e.matmul(bank[4 + t % 2][:, DV * h:DV * h + DV], CT[:, t % 2, h, :],
                                                VA[:, t, h, :], start=True, stop=True)
                            last.then_inc(intra_made, 1)
                            if j < TPB - 1:
                                e.wait_ge(ks_ready, n + 1)
                                if n:
                                    e.wait_ge(state_ready, n)
                                e.matmul(bank[7][:, 0:wide], KS[:, n % AHEAD, :, :], VA[:, t, :, :],
                                         start=True, stop=True).then_inc(kv_made, 1)
                            if j:
                                e.wait_ge(state_ready, n)
                                if n > 1:
                                    e.wait_ge(inter_read, n - 1)
                                e.matmul(bank[6][:, 0:wide], qT[:, P * t:P * t + P], St[:, (j - 1) % 2, :, :],
                                         start=True, stop=True).then_inc(inter_made, 1)

                        for t in range(2):
                            unit(t)
                        for t in range(NT):
                            tile(t)
                            if t + 2 < NT:
                                unit(t + 2)

                    @block.scalar
                    def _(e):
                        for t in range(NT):
                            e.wait_ge(d_made, t + 1)
                            if t >= 2:
                                e.wait_ge(c_ready, t - 1)
                            b, j = t // TPB, t % TPB
                            for h in range(NH):
                                last = e.activation(Dm[:, t % 2, h, :], bank[t % 2][:, P * h:P * h + P], ACT.Exp,
                                                    bias=aT[:, j, 32 * b + h:32 * b + h + 1])
                            last.then_inc(d_ready, 1)

                    @block.vector
                    def _(e):
                        link = chain(e, dve_order)

                        def per_head(m, b, n):
                            return m[:, 32 * b:32 * b + NH].rearrange("p (h o) -> p h o", o=1).to_broadcast([P, NH, n])

                        def product(t):
                            e.wait_ge(d_ready, t + 1)
                            e.wait_ge(st_made, t + 1)
                            if t >= 2:
                                e.wait_ge(intra_made, t - 1)
                            e.tensor_tensor(CT[:, t % 2, :, :], Dm[:, t % 2, :, :],
                                            bank[2 + t % 2][:, :].rearrange("p (h n) -> p h n", h=NH),
                                            ALU.mult).then_inc(c_ready, 1)

                        def tile(t):
                            b, j = t // TPB, t % TPB
                            n = (TPB - 1) * b + j
                            po = bank[4 + t % 2][:, 0:wide].rearrange("p (h d) -> p h d", h=NH)
                            pi = bank[6][:, 0:wide].rearrange("p (h d) -> p h d", h=NH)
                            if j:
                                e.wait_ge(inter_made, n)
                                e.tensor_tensor(part[:, :, :], pi, per_head(q_scale[:, j - 1, :], b, DV), ALU.mult).then_inc(inter_read, 1)
                                e.wait_ge(inter_read, n)
                                e.wait_ge(intra_made, t + 1)
                                e.tensor_tensor(O[:, t, :, :], part[:, :, :], po, ALU.add).then_inc(o_ready, 1)
                            else:
                                e.wait_ge(intra_made, t + 1)
                                e.tensor_copy(O[:, t, :, :], po).then_inc(o_ready, 1)
                            if j < TPB - 1:
                                e.wait_ge(kv_made, n + 1)
                                kv = bank[7][:, 0:wide].rearrange("p (h d) -> p h d", h=NH)
                                blocks = w["diag"].rearrange("p (h d) -> p h d", h=NH)
                                if j == 0:
                                    e.tensor_tensor(St[:, 0, :, :], kv, blocks, ALU.mult).then_inc(state_ready, 1)
                                    e.wait_ge(state_ready, n + 1)
                                else:
                                    e.tensor_tensor(inc[:, :, :], kv, blocks, ALU.mult)
                                    link(e.tensor_tensor(St[:, j % 2, :, :], St[:, (j - 1) % 2, :, :],
                                                         per_head(decay[:, j - 1, :], b, DV), ALU.mult))
                                    e.tensor_tensor(St[:, j % 2, :, :], St[:, j % 2, :, :], inc[:, :, :], ALU.add).then_inc(state_ready, 1)
                                    e.wait_ge(state_ready, n + 1)

                        def route(b, step):
                            tb = slice(TPB * b, TPB * b + TPB)
                            if step == 0:
                                for j in range(TPB):
                                    last = e.max(top[:, j, :], logits[:, TPB * b + j, :])
                                link(last)
                            elif step == 1:
                                for j in range(TPB):
                                    last = e.match_replace(zap[:, j, :], top[:, j, :], logits[:, TPB * b + j, :], 1.0)
                                link(last)
                                link(e.scalar_tensor_tensor(prob[:, tb, :], zap[:, :, :], 0.0, prob[:, tb, :],
                                                            ALU.is_gt, ALU.mult))
                            elif step == 2:
                                sums = tot[:, b, :]
                                link(e.tensor_reduce(sums, prob[:, tb, :], AX.X, ALU.add))
                                link(e.tensor_scalar(sums, sums, 1e-9, None, ALU.add))
                                link(e.reciprocal(sums, sums))
                                e.tensor_scalar(sums, sums, ROUTED_SCALE, None, ALU.mult).then_inc(tot_ready, 1)

                        product(0)
                        for t in range(NT):
                            b, j = t // TPB, t % TPB
                            if t + 1 < NT:
                                product(t + 1)
                            tile(t)
                            if t < 3 * B:
                                route(t // 3, t % 3)
                            if b and j == 0:
                                head_divisors(e, link, b - 1).then_inc(div_ready, 1)
                            if b and j == 1:
                                e.wait_ge(divided, b)
                                head_means(e, link, b - 1).then_inc(mean_ready, 1)
                            if b and j == 3:
                                e.wait_ge(squares_ready, b)
                                link(head_vars(e, link, b - 1))
                    @block.gpsimd
                    def _(e):
                        def queries(t):
                            if t >= AHEAD:
                                e.wait_ge(st_made, t - AHEAD + 1)
                            e.tensor_tensor(qb[:, t % AHEAD, :, :],
                                            qT[:, P * t:P * t + P].rearrange("p (o n) -> p o n", o=1).to_broadcast([P, NH, P]),
                                            w["diag"].rearrange("p (h d) -> p h d", h=NH)[:, :, 0:1].to_broadcast([P, NH, P]),
                                            ALU.mult).then_inc(qb_ready, 1)

                        def keys(t):
                            b, j = t // TPB, t % TPB
                            n = (TPB - 1) * b + j
                            if j == TPB - 1:
                                return
                            if n >= AHEAD:
                                e.wait_ge(kv_made, n - AHEAD + 1)
                            scale = k_scale[:, j, 32 * b:32 * b + NH].rearrange("p (h o) -> p h o", o=1).to_broadcast([P, NH, DH])
                            e.tensor_tensor(KS[:, n % AHEAD, :, :], K[:, t, :].rearrange("p (h d) -> p h d", h=NH), scale,
                                            ALU.mult).then_inc(ks_ready, 1)

                        for t in range(AHEAD):
                            queries(t)
                            if t < AHEAD - 1:
                                keys(t)
                        for t in range(NT):
                            if t + AHEAD - 1 < NT:
                                keys(t + AHEAD - 1)
                            if t + AHEAD < NT:
                                queries(t + AHEAD)
                            b, j = t // TPB, t % TPB
                            if t < 3 * B and t % 3 == 2:
                                r = t // 3
                                tb = slice(TPB * r, TPB * r + TPB)
                                e.wait_ge(tot_ready, r + 1)
                                e.tensor_tensor(prob[:, tb, :], prob[:, tb, :],
                                                tot[:, r, :].rearrange("p (t o) -> p t o", o=1).to_broadcast([P, TPB, E1]),
                                                ALU.mult)
                            if b and j == 0:
                                e.wait_ge(div_ready, b)
                                head_divide(e, b - 1).then_inc(divided, 1)
                            if b and j == 1:
                                e.wait_ge(mean_ready, b)
                                head_center(e, b - 1).then_inc(centered, 1)
                                e.wait_ge(centered, b)
                                head_squares(e, b - 1).then_inc(squares_ready, 1)
                            if j == TPB - 1:
                                tb = slice(t + 1 - TPB, t + 1)
                                e.tensor_tensor(og[:, tb, :], og[:, tb, :], w["norm_w"].rearrange("p (o d) -> p o d", o=1)
                                                .to_broadcast([P, TPB, D]), ALU.mult)

                with ExitStack() as ph:
                    combT = sb("combT", [TB, B, NB, S], ctx=ph)
                    LAST_B = TPB * (B - 1)
                    ho = sb("ho", [P, NT, D], ctx=ph)
                    HT = sb("HT", [P, 2, S], ctx=ph)
                    var_ready, std_ready = sem("var_ready"), sem("head_std_ready")
                    comb_turned, comb_copied, comb_stored = sem("comb1_turned"), sem("comb1_copied"), sem("comb_stored")
                    ho_ready, ho_turned, ht_ready, s_made = sem("ho_ready"), sem("ho_turned"), sem("ht_ready"), sem("s1_made")
                    dve_order, s_read, sh_made = sem("dve_order_f"), sem("s_read"), sem("sh_made")
                    block = ph.enter_context(nc.Block())

                    @block.sync
                    def _(e):
                        for s in range(2):
                            load_chunk(e, s, slice(s, s + 1))
                        rows = comb_dram.rearrange("(k r) n -> r k n", r=TB)
                        for b in range(B):
                            e.wait_ge(comb_copied, b + 1)
                            e.dma_start(rows[:, :, S * b:S * b + S], combT[:, b, :, :]).then_inc(comb_stored, 16)
                        e.wait_ge(comb_stored, 16 * B)
                        for s in range(2):
                            for h in range(HALVES):
                                load_comb(e, s, h, EPC1 * s)

                    @block.gpsimd
                    def _(e):
                        e.memset(zeros[:, :], 0.0).then_inc(zeros_ready, 1)
                        e.wait_ge(zeros_ready, 1)
                        for s in range(2):
                            split(e, 0, s)

                    @block.scalar
                    def _(e):
                        e.activation(var[:, 0:LAST_B, :], var[:, 0:LAST_B, :], ACT.Sqrt).then_inc(std_ready, 1)
                        for b in range(B):
                            e.wait_ge(comb_turned, b + 1)
                            for k in range(NB):
                                last = e.copy(combT[:, b, k, :], bank[NB * (b % 2) + k][0:TB, :])
                            last.then_inc(comb_copied, 1)
                            if b == 1:
                                e.wait_ge(var_ready, 1)
                                e.activation(var[:, LAST_B:NT, :], var[:, LAST_B:NT, :], ACT.Sqrt).then_inc(std_ready, 1)
                        for b in range(B):
                            e.wait_ge(ho_turned, b + 1)
                            e.copy(HT[:, b % 2, :], bank[4 + b % 2][:, :]).then_inc(ht_ready, 1)
                            e.wait_ge(sh_made, b + 1)
                            e.activation(shared[:, b, :], bank[b][0:H1, :], ACT.Silu)

                    @block.vector
                    def _(e):
                        link = chain(e, dve_order)
                        link(head_divisors(e, link, B - 1))
                        link(head_divide(e, B - 1))
                        link(head_means(e, link, B - 1))
                        link(head_center(e, B - 1))
                        link(head_squares(e, B - 1))
                        head_vars(e, link, B - 1).then_inc(var_ready, 1)
                        for b in range(B):
                            tb = slice(TPB * b, TPB * b + TPB)
                            if b == 0:
                                e.wait_ge(std_ready, 1)
                                link(e.reciprocal(var[:, 0:LAST_B, :], var[:, 0:LAST_B, :]))
                            if b == B - 1:
                                e.wait_ge(std_ready, 2)
                                link(e.reciprocal(var[:, LAST_B:NT, :], var[:, LAST_B:NT, :]))
                            hv = ho[:, tb, :].rearrange("p t (h d) -> p (t h) d", h=NH)
                            link(e.tensor_tensor(hv, values_of(b), spread(var, tb), ALU.mult))
                            e.tensor_tensor(ho[:, tb, :], ho[:, tb, :], og[:, tb, :], ALU.mult).then_inc(ho_ready, 1)
                        for b in range(B):
                            e.wait_ge(s_made, b + 1)
                            e.tensor_copy(S1[:, TPB * b:TPB * b + TPB, :],
                                          bank[6 + b % 2][:, :].rearrange("p (t d) -> p t d", d=D)).then_inc(s_read, 1)

                    @block.tensor
                    def _(e):
                        for b in range(B):
                            if b >= 2:
                                e.wait_ge(comb_copied, b - 1)
                            for k in range(NB):
                                for j in range(TPB):
                                    last = e.transpose(bank[NB * (b % 2) + k][0:TB, P * j:P * j + P],
                                                       prob[:, TPB * b + j, TB * k:TB * k + TB], a["ident"])
                            last.then_inc(comb_turned, 1)
                        for b in range(B):
                            if b % 2 == 0:
                                e.wait_ge(comb_copied, B - 1 + b // 2)
                            e.matmul(bank[b][0:H1, :], w["shared_gate"], XT[:, S * b:S * b + S],
                                     start=True, stop=True).then_inc(sh_made, 1)

                        def turn(b):
                            e.wait_ge(ho_ready, b + 1)
                            if b >= 2:
                                e.wait_ge(ht_ready, b - 1)
                            for j in range(TPB):
                                last = e.transpose(bank[4 + b % 2][:, P * j:P * j + P], ho[:, TPB * b + j, :], a["ident"])
                            last.then_inc(ho_turned, 1)

                        turn(0)
                        for b in range(B):
                            if b + 1 < B:
                                turn(b + 1)
                            e.wait_ge(ht_ready, b + 1)
                            if b >= 2:
                                e.wait_ge(s_read, b - 1)
                            for j in range(TPB):
                                last = e.matmul(bank[6 + b % 2][:, P * j:P * j + P], HT[:, b % 2, P * j:P * j + P], w["wdown"],
                                                start=True, stop=True)
                            last.then_inc(s_made, 1)

            with ExitStack() as ph:
                LAG = 6
                LEAD = 2
                RING = PAIR
                act = sb("act", [P, 4, S], ctx=ph)
                hid = sb("hid", [P, RING, S], ctx=ph)
                hid_hi = sb("hid_hi", [P, RING, S], F32R, ctx=ph)
                hid_lo = sb("hid_lo", [P, RING, S], F32R, ctx=ph)
                yT = sb("yT", [P, N], ctx=ph)
                res = sb("res", [P, NT, D], ctx=ph)
                act_ready = sem("act1_ready")
                hid_ready, hi_ready, lo_ready = sem("hid_ready"), sem("hi_ready"), sem("lo_ready")
                yt_ready, y_turned, res_ready, x_ready = sem("yt_ready"), sem("y_turned"), sem("res_ready"), sem("x_ready")
                stored = [sem(f"stored{b}") for b in range(B)]
                block = ph.enter_context(nc.Block())

                @block.sync
                def _(e):
                    with e.Fori(1, TURNS) as i:
                        for s in range(2):
                            e.wait_ge(down_ready, i * 2 + (s - 1))
                            load_chunk(e, s, bass.ds(i * 2 + s, 1))
                            for h in range(HALVES):
                                e.wait_ge(hid_ready, i * PAIR + (G * s - PAIR + GPH * (h + 1)))
                                load_comb(e, s, h, i * (2 * EPC1) + EPC1 * s)
                    for b in range(B):
                        tb = slice(TPB * b, TPB * b + TPB)
                        e.wait_ge(x_ready, b + 1)
                        e.dma_start(out_rows[:, tb, :], X[:, tb, :]).then_inc(stored[b], 16)
                    for b in range(B):
                        e.wait_ge(stored[b], 16)

                @block.gpsimd
                def _(e):
                    with e.Fori(1, TURNS) as i:
                        for s in range(2):
                            split(e, i, s)

                @block.tensor
                def _(e):
                    def up(i, j):
                        s, g = (j // G) % 2, j % G
                        if g == 0:
                            e.wait_ge(gate_ready, i * 2 + (j // G + 1))
                        if not (isinstance(i, int) and i == 0 and j < 4):
                            e.wait_ge(act_ready, i * PAIR + (j - 3))
                        xs = slice(S * g, S * g + S)
                        e.matmul(bank[j % 4][:, :], gate_hi[:, s, :], XH[:, xs], start=True, stop=False)
                        e.matmul(bank[j % 4][:, :], gate_hi[:, s, :], XL[:, xs], start=False, stop=False)
                        e.matmul(bank[j % 4][:, :], gate_lo[:, s, :], XH[:, xs], start=False, stop=True).then_inc(up_made, 1)

                    def down(i, j, last=False):
                        s, g = (j // G) % 2, j % G
                        if g == 0:
                            e.wait_ge(down_ready, i * 2 + (j // G + 1))
                        e.wait_ge(lo_ready, i * PAIR + (j + 1))
                        y = bank[4 + g][:, :]
                        e.matmul(y, down_hi[:, s, :], hid_hi[:, j % RING, :], start=False, stop=False)
                        e.matmul(y, down_hi[:, s, :], hid_lo[:, j % RING, :], start=False, stop=False)
                        e.matmul(y, down_lo[:, s, :], hid_hi[:, j % RING, :], start=False, stop=last).then_inc(y_made, 1)

                    for j in range(4):
                        up(0, j)
                    for g in range(G):
                        e.matmul(bank[4 + g][:, :], w["shared_down"][0:H1, :], shared[:, g, :], start=True, stop=False)
                    for j in range(4, LAG):
                        up(0, j)
                    with e.Fori(0, TURNS - 1) as i:
                        for j in range(PAIR):
                            down(i, j)
                            up(i, j + LAG)
                    for j in range(PAIR):
                        down(TURNS - 1, j, last=(j >= G))
                        if j + LAG < PAIR:
                            up(TURNS - 1, j + LAG)
                    for b in range(B):
                        e.wait_ge(yt_ready, b + 1)
                        for j in range(TPB):
                            last = e.transpose(bank[b][:, P * j:P * j + P], yT[:, S * b + P * j:S * b + P * j + P], a["ident"])
                        last.then_inc(y_turned, 1)

                @block.scalar
                def _(e):
                    def silu(i, j):
                        e.wait_ge(up_made, i * PAIR + (j + 1))
                        if not (isinstance(i, int) and i == 0 and j < 2):
                            e.wait_ge(hid_ready, i * PAIR + (j - 1))
                        e.activation(act[:, j % 4, :], bank[j % 4][:, :], ACT.Silu).then_inc(act_ready, 1)

                    def high(i, j):
                        e.wait_ge(hid_ready, i * PAIR + (j + 1))
                        e.copy(hid_hi[:, j % RING, :], hid[:, j % RING, :]).then_inc(hi_ready, 1)

                    for j in range(LEAD):
                        silu(0, j)
                    with e.Fori(0, TURNS - 1) as i:
                        for j in range(PAIR):
                            silu(i, j + LEAD)
                            high(i, j)
                    for j in range(PAIR):
                        if j + LEAD < PAIR:
                            silu(TURNS - 1, j + LEAD)
                        high(TURNS - 1, j)
                    for b in range(B):
                        e.wait_ge(y_made, C1 * G - (B - 1) + b)
                        e.activation(yT[:, S * b:S * b + S], bank[4 + b][:, :], ACT.Silu).then_inc(yt_ready, 1)

                @block.vector
                def _(e):
                    def weigh(i, j):
                        e.wait_ge(act_ready, i * PAIR + (j + 1))
                        s, g = (j // G) % 2, j % G
                        if g % GPH == 0:
                            e.wait_ge(comb_in[s][g // GPH], (i + j // PAIR) * (16 * EPC1) + 16 * EPC1)
                        e.tensor_tensor(hid[:, j % RING, :], act[:, j % 4, :], comb[:, s, S * g:S * g + S], ALU.mult).then_inc(hid_ready, 1)

                    def low(i, j):
                        e.wait_ge(hi_ready, i * PAIR + (j + 1))
                        e.tensor_tensor(hid_lo[:, j % RING, :], hid[:, j % RING, :], hid_hi[:, j % RING, :].bitcast(F32),
                                        ALU.subtract).then_inc(lo_ready, 1)

                    for j in range(LEAD):
                        weigh(0, j)
                    with e.Fori(0, TURNS - 1) as i:
                        for j in range(PAIR):
                            weigh(i, j + LEAD)
                            low(i, j)
                    for j in range(PAIR):
                        if j + LEAD < PAIR:
                            weigh(TURNS - 1, j + LEAD)
                        low(TURNS - 1, j)
                    for b in range(B):
                        tb = slice(TPB * b, TPB * b + TPB)
                        e.wait_ge(y_turned, b + 1)
                        e.tensor_tensor(res[:, tb, :], S1[:, tb, :], bank[b][:, :].rearrange("p (t d) -> p t d", d=D),
                                        ALU.mult).then_inc(res_ready, 1)
                        e.wait_ge(res_ready, b + 1)
                        e.tensor_tensor(X[:, tb, :], X[:, tb, :], res[:, tb, :], ALU.add).then_inc(x_ready, 1)


def kernel(**inputs):
    import numpy as np
    import concourse.bacc as bacc
    from concourse.bass_utils import run_bass_kernel_spmd

    i = {k: np.asarray(v) for k, v in inputs.items()}
    f = np.float32

    def rows(v):
        return np.tile(np.reshape(v, (1, -1)), (P, 1))

    def down(m, n=P):
        out = np.zeros((n,) + m.shape[1:], f)
        out[:m.shape[0]] = m
        return out

    turn = np.zeros((P, P), f)
    for k in range(0, P, 2):
        turn[k, k + 1], turn[k + 1, k] = -1, 1
    sel0 = np.zeros((P, C0, P), f)
    for r in range(R0):
        c, e = r // (3 * EPC0), r % EPC0
        sel0[r, c, H0 * e:H0 * e + H0] = 1
    masked = np.where(np.arange(P)[:, None] > np.arange(P)[None, :], MASKED, 0).astype(f)
    lane = np.zeros((P, NH), f)
    for r in range(P):
        if r % 32 < NH:
            lane[r, r % 32] = 1
    diag = np.zeros((P, NH, DV), f)
    for h in range(NH):
        diag[DH * h:DH * h + DH, h] = 1

    a = dict(ident=np.eye(P, dtype=f), turn=turn, ones=np.ones((P, P), f), sel0=sel0,
             expert_sel=i["L0_ffn_expert_sel"].T, keys=i["L0_ffn_keys"].transpose(1, 0, 2),
             values=i["L0_ffn_values"].reshape(C0, P, D).transpose(1, 0, 2),
             rot_c=np.repeat(i["L0_attn_rot_w"][:, 0::2], 2, axis=1).T,
             rot_s=np.repeat(i["L0_attn_rot_w"][:, 1::2], 2, axis=1).T,
             scale=rows(i["L0_attn_scale"]), bias=rows(i["L0_attn_bias"]), route_scale=rows(i["L0_ffn_route_scale"]))
    lanes = np.zeros((B, 32), f)

    def per_lane(v):
        out = lanes.copy()
        out[:, :NH] = v
        return out.reshape(P, 1)

    def per_col(m):
        out = np.zeros((P, 32), f)
        out[:, :NH] = m
        return out

    b = dict(masked=masked, wv=i["L1_attn_Wv"], wo=i["L1_attn_Wo"], wk=i["L1_attn_Wk"], wq=i["L1_attn_Wq"],
             wig=per_col(i["L1_attn_Wig"]), wfg=per_col(i["L1_attn_Wfg"]), router=i["L1_ffn_router_w"].T,
             wdown=i["L1_attn_Wdown"], norm_w=rows(i["L1_attn_norm_w"]), expert_bias=rows(i["L1_ffn_expert_bias"]),
             big=per_lane(i["L1_attn_big"]), bfg=per_lane(i["L1_attn_bfg"]),
             shared_gate=i["L1_ffn_w_gate_shared"].T, shared_down=down(i["L1_ffn_w_down_shared"].T), diag=diag, lane=lane)
    packed = {
        "x": i["L0_attn_Q"].reshape(N, D),
        "layer0": np.concatenate([a[k].reshape(P, n) for k, n in A_COLS.items()], axis=1),
        "layer1": np.concatenate([b[k].reshape(P, n) for k, n in B_COLS.items()], axis=1),
        "experts": np.concatenate([i["L1_ffn_w_gate"].reshape(C1, P, D).transpose(0, 2, 1),
                                   i["L1_ffn_w_down"].transpose(0, 2, 1).reshape(C1, P, D)], axis=2),
    }
    nc = bacc.Bacc("TRN2", target_bir_lowering=False, num_devices=1)
    arrays, args = {}, []
    for name, v in packed.items():
        v = np.ascontiguousarray(v)
        arrays[f"in_{name}"] = v
        args.append(nc.dram_tensor(f"in_{name}", v.shape, mybir.dt.from_np(v.dtype), kind="ExternalInput").ap())
    args.append(nc.dram_tensor("out", (N, D), F32, kind="ExternalOutput").ap())
    build(nc, *args)
    r = run_bass_kernel_spmd(nc, [arrays], core_ids=[0])
    return r.results[0]["out"].reshape(B, S, D)
```
